# Optimizing a Trainium2 kernel written in Bass

```python
import numpy as np
import jax
import jax.numpy as jnp

def _softmax(x, axis=-1):
    return jax.nn.softmax(x, axis=axis)

def _gelu(x):
    return jax.nn.gelu(x, approximate=True)

def _silu(x):
    return jax.nn.silu(x)

def _sigmoid(x):
    return jax.nn.sigmoid(x)

def _layernorm(x, axis=-1, eps=1e-05):
    m = jnp.mean(x, axis=axis, keepdims=True)
    v = jnp.var(x, axis=axis, keepdims=True)
    return (x - m) / jnp.sqrt(v + eps)

def _scatter_add(tgt, idx, src, axis=0):
    return tgt.at[idx].add(src)

def _segment_sum(src, seg, n):
    return jax.ops.segment_sum(src, seg, n)
kernel_name = 'mk_adaln_ffn_d2_seqx_r4_095542'

def setup_inputs(seed: int=0):
    np.random.seed(seed)
    _w = jnp.asarray

    def _rec_inputs():
        import jax
        import jax.numpy as jnp
        _rk = jax.random.key(seed)
        x = -0.000125 + 0.9999 * jax.random.normal(jax.random.fold_in(_rk, 1), (2, 1024, 256), jnp.float32)
        _lenS = 1024 - jax.random.randint(jax.random.fold_in(_rk, 7), (2,), 0, max(1, 1024 // 4) + 1, jnp.int32)
        _lenS2 = 1024 - jax.random.randint(jax.random.fold_in(_rk, 8), (2,), 0, max(1, 1024 // 4) + 1, jnp.int32)
        cond_1024 = 0.00513981 + 1.0024 * jax.random.normal(jax.random.fold_in(_rk, 11), (2, 256), jnp.float32)
        return (x, cond_1024)
    x, cond_1024 = _rec_inputs()

    def _L0_cond_setup():
        import jax, jax.numpy as jnp
        import numpy as np
        IN_FEATURES = 256
        OUT_FEATURES = 256
        BATCH = 32
        SEQ = 256
        EPS = 1e-08
        key = jax.random.key(seed)
        k1, k2, k3 = jax.random.split(key, 3)
        Efou = jax.random.normal(k1, (BATCH, SEQ, IN_FEATURES), dtype=jnp.float32)
        y = jax.random.normal(k2, (BATCH, IN_FEATURES), dtype=jnp.float32)
        weight = jax.random.normal(k3, (IN_FEATURES, OUT_FEATURES), dtype=jnp.float32)
        return {'Efou': Efou, 'y': y, 'weight': weight}
    _L0_cond_all = _L0_cond_setup()
    _L0_cond_in = {k: v for k, v in _L0_cond_all.items() if k in ('weight',)}
    del _L0_cond_all

    def _L0_ffn_setup():
        import jax, jax.numpy as jnp
        import numpy as np

        def _ste(w, w_q):
            return w + jax.lax.stop_gradient(w_q - w)

        def quantize_w8_per(w, axis):
            amax = jnp.clip(jnp.max(jnp.abs(w), axis=axis, keepdims=True), 1e-08, None)
            scale = 127.0 / amax
            w_q = jnp.clip(jnp.round(w * scale), -128.0, 127.0) / scale
            return _ste(w, w_q)

        def quantize_a16(x):
            amax = jnp.clip(jnp.max(jnp.abs(x)), 1e-08, None)
            scale = 32767.0 / amax
            x_q = jnp.clip(jnp.round(x * scale), -32768.0, 32767.0) / scale
            return _ste(x, x_q)
        key = jax.random.key(seed)
        k1, k2, k3 = jax.random.split(key, 3)
        d_model, d_ff = (256, 1024)
        x = jax.random.normal(k1, (4, 512, d_model), dtype=jnp.float32)
        W_in = jax.random.normal(k2, (d_model, d_ff), dtype=jnp.float32) / np.sqrt(d_model)
        b_in = jnp.zeros((d_ff,), dtype=jnp.float32)
        W_out = jax.random.normal(k3, (d_ff, d_model), dtype=jnp.float32) / np.sqrt(d_ff)
        b_out = jnp.zeros((d_model,), dtype=jnp.float32)
        return {'x': x, 'W_in': W_in, 'b_in': b_in, 'W_out': W_out, 'b_out': b_out}
    _L0_ffn_all = _L0_ffn_setup()
    _L0_ffn_in = {k: v for k, v in _L0_ffn_all.items() if k in ('W_in', 'b_in', 'W_out', 'b_out')}
    del _L0_ffn_all

    def _L1_cond_setup():
        import jax, jax.numpy as jnp
        import numpy as np
        EPS = 1e-08
        key = jax.random.key(seed)
        ks = jax.random.split(key, 8)
        B, S, D, H = (8, 512, 256, 256)
        scale = 1.0 / np.sqrt(D)
        return {'input_seq': jax.random.normal(ks[0], (B, S, D), dtype=jnp.float32), 'initial_hidden': jax.random.normal(ks[1], (B, H), dtype=jnp.float32), 'W_f': jax.random.normal(ks[2], (H, D), dtype=jnp.float32) * scale, 'b_f': jnp.zeros((H,), dtype=jnp.float32), 'W_i': jax.random.normal(ks[3], (H, D), dtype=jnp.float32) * scale, 'b_i': jnp.zeros((H,), dtype=jnp.float32), 'W_h': jax.random.normal(ks[4], (H, D), dtype=jnp.float32) * scale, 'b_h': jnp.zeros((H,), dtype=jnp.float32)}
    _L1_cond_all = _L1_cond_setup()
    _L1_cond_in = {k: v for k, v in _L1_cond_all.items() if k in ('W_f', 'b_f', 'W_i', 'b_i', 'W_h', 'b_h')}
    del _L1_cond_all

    def _L1_ffn_setup():
        import jax, jax.numpy as jnp
        import numpy as np
        B, S, D = (4, 512, 256)
        E = 8
        TOPK = 2
        I = 938

        def _swiglu(x, gate_up, down):
            h = jnp.einsum('bsd,fd->bsf', x, gate_up)
            g, u = jnp.split(h, 2, axis=-1)
            return jnp.einsum('bsi,di->bsd', jax.nn.silu(g) * u, down)
        key = jax.random.key(seed)
        ks = jax.random.split(key, 6)
        scale = 1.0 / np.sqrt(D)
        return {'hidden_states': jax.random.normal(ks[0], (B, S, D), dtype=jnp.float32), 'gate_weight': jax.random.normal(ks[1], (E, D), dtype=jnp.float32) * scale, 'shared_gate_up': jax.random.normal(ks[2], (2 * I, D), dtype=jnp.float32) * scale, 'shared_down': jax.random.normal(ks[3], (D, I), dtype=jnp.float32) * (1.0 / np.sqrt(I)), 'experts_gate_up': jax.random.normal(ks[4], (E, 2 * I, D), dtype=jnp.float32) * scale, 'experts_down': jax.random.normal(ks[5], (E, D, I), dtype=jnp.float32) * (1.0 / np.sqrt(I))}
    _L1_ffn_all = _L1_ffn_setup()
    _L1_ffn_in = {k: v for k, v in _L1_ffn_all.items() if k in ('gate_weight', 'shared_gate_up', 'shared_down', 'experts_gate_up', 'experts_down')}
    del _L1_ffn_all
    return {'x': x, 'cond_1024': cond_1024, 'L0_cond_weight': _L0_cond_in['weight'], 'L0_ffn_W_in': _L0_ffn_in['W_in'], 'L0_ffn_b_in': _L0_ffn_in['b_in'], 'L0_ffn_W_out': _L0_ffn_in['W_out'], 'L0_ffn_b_out': _L0_ffn_in['b_out'], 'L1_cond_W_f': _L1_cond_in['W_f'], 'L1_cond_b_f': _L1_cond_in['b_f'], 'L1_cond_W_i': _L1_cond_in['W_i'], 'L1_cond_b_i': _L1_cond_in['b_i'], 'L1_cond_W_h': _L1_cond_in['W_h'], 'L1_cond_b_h': _L1_cond_in['b_h'], 'L1_ffn_gate_weight': _L1_ffn_in['gate_weight'], 'L1_ffn_shared_gate_up': _L1_ffn_in['shared_gate_up'], 'L1_ffn_shared_down': _L1_ffn_in['shared_down'], 'L1_ffn_experts_gate_up': _L1_ffn_in['experts_gate_up'], 'L1_ffn_experts_down': _L1_ffn_in['experts_down']}

def reference(x, cond_1024, L0_cond_weight, L0_ffn_W_in, L0_ffn_b_in, L0_ffn_W_out, L0_ffn_b_out, L1_cond_W_f, L1_cond_b_f, L1_cond_W_i, L1_cond_b_i, L1_cond_W_h, L1_cond_b_h, L1_ffn_gate_weight, L1_ffn_shared_gate_up, L1_ffn_shared_down, L1_ffn_experts_gate_up, L1_ffn_experts_down):
    import jax
    import jax.numpy as jnp

    def _L0_cond_ref(Efou, y, weight):
        import jax, jax.numpy as jnp
        import numpy as np
        IN_FEATURES = 256
        OUT_FEATURES = 256
        BATCH = 32
        SEQ = 256
        EPS = 1e-08
        scale = 1.0 / np.sqrt(np.float32(weight.shape[0]))
        ys = y * scale
        d = jax.lax.rsqrt(jnp.einsum('bi,io->bo', ys * ys, weight * weight) + EPS)
        out = jnp.einsum('bsi,io->bso', Efou * ys[:, None, :], weight) * d[:, None, :]
        return out

    def _L0_ffn_ref(x, W_in, b_in, W_out, b_out):
        import jax, jax.numpy as jnp
        import numpy as np

        def _ste(w, w_q):
            return w + jax.lax.stop_gradient(w_q - w)

        def quantize_w8_per(w, axis):
            amax = jnp.clip(jnp.max(jnp.abs(w), axis=axis, keepdims=True), 1e-08, None)
            scale = 127.0 / amax
            w_q = jnp.clip(jnp.round(w * scale), -128.0, 127.0) / scale
            return _ste(w, w_q)

        def quantize_a16(x):
            amax = jnp.clip(jnp.max(jnp.abs(x)), 1e-08, None)
            scale = 32767.0 / amax
            x_q = jnp.clip(jnp.round(x * scale), -32768.0, 32767.0) / scale
            return _ste(x, x_q)
        W_in_sim = quantize_w8_per(W_in, axis=0)
        W_out_sim = quantize_w8_per(W_out, axis=1)
        x_sim = quantize_a16(x)
        hidden = jax.nn.gelu(x_sim @ W_in_sim + b_in, approximate=False)
        hidden_sim = quantize_a16(hidden)
        out = hidden_sim @ W_out_sim + b_out
        return out

    def _L1_cond_ref(input_seq, initial_hidden, W_f, b_f, W_i, b_i, W_h, b_h):
        import jax, jax.numpy as jnp
        import numpy as np
        EPS = 1e-08
        forget_gate = jax.nn.sigmoid(jnp.einsum('bsd,hd->bsh', input_seq, W_f) + b_f)
        input_gate = jax.nn.sigmoid(jnp.einsum('bsd,hd->bsh', input_seq, W_i) + b_i)
        gate_sum = forget_gate + input_gate + EPS
        forget_norm = forget_gate / gate_sum
        input_norm = input_gate / gate_sum
        candidate = jnp.einsum('bsd,hd->bsh', input_seq, W_h) + b_h
        new_info = input_norm * candidate
        log_ret = jnp.log(forget_norm + EPS)
        log_cumprod = jnp.cumsum(log_ret, axis=1)
        B, _, H = log_cumprod.shape
        padded = jnp.concatenate([jnp.zeros((B, 1, H), dtype=log_cumprod.dtype), log_cumprod], axis=1)
        scaling = jnp.exp(log_cumprod[:, -1:, :] - padded[:, :-1, :])
        hidden = jnp.cumsum(scaling * new_info, axis=1)
        hidden = hidden + jnp.exp(log_cumprod) * initial_hidden[:, None, :]
        return hidden

    def _L1_ffn_ref(hidden_states, gate_weight, shared_gate_up, shared_down, experts_gate_up, experts_down):
        import jax, jax.numpy as jnp
        import numpy as np
        B, S, D = (4, 512, 256)
        E = 8
        TOPK = 2
        I = 938

        def _swiglu(x, gate_up, down):
            h = jnp.einsum('bsd,fd->bsf', x, gate_up)
            g, u = jnp.split(h, 2, axis=-1)
            return jnp.einsum('bsi,di->bsd', jax.nn.silu(g) * u, down)
        x = hidden_states
        out = _swiglu(x, shared_gate_up, shared_down)
        logits = jnp.einsum('bsd,ed->bse', x, gate_weight)
        probs = jax.nn.softmax(logits.astype(jnp.float32), axis=-1)
        top_p, sel = jax.lax.top_k(probs, TOPK)
        top_p = top_p / (jnp.sum(top_p, axis=-1, keepdims=True) + 1e-08)
        cw = jnp.sum(top_p[..., None] * jax.nn.one_hot(sel, E, dtype=top_p.dtype), axis=2)
        for e in range(E):
            y = _swiglu(x, experts_gate_up[e], experts_down[e])
            out = out + cw[..., e:e + 1] * y
        return out
    x = x + _L0_ffn_ref(_L0_cond_ref(x, cond_1024, L0_cond_weight), L0_ffn_W_in, L0_ffn_b_in, L0_ffn_W_out, L0_ffn_b_out)
    x = x + _L1_ffn_ref(_L1_cond_ref(x, cond_1024, L1_cond_W_f, L1_cond_b_f, L1_cond_W_i, L1_cond_b_i, L1_cond_W_h, L1_cond_b_h), L1_ffn_gate_weight, L1_ffn_shared_gate_up, L1_ffn_shared_down, L1_ffn_experts_gate_up, L1_ffn_experts_down)
    return x

_drawn_inputs = setup_inputs


def setup_inputs(seed=0):
    import zlib

    import numpy as np

    out = dict(_drawn_inputs(seed))
    spreads = {'L0_ffn_b_in': (0.0, 0.1),
     'L0_ffn_b_out': (0.0, 0.1),
     'L1_cond_b_f': (0.0, 0.8),
     'L1_cond_b_i': (0.0, 0.8),
     'L1_cond_b_h': (0.0, 0.8)}
    factors = {'L1_cond_W_f': 8.0,
     'L1_cond_W_i': 8.0,
     'L1_cond_W_h': 8.0,
     'L1_ffn_gate_weight': 8.0,
     'L1_ffn_shared_gate_up': 8.0,
     'L1_ffn_shared_down': 8.0,
     'L1_ffn_experts_gate_up': 8.0,
     'L1_ffn_experts_down': 8.0}
    for name, (base, spread) in spreads.items():
        noise = np.random.default_rng([zlib.crc32(name.encode()), seed]).standard_normal(out[name].shape)
        drawn = base * np.exp(spread * noise) if base else spread * noise
        out[name] = jnp.asarray(drawn.astype(out[name].dtype))
    for name, factor in factors.items():
        out[name] = (out[name] * factor).astype(out[name].dtype)
    return out
```

```python
import concourse.bass as bass
from concourse import mybir
from contextlib import ExitStack

F32 = mybir.dt.float32
F16 = mybir.dt.float16
BF16 = mybir.dt.bfloat16
I32 = mybir.dt.int32
U32 = mybir.dt.uint32
ALU = mybir.AluOpType
ACT = mybir.ActivationFunctionType
AX = mybir.AxisListType
ABSMAX = bass.bass_isa.ReduceOp.absmax

P = 128
BATCH, SEQ, D = 2, 1024, 256
TOK = BATCH * SEQ
DC = D // P
FF = 1024
FC = FF // P
E = 8
TOPK = 2
I = 938
IC = -(-I // P)
HALF = I // 2
PAIRS = 2 * DC
DU = IC * D // PAIRS
PAIR = I + DU
EW = PAIRS * PAIR
SHIFT = 1024
BANK = 512
BLK = 512
NB = TOK // BLK
T = TOK // P
JT = TOPK * TOK // P + E
KT = T + JT
RING = 4
FIRST = 2 * RING
PLANNED = 6 * RING
ROW = D + 4
INV, WGT, DST = D, D + 1, D + 2
SLOTS = (KT + 1) * P
OUTR = TOK + P
SHARED_SLOT = E - 1

ROUND = 1.5 * 2.0 ** 23
ROUND256 = ROUND * 256
EPS = 1e-8
TINY = 1e-30
TOP = 2.0 ** 14

STEPS = 4
BESIDE = {}
for n in range(3 * STEPS):
    BESIDE.setdefault(4 + 3 * n // 4, []).append((1 + n // STEPS, n % STEPS))
for n in range(2 * STEPS):
    BESIDE.setdefault(14 + n // 2, []).append((4 + n // STEPS, n % STEPS))
for n in range(2 * STEPS):
    BESIDE.setdefault(19 + n // 2, []).append((6 + n // STEPS, n % STEPS))
SENDS = {k: range(4 * (k - 4), 4 * (k - 3)) for k in range(4, 12)}


def adaln_ffn_moe(nc, x_t, cond_t, cond_w, w_in_t, w_out, bias, rec_w, gate_w, experts, out):
    moved = nc.dram_tensor("moved_rows", (SLOTS, ROW), F32, kind="Internal").ap()
    ctx = ExitStack()
    with ctx:
        def sb(name, shape, dt=F32):
            return ctx.enter_context(nc.sbuf_tensor(name, shape, dt))

        def sem(name):
            return ctx.enter_context(nc.semaphore(name))

        W = sb("weight_slots", [P, SHIFT + E * EW])
        Wh = W[:].bitcast(F16)

        def chunks(ap, c):
            return ap.rearrange("p (c n) -> p c n", c=c)

        def raw(e):
            return SHIFT + e * EW

        NX = DC * TOK
        x0 = chunks(W[:, 0:NX], DC)
        condw = chunks(W[:, NX:NX + DC * D], DC)
        condw_b = W[:, NX + DC * D:NX + 3 * DC * D].rearrange("p (b c n) -> p b c n", b=BATCH, c=DC)
        condw2 = chunks(W[:, NX + 3 * DC * D:NX + 4 * DC * D], DC)
        at = raw(1)
        win_raw = chunks(W[:, at:at + FC * D], FC)
        wout_q = win_raw
        at += FC * D
        win_q = W[:, at:at + DC * FF // 2].bitcast(BF16).rearrange("p (c f) -> p c f", c=DC)
        at += DC * FF // 2
        wout = chunks(W[:, at:at + FC * D], FC)
        at = raw(2)
        hid = chunks(W[:, at:at + FC * TOK], FC)
        fgate = chunks(W[:, at:at + NX], DC)
        igate = chunks(W[:, at + NX:at + 2 * NX], DC)
        cand = chunks(W[:, at + 2 * NX:at + 3 * NX], DC)
        at += 3 * NX
        rows = chunks(W[:, at:at + T * ROW], T)

        def gsum(b, c):
            g = at + b * BLK // SEQ * (T // BATCH * ROW) + (b % (SEQ // BLK) * DC + c) * BLK
            return W[:, g:g + BLK]

        x1 = chunks(W[:, raw(5):raw(5) + NX], DC)
        a5 = raw(5) + NX
        recw = W[:, a5:a5 + 3 * DC * D].rearrange("p (g c h) -> p g c h", g=3, c=DC)
        rt = chunks(W[:, a5:a5 + 8 * P], 8)
        top = W[:, a5 + 8 * P:a5 + 9 * P].rearrange("p (t n) -> p t n", t=T)
        topi = W[:, a5 + 9 * P:a5 + 10 * P].bitcast(U32).rearrange("p (t n) -> p t n", t=T)
        owner_f = W[0:1, a5:a5 + (JT + 1) * E].rearrange("p (j e) -> p j e", e=E)
        a6 = raw(6)
        xq = W[:, a6:a6 + NX].bitcast(BF16).rearrange("p (h c t) -> p h c t", h=2, c=DC)
        hT = chunks(W[:, a6:a6 + NX], DC)
        blank = W[:, a6 + NX:a6 + NX + ROW]
        assert a6 + NX + ROW <= SHARED_SLOT * EW

        cond = sb("cond", [P, DC, BATCH])
        ys = sb("ys", [P, DC, BATCH])
        ys2 = sb("ys2", [P, DC, BATCH])
        dinv = sb("dinv", [P, DC, BATCH])
        bia = sb("bia", [P, 16])
        b_in, b_out = bia[:, 0:FC], bia[:, FC:FC + DC]
        b_rec = bia[:, FC + DC:FC + 4 * DC].rearrange("p (g c) -> p g c", g=3)
        eps = sb("eps", [P, 1])
        big = sb("big", [P, 1])
        ident = sb("ident", [P, P])
        ident_h = sb("ident_h", [P, P], F16)
        before = sb("before", [P, P], BF16)
        ones = sb("ones", [P, P], BF16)
        notfirst = sb("notfirst", [P, E, T])
        wstat = sb("wstat", [P, 8, FC])
        amax = sb("amax", [P, 44])
        sc = sb("sc", [P, 8])
        gsc = sb("gsc", [P, FC])
        gatew = sb("gatew", [P, DC, E])
        rstat = sb("rstat", [P, 3, 4])
        r1 = sb("r1", [P, 8, T])
        topf = sb("topf", [P, TOPK, T])
        chosen = sb("chosen", [P, T, E], BF16)
        iota_i = sb("iota_i", [P, JT + 1], I32)
        iota_f = sb("iota_f", [P, JT + 1])
        rowid = sb("rowid", [P, T], I32)
        r8 = sb("r8", [P, 6, E])
        slot_of = sb("slot_of", [P, TOPK, T], U32)
        owner_r = sb("owner_r", [1, JT + 1])
        tile_v = sb("tile_v", [1, KT + 1], I32)
        tile_at = sb("tile_at", [1, KT + 1], I32)
        part_max = sb("part_max", [P, 2, 2])
        own_max = sb("own_max", [P, 2])
        all_max = sb("all_max", [P, 2])
        wscale = sb("wscale", [P, 2])
        winv = sb("winv", [P, 2, E + 1])
        xin = sb("xin", [P, RING, ROW])
        gup_inv = sb("gup_inv", [P, KT + 1])
        out_wgt = sb("out_wgt", [P, KT + 1])
        y_scale = sb("y_scale", [P, KT])
        dst = sb("dst", [P, KT + 1], I32)
        xT = sb("xT", [P, 2, DC, P], F16)
        work = sb("work", [P, 2 * I])
        silu = work[:, 0:I].rearrange("p (b n) -> p b n", b=2)
        h = work[:, I:2 * I]
        x0_hi = chunks(work[:, 0:DC * BLK], DC)
        x1r = chunks(work[:, 0:4 * D], 4)
        h_inv = sb("h_inv", [P, 3])
        hn = sb("hn", [P, IC * P])
        h_T = sb("h_T", [P, 2, IC, P], F16)
        yb = sb("yb", [P, RING, D])
        idx = sb("idx", [P, RING], U32)

        ps = ctx.enter_context(nc.psum_tensor("ps", [P, 8 * BANK], F32))

        def bank(b, a=0, n=BANK):
            return ps[:, b * BANK + a:b * BANK + a + n]

        def unit_views(slot, p, unit):
            a = slot * EW + p * PAIR + unit * I
            n = (I, DU)[unit]
            return W[:, a + SHIFT:a + SHIFT + n], Wh[:, 2 * a:2 * a + n], Wh[:, 2 * a + n:2 * a + 2 * n]

        ld_cond = sem("ld_cond")
        ld_small = sem("ld_small")
        ld_win = sem("ld_win")
        ld_wout = sem("ld_wout")
        ld_shared = sem("ld_shared")
        consts = sem("consts")
        ident_ok = sem("ident_ok")
        blank_ok = sem("blank_ok")
        blank_out = sem("blank_out")
        dve_step = sem("dve_step")
        pool_step = sem("pool_step")
        condw_ready = sem("condw_ready")
        dsum_done = sem("dsum_done")
        sqrt_done = sem("sqrt_done")
        dinv_ready = sem("dinv_ready")
        xs_mm = sem("xs_mm")
        x0_ready = sem("x0_ready")
        xmax_part = sem("xmax_part")
        xmax_all = sem("xmax_all")
        winq_ready = sem("winq_ready")
        wint_done = sem("wint_done")
        win_ready = sem("win_ready")
        wstat_ready = sem("wstat_ready")
        wq_step = sem("wq_step")
        gsc_ready = sem("gsc_ready")
        xround = sem("xround")
        xq_ready = sem("xq_ready")
        mm1_done = sem("mm1_done")
        gelu_done = sem("gelu_done")
        hmax_part = sem("hmax_part")
        hmax_all = sem("hmax_all")
        hsc_ready = sem("hsc_ready")
        hround = sem("hround")
        hq_ready = sem("hq_ready")
        woutq_ready = sem("woutq_ready")
        xb_ready = sem("xb_ready")
        mm2_done = sem("mm2_done")
        x1_ready = sem("x1_ready")
        rec_done = sem("rec_done")
        gates_done = sem("gates_done")
        inv_ready = sem("inv_ready")
        rec_step = sem("rec_step")
        info_ready = sem("info_ready")
        decay_ready = sem("decay_ready")
        hid_ready = sem("hid_ready")
        x1t_done = sem("x1t_done")
        x1r_ready = sem("x1r_ready")
        rowt_done = sem("rowt_done")
        rows_raw = sem("rows_raw")
        rows_ready = sem("rows_ready")
        rows_low = sem("rows_low")
        rows_high = sem("rows_high")
        logits_done = sem("logits_done")
        logits_kept = sem("logits_kept")
        shifted = sem("shifted")
        exp_done = sem("exp_done")
        chosen_ready = sem("chosen_ready")
        rank_done = sem("rank_done")
        ranks_kept = sem("ranks_kept")
        route_ready = sem("route_ready")
        weight_set = sem("weight_set")
        sent = sem("sent")
        owner_ready = sem("owner_ready")
        wmax_part = sem("wmax_part")
        wmax_all = sem("wmax_all")
        wscale_ready = sem("wscale_ready")
        high_done = sem("high_done")
        low_done = sem("low_done")
        split_done = sem("split_done")
        xT_raw = sem("xT_raw")
        xT_ready = sem("xT_ready")
        meta_ready = sem("meta_ready")
        g_done = sem("g_done")
        u_done = sem("u_done")
        silu_ready = sem("silu_ready")
        h_ready = sem("h_ready")
        h_step = sem("h_step")
        yscale_ready = sem("yscale_ready")
        hn_ready = sem("hn_ready")
        t_done = sem("t_done")
        hT_high = sem("hT_high")
        hT_low = sem("hT_low")
        d_done = sem("d_done")
        y_ready = sem("y_ready")
        idx_ready = sem("idx_ready")
        add_turn = sem("add_turn")
        added = sem("added")
        ld_x = [sem(f"ld_x{b}") for b in range(NB)]
        stored = [sem(f"stored{u}") for u in range(4)]
        xin_ready = [sem(f"xin_ready{u}") for u in range(RING)]
        ld_exp = [sem(f"ld_exp{e}") for e in range(E)]

        block = ctx.enter_context(nc.Block())

        @block.sync
        def _(sp):
            sp.dma_start(cond[:], cond_t).then_inc(ld_cond, 16)
            sp.dma_start(condw, cond_w).then_inc(ld_cond, 16)
            for b in range(NB):
                t = slice(b * BLK, (b + 1) * BLK)
                sp.dma_start(x1[:, :, t], x_t[:, :, t]).then_inc(ld_x[b], 16)
            sp.dma_start(win_raw, w_in_t).then_inc(ld_win, 16)
            sp.dma_start(bia[:], bias).then_inc(ld_small, 16)
            sp.dma_start(wout, w_out).then_inc(ld_wout, 16)
            sp.dma_start(recw, rec_w).then_inc(ld_small, 16)
            sp.dma_start(gatew[:], gate_w).then_inc(ld_small, 16)
            sp.dma_start(W[:, raw(SHARED_SLOT):raw(SHARED_SLOT) + EW], experts[E]).then_inc(ld_shared, 16)
            sp.wait_ge(blank_ok, 1)
            sp.dma_start(moved[TOK:SLOTS, :].rearrange("(j p) n -> p j n", p=P),
                         blank.unsqueeze(1).to_broadcast([P, JT + 1, ROW])).then_inc(blank_out, 16)

            def load_expert(e):
                sp.dma_start(W[:, raw(e):raw(e) + EW], experts[e]).then_inc(ld_exp[e], 16)

            sp.wait_ge(xq_ready, NB)
            sp.wait_ge(xs_mm, NB * DC)
            load_expert(0)
            sp.wait_ge(mm2_done, NB * DC)
            load_expert(1)
            for t in range(T):
                sp.wait_ge(x1r_ready, t + 1)
                sp.dma_start(out[t * P:(t + 1) * P, :], x1r[:, t % 4, :]).then_inc(stored[t % 4], 16)

            def store_rows(t0, n):
                for t in range(t0, t0 + n):
                    sp.wait_ge(rows_ready, t + 1)
                    sp.dma_start(moved[t * P:(t + 1) * P, :], rows[:, t, :]).then_inc(
                        rows_low if t < T // 2 else rows_high, 16)

            def load_x(i, u):
                sp.dma_start(xin[:, u, :], moved[bass.ds(i * P, P), :]).then_inc(xin_ready[u], 16)

            store_rows(0, T // 2)
            sp.wait_ge(rows_low, 16 * T // 2)
            for i in range(RING):
                load_x(i, i)
            sp.wait_ge(hid_ready, BATCH * DC)
            load_expert(2)
            load_expert(3)
            for i in range(RING, PLANNED):
                if i == 5:
                    store_rows(T // 2, 4)
                if i == 6:
                    store_rows(T // 2 + 4, 4)
                if i == T // 2:
                    sp.wait_ge(rows_high, 16 * T // 2)
                    sp.wait_ge(owner_ready, 1)
                    sp.wait_ge(rowt_done, T)
                    load_expert(5)
                sp.wait_ge(xT_ready, i - RING + 1)
                sp.wait_ge(meta_ready, i - RING + 1)
                if i == T:
                    sp.wait_ge(sent, 16 * TOPK * T)
                    sp.wait_ge(blank_out, 16)
                    load_expert(4)
                load_x(i, i % RING)
                if i == 22:
                    sp.wait_ge(d_done, T)
                    load_expert(6)
                    load_expert(7)
            with sp.Fori(PLANNED // RING, KT // RING) as g:
                for u in range(RING):
                    sp.wait_ge(xT_ready, g * RING + (u - RING + 1))
                    sp.wait_ge(meta_ready, g * RING + (u - RING + 1))
                    load_x(g * RING + u, u)
            sp.wait_ge(xT_ready, KT - RING + 1)
            sp.wait_ge(meta_ready, KT - RING + 1)
            load_x(KT, 0)
            sp.wait_ge(xin_ready[0], 16 * (KT // RING + 1))
            sp.wait_ge(added, 16 * (KT + 2))

        @block.gpsimd
        def _(pool):
            G = nc.gpsimd
            G.memset(ident[:], 0.0).then_inc(pool_step, 1)
            G.memset(before[:], 1.0).then_inc(pool_step, 1)
            G.memset(notfirst[:], 1.0).then_inc(pool_step, 1)
            G.memset(blank, 0.0).then_inc(pool_step, 1)
            G.iota(iota_i[:], [[1, JT + 1]], base=0, channel_multiplier=0).then_inc(pool_step, 1)
            G.memset(eps[:], EPS).then_inc(consts, 1)
            G.memset(big[:], ROUND).then_inc(consts, 1)
            G.memset(ones[:], 1.0).then_inc(consts, 1)
            G.iota(rowid[:], [[P, T]], base=0, channel_multiplier=1).then_inc(consts, 1)
            G.memset(hn[:, I:IC * P], 0.0).then_inc(consts, 1)
            G.memset(tile_v[0:1, 0:T], 0).then_inc(consts, 1)
            G.memset(tile_at[0:1, 0:T], 2 * SHARED_SLOT * EW).then_inc(consts, 1)
            pool.wait_ge(pool_step, 5)
            G.affine_select(out=ident[:], in_=ident[:], compare_op=ALU.not_equal, fill=1.0, base=0,
                            pattern=[[-1, P]], channel_multiplier=1).then_inc(ident_ok, 1)
            G.affine_select(out=before[:], in_=before[:], compare_op=ALU.is_gt, fill=0.0, base=0,
                            pattern=[[1, P]], channel_multiplier=-1).then_inc(consts, 1)
            G.memset(notfirst[:, :, 0:1], 0.0).then_inc(consts, 1)
            G.iota(blank[:, DST:DST + 1].bitcast(I32), [[0, 1]], base=TOK, channel_multiplier=1)\
                .then_inc(blank_ok, 1)
            G.tensor_copy(iota_f[:], iota_i[:]).then_inc(consts, 1)
            pool.wait_ge(ident_ok, 1)
            G.tensor_copy(ident_h[:], ident[:]).then_inc(consts, 1)
            pool.wait_ge(blank_ok, 1)
            for q in range(2):
                G.dma_start(out[TOK + q * 64:TOK + q * 64 + 64, :], blank[q * 64:q * 64 + 64, 0:D])\
                    .then_inc(added, 16)
            pool.wait_ge(xmax_part, 1)
            G.partition_all_reduce(amax[:, 9:10], amax[:, 8:9], P, ABSMAX).then_inc(xmax_all, 1)
            pool.wait_ge(ld_small, 16 * 3)
            pool.wait_ge(xs_mm, NB * DC)
            for c in range(DC):
                G.tensor_scalar(x1[:, c, :], x1[:, c, :], b_out[:, c:c + 1], 1.0, ALU.add, ALU.mult)\
                    .then_inc(xb_ready, 1)
            pool.wait_ge(wstat_ready, 1)
            pool.wait_ge(wint_done, 2 * DC)
            for f in range(FC):
                G.tensor_scalar(wout[:, f, :], wout[:, f, :], wstat[:, 6, f:f + 1], ROUND, ALU.mult, ALU.add)\
                    .then_inc(wq_step, 1)
            pool.wait_ge(wq_step, FC)
            G.tensor_scalar(wout, wout, ROUND + 127.0, ROUND - 128.0, ALU.min, ALU.max).then_inc(wq_step, 1)
            pool.wait_ge(wq_step, FC + 1)
            for f in range(FC):
                G.tensor_scalar(wout_q[:, f, :], wout[:, f, :], -ROUND, wstat[:, 7, f:f + 1], ALU.add, ALU.mult)\
                    .then_inc(woutq_ready, 1)
            pool.wait_ge(hmax_part, 1)
            G.partition_all_reduce(amax[:, 43:44], amax[:, 42:43], P, ABSMAX).then_inc(hmax_all, 1)

            def full_max(v):
                pool.wait_ge(wmax_part, v + 1)
                G.partition_all_reduce(all_max[:], own_max[:], P, ABSMAX).then_inc(wmax_all, 1)

            def high_halves(slot, v, pairs):
                pool.wait_ge(wscale_ready, v + 1)
                for p in pairs:
                    for unit in range(2):
                        src, hi, _ = unit_views(slot, p, unit)
                        pool.wait_ge(low_done, 2 * (v * PAIRS + p) + unit + 1)
                        G.tensor_scalar(hi, src, wscale[:, unit:unit + 1], 0.0, ALU.mult, ALU.add)\
                            .then_inc(high_done, 1)

            for slot, v in ((SHARED_SLOT, 0), (0, 1)):
                full_max(v)
                high_halves(slot, v, range(PAIRS))
            n = 0
            for b in range(NB):
                for c in range(DC):
                    n += 1
                    t = slice(b * BLK, (b + 1) * BLK)
                    pool.wait_ge(inv_ready, n)
                    G.tensor_tensor(fgate[:, c, t], fgate[:, c, t], gsum(b, c), ALU.mult).then_inc(rec_step, 1)
                    G.tensor_tensor(igate[:, c, t], igate[:, c, t], gsum(b, c), ALU.mult).then_inc(rec_step, 1)
                    pool.wait_ge(rec_step, 2 * n - 1)
                    G.tensor_scalar(fgate[:, c, t], fgate[:, c, t], EPS, 1.0, ALU.add, ALU.mult)\
                        .then_inc(decay_ready, 1)
                    pool.wait_ge(rec_step, 2 * n)
                    G.tensor_tensor(igate[:, c, t], igate[:, c, t], cand[:, c, t], ALU.mult).then_inc(info_ready, 1)

            def add(i, u):
                G.tensor_copy(idx[:, u:u + 1].bitcast(I32), dst[:, bass.ds(i, 1)]).then_inc(idx_ready, 1)
                pool.wait_ge(y_ready, i + 1)
                pool.wait_ge(added, (i + 2) * 16)
                pool.wait_ge(idx_ready, i + 1)
                pool.sem_inc(add_turn, 1)
                G.indirect_dma_start(out, bass.IndirectOffsetOnAxis(ap=idx[:, u:u + 1], axis=0), yb[:, u, :],
                                     None, compute_op=ALU.add).then_inc(added, 16)

            for k in range(PLANNED):
                if k == 2:
                    for u in range(4):
                        pool.wait_ge(stored[u], 16 * T // 4)
                if k == 4:
                    pool.wait_ge(route_ready, 1)
                    pool.wait_ge(blank_out, 16)
                for n in SENDS.get(k, ()):
                    choice, t = divmod(n, T)
                    if n == T:
                        pool.wait_ge(sent, 16 * T)
                        G.tensor_copy(rows[:, :, WGT:WGT + 1], r1[:, 5, :].unsqueeze(2)).then_inc(weight_set, 1)
                        pool.wait_ge(weight_set, 1)
                    G.indirect_dma_start(moved, bass.IndirectOffsetOnAxis(ap=slot_of[:, choice, t:t + 1], axis=0),
                                         rows[:, t, :], None).then_inc(sent, 16)
                if k >= 2:
                    pool.wait_ge(meta_ready, k - 1)
                    add(k - 2, (k - 2) % RING)
                for e, step in BESIDE.get(k, ()):
                    if step == 1:
                        full_max(e + 1)
                    if step >= 2:
                        high_halves(e, e + 1, range(2 * step - 4, 2 * step - 2))
            with pool.Fori(PLANNED // RING, KT // RING) as g:
                for u in range(RING):
                    add(g * RING + (u - 2), (u - 2) % RING)
            for i in range(KT - 2, KT):
                add(i, i % RING)

        @block.scalar
        def _(act):
            A = nc.scalar.activation
            act.wait_ge(consts, 2)
            act.wait_ge(dsum_done, 1)
            A(dinv[:].rearrange("p c b -> p (c b)"), bank(7, 0, DC * BATCH), ACT.Sqrt, bias=eps[:, 0:1])\
                .then_inc(sqrt_done, 1)
            act.wait_ge(dinv_ready, 1)
            n = 0
            for b in range(NB):
                for c in range(DC):
                    n += 1
                    act.wait_ge(xs_mm, n)
                    bb = b * BLK // SEQ
                    A(x0[:, c, b * BLK:(b + 1) * BLK], bank(n - 1), ACT.Copy, scale=dinv[:, c, bb:bb + 1])\
                        .then_inc(x0_ready, 1)
            for c in range(DC):
                for half in range(2):
                    act.wait_ge(wint_done, 2 * c + half + 1)
                    A(win_q[:, c, half * BANK:(half + 1) * BANK], bank(2 * c + half), ACT.Copy).then_inc(win_ready, 1)
            act.wait_ge(gsc_ready, 1)
            for b in range(NB):
                t = slice(b * BLK, (b + 1) * BLK)
                A(x0[:, :, t], x0[:, :, t], ACT.Identity, bias=big[:, 0:1], scale=sc[:, 2:3]).then_inc(xround, 1)
            for g in range(NB * FC):
                b, f = divmod(g, FC)
                act.wait_ge(mm1_done, g + 1)
                A(hid[:, f, b * BLK:(b + 1) * BLK], bank((g + 4) % 8), ACT.Gelu, bias=b_in[:, f:f + 1],
                  scale=gsc[:, f:f + 1]).then_inc(gelu_done, 1)
            act.wait_ge(hsc_ready, 1)
            for b in range(NB):
                for f in range(FC):
                    piece = hid[:, f, b * BLK:(b + 1) * BLK]
                    A(piece, piece, ACT.Identity, bias=big[:, 0:1], scale=sc[:, 4:5]).then_inc(hround, 1)

            def gates(n):
                b, c = divmod(n, DC)
                t = slice(b * BLK, (b + 1) * BLK)
                act.wait_ge(rec_done, n + 1)
                a = 3 * (n % 2)
                A(fgate[:, c, t], bank(a), ACT.Sigmoid, bias=b_rec[:, 0, c:c + 1])
                A(igate[:, c, t], bank(a + 1), ACT.Sigmoid, bias=b_rec[:, 1, c:c + 1])
                A(cand[:, c, t], bank(a + 2), ACT.Identity, bias=b_rec[:, 2, c:c + 1]).then_inc(gates_done, 1)

            for b in range(NB):
                gates(DC * b)
                gates(DC * b + 1)
                for t in range(4 * b, 4 * b + 4):
                    act.wait_ge(x1t_done, t + 1)
                    if t >= 4:
                        act.wait_ge(stored[t % 4], 16 * (t // 4))
                    A(x1r[:, t % 4, :], bank(6 + t % 2, 0, D), ACT.Copy).then_inc(x1r_ready, 1)

            def drain_rows(t0):
                for t in range(t0, t0 + 4):
                    act.wait_ge(rowt_done, t + 1)
                    if t >= 4:
                        act.wait_ge(rows_ready, t - 3)
                    A(yb[:, t % 4, :], bank(6 + t % 2, D, D), ACT.Copy).then_inc(rows_raw, 1)

            drain_rows(0)
            drain_rows(4)

            gate_ps = ps[:, 0:2 * BANK].rearrange("p (b n) -> p b n", b=2)[:, :, 0:HALF]

            def silu_of(k, first=False):
                act.wait_ge(g_done, k + 1)
                act.wait_ge(meta_ready, k + 1)
                if not first:
                    act.wait_ge(h_ready, k)
                A(silu, gate_ps, ACT.Silu, scale=gup_inv[:, bass.ds(k, 1)]).then_inc(silu_ready, 1)

            def drain_y(i, u):
                act.wait_ge(d_done, i + 1)
                act.wait_ge(yscale_ready, i + 1)
                A(yb[:, u, :], bank(6, 0, D), ACT.Copy, scale=y_scale[:, bass.ds(i, 1)]).then_inc(y_ready, 1)

            def drain_x(k):
                act.wait_ge(xT_raw, k + 1)
                A(xT[:].rearrange("p s c t -> p (s c t)"), bank(7, 0, D).bitcast(F16), ACT.Copy).then_inc(xT_ready, 1)

            def high_h(k):
                act.wait_ge(t_done, k + 1)
                A(h_T[:, 0].rearrange("p c t -> p (c t)"), ps[:, 4 * BANK:6 * BANK], ACT.Copy).then_inc(hT_high, 1)

            def norm_h(k):
                act.wait_ge(h_step, 3 * k + 3)
                A(hn[:, 0:I], h, ACT.Copy, scale=h_inv[:, 2:3]).then_inc(hn_ready, 1)

            drain_x(0)
            for u in range(4):
                act.wait_ge(stored[u], 16 * T // 4)
            for k in range(FIRST):
                silu_of(k, k == 0)
                if k >= 2:
                    if k == 2:
                        act.wait_ge(rows_ready, T)
                    if k >= 2 + RING:
                        act.wait_ge(added, (k - 3) * 16)
                    drain_y(k - 2, (k - 2) % RING)
                drain_x(k + 1)
                if k >= 1:
                    high_h(k - 1)
                if k == 0:
                    act.wait_ge(consts, 11)
                norm_h(k)
                if k < 2:
                    drain_rows(8 + 4 * k)
                if k == 2:
                    act.wait_ge(shifted, 1)
                    A(rt[:, 1, :], rt[:, 0, :], ACT.Exp).then_inc(exp_done, 1)
            with act.Fori(FIRST // RING, KT // RING) as g:
                for u in range(RING):
                    k = g * RING + u
                    silu_of(k)
                    act.wait_ge(added, (g * RING + (u - 3)) * 16)
                    drain_y(g * RING + (u - 2), (u - 2) % RING)
                    drain_x(k + 1)
                    high_h(g * RING + (u - 1))
                    norm_h(k)
            act.wait_ge(added, 16 * (KT - 3))
            drain_y(KT - 2, (KT - 2) % RING)
            high_h(KT - 1)
            act.wait_ge(added, 16 * (KT - 2))
            drain_y(KT - 1, (KT - 1) % RING)

        @block.vector
        def _(dve):
            steps = [0]

            def then(ins):
                steps[0] += 1
                ins.then_inc(dve_step, 1)
                dve.wait_ge(dve_step, steps[0])

            V = nc.vector
            dve.wait_ge(ld_cond, 32)
            then(V.tensor_scalar(ys[:], cond[:], 1.0 / 16.0, None, ALU.mult))
            for b in range(BATCH):
                for c in range(DC):
                    V.tensor_scalar(condw_b[:, b, c, :], condw[:, c, :], ys[:, c, b:b + 1], None, ALU.mult)\
                        .then_inc(condw_ready, 1)
            V.tensor_tensor(ys2[:], ys[:], ys[:], ALU.mult).then_inc(condw_ready, 1)
            V.tensor_tensor(condw2, condw, condw, ALU.mult).then_inc(condw_ready, 1)
            dve.wait_ge(sqrt_done, 1)
            V.reciprocal(dinv[:], dinv[:]).then_inc(dinv_ready, 1)

            def weight_scale(w, a):
                then(V.tensor_reduce(wstat[:, a, :], w, AX.X, ALU.max, apply_absolute_value=True))
                then(V.tensor_scalar(wstat[:, a, :], wstat[:, a, :], EPS, None, ALU.max))
                then(V.reciprocal(wstat[:, a + 1, :], wstat[:, a, :]))
                V.tensor_scalar(wstat[:, a + 2, :], wstat[:, a + 1, :], 127.0, None, ALU.mult)
                return V.tensor_scalar(wstat[:, a + 3, :], wstat[:, a, :], 1.0 / 127.0, None, ALU.mult)

            dve.wait_ge(ld_win, 16)
            then(weight_scale(win_raw, 0))
            for f in range(FC):
                ins = V.tensor_scalar(win_raw[:, f, :], win_raw[:, f, :], wstat[:, 2, f:f + 1], ROUND, ALU.mult,
                                      ALU.add)
            then(ins)
            then(V.tensor_scalar(win_raw, win_raw, ROUND + 127.0, ROUND - 128.0, ALU.min, ALU.max))
            V.tensor_scalar(win_raw, win_raw, ROUND, None, ALU.subtract).then_inc(winq_ready, 1)
            n = 0
            for b in range(NB):
                for c in range(DC):
                    n += 1
                    dve.wait_ge(x0_ready, n)
                    ins = V.tensor_reduce(amax[:, n - 1:n], x0[:, c, b * BLK:(b + 1) * BLK], AX.X, ALU.max,
                                          apply_absolute_value=True)
                    if n == 2:
                        dve.wait_ge(ld_wout, 16)
                        weight_scale(wout, 4).then_inc(wstat_ready, 1)
            then(ins)
            V.tensor_reduce(amax[:, 8:9], amax[:, 0:8], AX.X, ALU.max).then_inc(xmax_part, 1)
            dve.wait_ge(xmax_all, 1)
            then(V.tensor_scalar(sc[:, 0:1], amax[:, 9:10], EPS, None, ALU.max))
            then(V.reciprocal(sc[:, 1:2], sc[:, 0:1]))
            V.tensor_scalar(sc[:, 2:3], sc[:, 1:2], 32767.0, None, ALU.mult)
            then(V.tensor_scalar(sc[:, 3:4], sc[:, 0:1], 1.0 / 32767.0, None, ALU.mult))
            V.tensor_scalar(gsc[:], wstat[:, 3, :], sc[:, 3:4], None, ALU.mult).then_inc(gsc_ready, 1)
            for b in range(NB):
                t = slice(b * BLK, (b + 1) * BLK)
                dve.wait_ge(xround, b + 1)
                then(V.tensor_scalar(x0[:, :, t], x0[:, :, t], ROUND - 32768.0, ROUND + 32767.0, ALU.max, ALU.min))
                then(V.tensor_scalar(x0_hi, x0[:, :, t], ROUND, ROUND256, ALU.subtract, ALU.add))
                then(V.tensor_scalar(xq[:, 0, :, t], x0_hi, ROUND256, None, ALU.subtract))
                V.scalar_tensor_tensor(xq[:, 1, :, t], x0[:, :, t], ROUND, xq[:, 0, :, t], ALU.subtract,
                                       ALU.subtract).then_inc(xq_ready, 1)
            for n in range(NB * FC):
                b, f = divmod(n, FC)
                dve.wait_ge(gelu_done, n + 1)
                ins = V.tensor_reduce(amax[:, 10 + n:11 + n], hid[:, f, b * BLK:(b + 1) * BLK], AX.X, ALU.max,
                                      apply_absolute_value=True)
            then(ins)
            V.tensor_reduce(amax[:, 42:43], amax[:, 10:42], AX.X, ALU.max).then_inc(hmax_part, 1)
            dve.wait_ge(hmax_all, 1)
            then(V.tensor_scalar(sc[:, 5:6], amax[:, 43:44], EPS, None, ALU.max))
            then(V.reciprocal(sc[:, 6:7], sc[:, 5:6]))
            V.tensor_scalar(sc[:, 7:8], sc[:, 5:6], 1.0 / 32767.0, None, ALU.mult)
            V.tensor_scalar(sc[:, 4:5], sc[:, 6:7], 32767.0, None, ALU.mult).then_inc(hsc_ready, 1)

            def round_hidden(b):
                for f in range(FC):
                    piece = hid[:, f, b * BLK:(b + 1) * BLK]
                    dve.wait_ge(hround, b * FC + f + 1)
                    then(V.tensor_scalar(piece, piece, ROUND - 32768.0, ROUND + 32767.0, ALU.max, ALU.min))
                    V.tensor_scalar(piece, piece, ROUND, None, ALU.subtract).then_inc(hq_ready, 1)

            def drain_x1(b):
                dve.wait_ge(xb_ready, DC)
                for c in range(DC):
                    g = DC * b + c
                    t = slice(b * BLK, (b + 1) * BLK)
                    dve.wait_ge(mm2_done, g + 1)
                    V.scalar_tensor_tensor(x1[:, c, t], bank(g), sc[:, 7:8], x1[:, c, t], ALU.mult, ALU.add)\
                        .then_inc(x1_ready, 1)

            def maxima(slot, v, half):
                pairs = W[:, raw(slot):raw(slot) + EW].rearrange("p (q n) -> p q n", q=PAIRS)
                q = slice(2 * half, 2 * half + 2)
                V.tensor_reduce(part_max[:, 0, half:half + 1], pairs[:, q, 0:I], AX.XY, ALU.max,
                                apply_absolute_value=True)
                ins = V.tensor_reduce(part_max[:, 1, half:half + 1], pairs[:, q, I:PAIR], AX.XY, ALU.max,
                                      apply_absolute_value=True)
                if half:
                    then(ins)
                    V.tensor_reduce(own_max[:], part_max[:], AX.X, ALU.max).then_inc(wmax_part, 1)

            def weight_scales(v):
                dve.wait_ge(wmax_all, v + 1)
                then(V.tensor_scalar(winv[:, :, v], all_max[:], TINY, 1.0 / TOP, ALU.max, ALU.mult))
                V.reciprocal(wscale[:], winv[:, :, v]).then_inc(wscale_ready, 1)
                dve.wait_ge(wscale_ready, v + 1)

            def low_halves(slot, v, pairs):
                for p in pairs:
                    for unit in range(2):
                        src, hi, lo = unit_views(slot, p, unit)
                        n = 2 * (v * PAIRS + p) + unit
                        dve.wait_ge(high_done, n + 1)
                        V.scalar_tensor_tensor(lo, src, wscale[:, unit:unit + 1], hi, ALU.mult, ALU.subtract)\
                            .then_inc(low_done, 1)
                if p == PAIRS - 1:
                    dve.wait_ge(low_done, 2 * (v + 1) * PAIRS + 1)
                    dve.sem_inc(split_done, 1)

            def weight_step(e, step):
                if step == 0:
                    dve.wait_ge(ld_exp[e], 16)
                if step < 2:
                    maxima(e, e + 1, step)
                else:
                    if step == 2:
                        weight_scales(e + 1)
                    low_halves(e, e + 1, range(2 * step - 4, 2 * step - 2))

            dve.sem_inc(low_done, 1)
            round_hidden(0)
            round_hidden(1)
            dve.wait_ge(ld_shared, 16)
            for half in range(2):
                maxima(SHARED_SLOT, 0, half)
            round_hidden(2)
            drain_x1(0)
            weight_scales(0)
            low_halves(SHARED_SLOT, 0, range(PAIRS))
            round_hidden(3)
            drain_x1(1)
            weight_step(0, 0)
            weight_step(0, 1)
            drain_x1(2)
            weight_step(0, 2)
            weight_step(0, 3)
            drain_x1(NB - 1)

            def gate_sum(b, c):
                t = slice(b * BLK, (b + 1) * BLK)
                n = DC * b + c + 1
                dve.wait_ge(gates_done, n)
                then(V.scalar_tensor_tensor(gsum(b, c), fgate[:, c, t], EPS, igate[:, c, t], ALU.add, ALU.add))
                V.reciprocal(gsum(b, c), gsum(b, c)).then_inc(inv_ready, 1)

            def recur(bb, c):
                t = slice(bb * SEQ, (bb + 1) * SEQ)
                dve.wait_ge(decay_ready, DC * (bb + 1) * (SEQ // BLK))
                f = fgate[:, c, t]
                V.tensor_tensor_scan(hT[:, c, t], f, f, cond[:, c, bb:bb + 1], ALU.mult, ALU.bypass)
                dve.wait_ge(info_ready, DC * (bb + 1) * (SEQ // BLK))
                suffix = cand[:, c, t]
                then(V.tensor_tensor_scan(suffix[:, ::-1], f[:, ::-1], f[:, ::-1], 1.0, ALU.mult, ALU.bypass))
                i = igate[:, c, t]
                then(V.tensor_tensor(i, i, suffix, ALU.mult))
                then(V.tensor_tensor_scan(suffix, i, i, 0.0, ALU.add, ALU.bypass))
                V.tensor_tensor(hT[:, c, t], hT[:, c, t], suffix, ALU.add).then_inc(hid_ready, 1)

            def make_rows(t0):
                dve.wait_ge(rows_raw, t0 + 4)
                then(V.tensor_reduce(rstat[:, 0, :], yb[:], AX.X, ALU.max, apply_absolute_value=True))
                then(V.tensor_scalar(rstat[:, 1, :], rstat[:, 0, :], TINY, 1.0 / TOP, ALU.max, ALU.mult))
                then(V.reciprocal(rstat[:, 2, :], rstat[:, 1, :]))
                r = rows[:, t0:t0 + 4, :]
                V.tensor_copy(r[:, :, INV:INV + 1], rstat[:, 1, :].unsqueeze(2))
                V.memset(r[:, :, WGT:WGT + 1], 1.0)
                V.memset(r[:, :, ROW - 1:ROW], 0.0)
                V.tensor_copy(r[:, :, DST:DST + 1].bitcast(I32), rowid[:, t0:t0 + 4].unsqueeze(2))
                for q in range(4):
                    halves = r[:, q, 0:D].bitcast(F16)
                    ins = V.tensor_scalar(halves[:, 0:D], yb[:, q, :], rstat[:, 2, q:q + 1], None, ALU.mult)
                then(ins)
                for q in range(4):
                    halves = r[:, q, 0:D].bitcast(F16)
                    V.scalar_tensor_tensor(halves[:, D:2 * D], yb[:, q, :], rstat[:, 2, q:q + 1], halves[:, 0:D],
                                           ALU.mult, ALU.subtract).then_inc(rows_ready, 1)

            gate_sum(0, 0)
            gate_sum(0, 1)
            gate_sum(1, 0)
            gate_sum(1, 1)
            gate_sum(2, 0)
            recur(0, 0)
            gate_sum(2, 1)
            recur(0, 1)
            gate_sum(3, 0)
            gate_sum(3, 1)
            dve.wait_ge(consts, 11)
            make_rows(0)
            make_rows(4)
            recur(1, 0)
            recur(1, 1)

            def te(i):
                return rt[:, i, :].rearrange("p (t e) -> p t e", e=E)

            def per_tile(i):
                return r1[:, i, :].unsqueeze(2).to_broadcast([P, T, E])

            def choose():
                logits = te(7)
                dve.wait_ge(logits_kept, 1)
                then(V.tensor_reduce(r1[:, 0, :], logits, AX.X, ALU.max))
                V.tensor_tensor(te(0), logits, per_tile(0), ALU.subtract).then_inc(shifted, 1)
                dve.wait_ge(exp_done, 1)
                then(V.tensor_reduce(r1[:, 1, :], te(1), AX.X, ALU.add))
                then(V.reciprocal(r1[:, 2, :], r1[:, 1, :]))
                then(V.tensor_tensor(te(2), te(1), per_tile(2), ALU.mult))
                for t in range(T):
                    ins = V.max(top[:, t, :], te(2)[:, t, :])
                then(ins)
                for t in range(T):
                    ins = V.max_index(topi[:, t, :], top[:, t, :], te(2)[:, t, :])
                then(ins)
                V.tensor_copy(topf[:], topi[:, :, 0:TOPK].rearrange("p t k -> p k t"))
                then(V.tensor_tensor(r1[:, 3, :], top[:, :, 0], top[:, :, 1], ALU.add))
                then(V.tensor_scalar(r1[:, 3, :], r1[:, 3, :], EPS, None, ALU.add))
                then(V.reciprocal(r1[:, 4, :], r1[:, 3, :]))
                V.tensor_tensor(r1[:, 5, :], top[:, :, 1], r1[:, 4, :], ALU.mult)
                V.tensor_tensor(r1[:, 6, :], top[:, :, 0], r1[:, 4, :], ALU.mult)
                experts_row = iota_f[:, 0:E].unsqueeze(1).to_broadcast([P, T, E])
                for k in range(TOPK):
                    ins = V.tensor_tensor(te(3 + k), experts_row, topf[:, k, :].unsqueeze(2).to_broadcast([P, T, E]),
                                          ALU.is_equal)
                then(ins)
                V.tensor_tensor(chosen[:], te(3), te(4), ALU.add).then_inc(chosen_ready, 1)

            def place():
                dve.wait_ge(rank_done, 1)
                V.tensor_copy(te(7), bank(7, D, P).rearrange("p (t e) -> p t e", e=E))
                et = rt[:, 5, :].rearrange("p (e t) -> p e t", e=E)
                V.tensor_copy(et, bank(7, D + P, P).rearrange("p (t e) -> p e t", e=E)).then_inc(ranks_kept, 1)
                dve.wait_ge(ranks_kept, 1)
                then(V.tensor_tensor_scan(rt[:, 6, :], notfirst.rearrange("p e t -> p (e t)"), rt[:, 5, :], 0.0,
                                          ALU.mult, ALU.add))
                count = rt[:, 6, :].rearrange("p (e t) -> p e t", e=E)
                then(V.tensor_scalar(r8[:, 0, :], count[:, :, T - 1], 1.0 / P, 0.5 - 0.5 / P, ALU.mult, ALU.add))
                then(V.tensor_scalar(r8[:, 1, :], r8[:, 0, :], ROUND, ROUND, ALU.add, ALU.subtract))
                then(V.tensor_scalar(r8[:, 2, :], r8[:, 1, :], 1.0, None, ALU.max))
                then(V.tensor_tensor_scan(r8[:, 3, :], r8[:, 2, :], r8[:, 2, :], 0.0, ALU.add, ALU.bypass))
                then(V.tensor_tensor(r8[:, 4, :], r8[:, 3, :], r8[:, 2, :], ALU.subtract))
                then(V.tensor_scalar(r8[:, 5, :], r8[:, 4, :], float(P), None, ALU.mult))
                then(V.tensor_tensor(rt[:, 5, :], rt[:, 6, :], rt[:, 5, :], ALU.subtract))
                then(V.tensor_tensor(te(7), te(7), et.rearrange("p e t -> p t e"), ALU.add))
                then(V.tensor_tensor(te(7), te(7), r8[:, 5, :].unsqueeze(1).to_broadcast([P, T, E]), ALU.add))
                for k in range(TOPK):
                    then(V.tensor_tensor(te(3 + k), te(3 + k), te(7), ALU.mult))
                    then(V.tensor_reduce(topf[:, k, :], te(3 + k), AX.X, ALU.add))
                V.tensor_scalar(slot_of[:], topf[:], float(TOK), None, ALU.add)
                dve.wait_ge(rows_low, 16 * T // 2)
                dve.wait_ge(rows_high, 16 * T // 2)
                V.tensor_copy(rows[:, :, WGT:WGT + 1], r1[:, 6, :].unsqueeze(2)).then_inc(route_ready, 1)
                then(V.tensor_tensor(owner_f, r8[0:1, 3, :].unsqueeze(1).to_broadcast([1, JT + 1, E]),
                                     iota_f[0:1, :].unsqueeze(2).to_broadcast([1, JT + 1, E]), ALU.is_le))
                then(V.tensor_reduce(owner_r[:], owner_f, AX.X, ALU.add))
                then(V.tensor_scalar(owner_r[:], owner_r[:], E - 1.0, None, ALU.min))
                V.tensor_scalar(tile_v[0:1, T:KT + 1], owner_r[:], 1.0, None, ALU.add)
                V.tensor_scalar(tile_at[0:1, T:KT + 1], owner_r[:], 2.0 * EW, None, ALU.mult).then_inc(owner_ready, 1)

            up_ps = ps[:, 2 * BANK:4 * BANK].rearrange("p (b n) -> p b n", b=2)[:, :, 0:HALF]

            def times_up(k, first=False):
                dve.wait_ge(u_done, k + 1)
                dve.wait_ge(silu_ready, k + 1)
                if not first:
                    dve.wait_ge(hn_ready, k)
                V.tensor_tensor(h.rearrange("p (b n) -> p b n", b=2), silu, up_ps, ALU.mult).then_inc(h_ready, 1)
                dve.wait_ge(h_ready, k + 1)
                V.tensor_reduce(h_inv[:, 0:1], h, AX.X, ALU.max, apply_absolute_value=True).then_inc(h_step, 1)
                dve.wait_ge(h_step, 3 * k + 1)
                V.tensor_scalar(h_inv[:, 1:2], h_inv[:, 0:1], TINY, 1.0 / TOP, ALU.max, ALU.mult).then_inc(h_step, 1)
                dve.wait_ge(h_step, 3 * k + 2)
                V.reciprocal(h_inv[:, 2:3], h_inv[:, 1:2]).then_inc(h_step, 1)
                one = bass.ds(k, 1)
                V.scalar_tensor_tensor(y_scale[:, one], h_inv[:, 1:2], gup_inv[:, one], out_wgt[:, one], ALU.mult,
                                       ALU.mult).then_inc(yscale_ready, 1)

            def take_meta(k, u, loaded, v):
                dve.wait_ge(*loaded)
                one = bass.ds(k, 1)
                V.tensor_tensor(gup_inv[:, one], xin[:, u, INV:INV + 1], winv[:, 0, bass.ds(v, 1)], ALU.mult)
                V.tensor_tensor(out_wgt[:, one], xin[:, u, WGT:WGT + 1], winv[:, 1, bass.ds(v, 1)], ALU.mult)
                V.tensor_copy(dst[:, one], xin[:, u, DST:DST + 1].bitcast(I32)).then_inc(meta_ready, 1)

            def low_h(k):
                dve.wait_ge(hT_high, k + 1)
                V.tensor_tensor(h_T[:, 1].rearrange("p c t -> p (c t)"), ps[:, 4 * BANK:6 * BANK],
                                h_T[:, 0].rearrange("p c t -> p (c t)"), ALU.subtract).then_inc(hT_low, 1)

            def scales_of(k):
                return dve.value_load(tile_v[0:1, bass.ds(k, 1)], min_val=0, max_val=E)

            take_meta(0, 0, (xin_ready[0], 16), 0)
            for k in range(PLANNED):
                times_up(k, k == 0)
                i = k + 1
                take_meta(i, i % RING, (xin_ready[i % RING], 16 * (i // RING + 1)), scales_of(i) if i >= T else 0)
                if k >= 1:
                    low_h(k - 1)
                if k == 0:
                    dve.wait_ge(logits_done, 1)
                    V.tensor_copy(rt[:, 7, :], bank(5, 0, P)).then_inc(logits_kept, 1)
                if k < 2:
                    make_rows(8 + 4 * k)
                if k == 2:
                    choose()
                if k == 3:
                    place()
                for e, step in BESIDE.get(k, ()):
                    weight_step(e, step)
            with dve.Fori(PLANNED // RING, KT // RING) as g:
                for u in range(RING):
                    k = g * RING + u
                    times_up(k)
                    i = g * RING + (u + 1)
                    v = (u + 1) % RING
                    take_meta(i, v, (xin_ready[v], (g + (1 if u < RING - 1 else 2)) * 16), scales_of(i))
                    low_h(g * RING + (u - 1))
            low_h(KT - 1)

        @block.tensor
        def _(pe):
            M = nc.tensor.matmul
            pe.wait_ge(condw_ready, BATCH * DC)
            n = 0
            for b in range(NB):
                pe.wait_ge(ld_x[b], 16)
                for o in range(DC):
                    n += 1
                    if n == 3:
                        pe.wait_ge(condw_ready, BATCH * DC + 2)
                        for oo in range(DC):
                            for c in range(DC):
                                ins = M(bank(7, oo * BATCH, BATCH), condw2[:, c, oo * P:(oo + 1) * P], ys2[:, c, :],
                                        start=(c == 0), stop=(c == DC - 1))
                        ins.then_inc(dsum_done, 1)
                    if n == 8:
                        pe.wait_ge(sqrt_done, 1)
                    for c in range(DC):
                        ins = M(bank(n - 1), condw_b[:, b * BLK // SEQ, c, o * P:(o + 1) * P],
                                x1[:, c, b * BLK:(b + 1) * BLK], start=(c == 0), stop=(c == DC - 1))
                    ins.then_inc(xs_mm, 1)
            pe.wait_ge(ident_ok, 1)
            pe.wait_ge(winq_ready, 1)
            for c in range(DC):
                for half in range(2):
                    pe.wait_ge(x0_ready, 2 * c + half + 1)
                    for q in range(4):
                        f = half * 4 + q
                        ins = nc.tensor.transpose(bank(2 * c + half, q * P, P), win_raw[:, f, c * P:(c + 1) * P],
                                                  ident[:])
                    ins.then_inc(wint_done, 1)
            pe.wait_ge(win_ready, 4)
            for g in range(NB * FC):
                b, f = divmod(g, FC)
                if f == 0:
                    pe.wait_ge(xq_ready, b + 1)
                if g < 4:
                    pe.wait_ge(x0_ready, 4 + g + 1)
                if g >= 8:
                    pe.wait_ge(gelu_done, g - 7)
                for c in range(DC):
                    for half in range(2):
                        ins = M(bank((g + 4) % 8), win_q[:, c, f * P:(f + 1) * P],
                                xq[:, half, c, b * BLK:(b + 1) * BLK], start=(c == 0 and half == 0),
                                stop=(c == DC - 1 and half == 1))
                ins.then_inc(mm1_done, 1)
            pe.wait_ge(woutq_ready, FC)
            pe.wait_ge(gelu_done, NB * FC)
            for b in range(NB):
                for f in range(FC):
                    pe.wait_ge(hq_ready, b * FC + f + 1)
                    for o in range(DC):
                        ins = M(bank(DC * b + o), wout_q[:, f, o * P:(o + 1) * P], hid[:, f, b * BLK:(b + 1) * BLK],
                                start=(f == 0), stop=(f == FC - 1))
                        if f == FC - 1:
                            ins.then_inc(mm2_done, 1)
            pe.wait_ge(ld_small, 16 * 3)
            for n in range(NB * DC):
                b, o = divmod(n, DC)
                a = 3 * (n % 2)
                pe.wait_ge(x1_ready, max(DC * (b + 1), a + 3))
                if n >= 2:
                    pe.wait_ge(gates_done, n - 1)
                for g in range(3):
                    for c in range(DC):
                        ins = M(bank(a + g), recw[:, g, c, o * P:(o + 1) * P], x1[:, c, b * BLK:(b + 1) * BLK],
                                start=(c == 0), stop=(c == DC - 1))
                ins.then_inc(rec_done, 1)
                if o:
                    pe.wait_ge(x1_ready, NB * DC)
                    for t in range(4 * b, 4 * b + 4):
                        if t >= 2:
                            pe.wait_ge(x1r_ready, t - 1)
                        for c in range(DC):
                            ins = nc.tensor.transpose(bank(6 + t % 2, c * P, P),
                                                      x1[:, c, t * P:(t + 1) * P], ident[:])
                        ins.then_inc(x1t_done, 1)

            def turn_rows(t0):
                for t in range(t0, t0 + 4):
                    if t >= 2:
                        pe.wait_ge(rows_raw, t - 1)
                    for c in range(DC):
                        ins = nc.tensor.transpose(bank(6 + t % 2, D + c * P, P), hT[:, c, t * P:(t + 1) * P],
                                                  ident[:])
                    ins.then_inc(rowt_done, 1)

            pe.wait_ge(x1r_ready, T)
            pe.wait_ge(hid_ready, DC)
            turn_rows(0)
            turn_rows(4)

            def turn_x(u, loaded):
                pe.wait_ge(*loaded)
                halves = xin[:, u, 0:D].bitcast(F16)
                to = bank(7, 0, D).bitcast(F16)
                for q in range(2 * DC):
                    ins = nc.tensor.transpose(to[:, q * P:(q + 1) * P], halves[:, q * P:(q + 1) * P], ident_h[:])
                ins.then_inc(xT_raw, 1)

            def product(which, at):
                for c in range(DC):
                    a = 2 * PAIR * (2 * c + which)
                    for part, low in ((0, 0), (0, 1), (1, 0)):
                        for b in range(2):
                            ins = M(bank(2 * which + b, 0, HALF), xT[:, part, c, :],
                                    Wh[:, bass.ds(at + (a + low * I + b * HALF), HALF)],
                                    start=(c == 0 and part == 0 and low == 0), stop=(c == DC - 1 and part == 1))
                return ins

            def gate_up(k, at, first=False):
                pe.wait_ge(xT_ready, k + 1)
                if not first:
                    pe.wait_ge(silu_ready, k)
                product(0, at).then_inc(g_done, 1)
                if not first:
                    pe.wait_ge(h_ready, k)
                product(1, at).then_inc(u_done, 1)

            def down(i, at, first=False):
                pe.wait_ge(hT_low, i + 1)
                if not first:
                    pe.wait_ge(y_ready, i)
                for c in range(IC):
                    a = 2 * (c // 2 * PAIR + I) + c % 2 * D
                    for part, low in ((0, 0), (0, 1), (1, 0)):
                        ins = M(bank(6, 0, D), h_T[:, part, c, :], Wh[:, bass.ds(at + (a + low * DU), D)],
                                start=(c == 0 and part == 0 and low == 0), stop=(c == IC - 1 and part == 1))
                ins.then_inc(d_done, 1)

            def turn_h(i, first=False):
                pe.wait_ge(hn_ready, i + 1)
                if not first:
                    pe.wait_ge(hT_low, i)
                for c in range(IC):
                    ins = nc.tensor.transpose(bank(4, c * P, P), hn[:, c * P:(c + 1) * P], ident[:])
                ins.then_inc(t_done, 1)

            def weights_of(k):
                v = pe.value_load(tile_v[0:1, bass.ds(k, 1)], min_val=0, max_val=E)
                pe.wait_ge(split_done, v + 1)
                return place_of(k)

            def place_of(k):
                return pe.value_load(tile_at[0:1, bass.ds(k, 1)], min_val=0, max_val=2 * SHARED_SLOT * EW)

            shared = 2 * SHARED_SLOT * EW
            pe.wait_ge(consts, 11)
            pe.wait_ge(split_done, 1)
            pe.wait_ge(gates_done, NB * DC)
            pe.wait_ge(rows_raw, 8)
            turn_x(0, (xin_ready[0], 16))
            for k in range(FIRST):
                gate_up(k, shared, k == 0)
                if k in (1, 2):
                    pe.wait_ge(rows_raw, 8 + 4 * k)
                if k == 4:
                    pe.wait_ge(ranks_kept, 1)
                if k >= 2:
                    down(k - 2, shared, k == 2)
                i = k + 1
                turn_x(i % RING, (xin_ready[i % RING], 16 * (i // RING + 1)))
                if k >= 1:
                    turn_h(k - 1, k == 1)
                if k == 0:
                    pe.wait_ge(hid_ready, BATCH * DC)
                    for t in range(T):
                        for c in range(DC):
                            ins = M(bank(5, t * E, E), hT[:, c, t * P:(t + 1) * P], gatew[:, c, :],
                                    start=(c == 0), stop=(c == DC - 1))
                    ins.then_inc(logits_done, 1)
                    pe.wait_ge(logits_kept, 1)
                if k < 2:
                    pe.wait_ge(xT_ready, k + 2)
                    turn_rows(8 + 4 * k)
                if k == 3:
                    pe.wait_ge(xT_ready, k + 2)
                    pe.wait_ge(chosen_ready, 1)
                    flat = chosen[:].rearrange("p t e -> p (t e)")
                    M(bank(7, D, P), before[:], flat, start=True, stop=True)
                    M(bank(7, D + P, P), ones[:], flat, start=True, stop=True).then_inc(rank_done, 1)
            pe.wait_ge(owner_ready, 1)
            with pe.Fori(FIRST // RING, KT // RING) as g:
                for u in range(RING):
                    k = g * RING + u
                    gate_up(k, weights_of(k))
                    down(g * RING + (u - 2), place_of(g * RING + (u - 2)))
                    v = (u + 1) % RING
                    turn_x(v, (xin_ready[v], (g + (1 if u < RING - 1 else 2)) * 16))
                    turn_h(g * RING + (u - 1))
            down(KT - 2, place_of(KT - 2))
            turn_h(KT - 1)
            down(KT - 1, place_of(KT - 1))


def kernel(**inputs):
    import numpy as np
    import concourse.bacc as bacc
    from concourse.bass_utils import run_bass_kernel_spmd as run

    def part(a, c):
        return np.ascontiguousarray(a.reshape(c, P, -1).transpose(1, 0, 2))

    n = {k: np.asarray(v) for k, v in inputs.items()}

    def expert(gate_up, down):
        gu = part(gate_up.T, DC).reshape(P, PAIRS, I)
        dn = part(np.pad(down.T, ((0, IC * P - I), (0, 0))), IC).reshape(P, PAIRS, DU)
        return np.concatenate([gu, dn], 2).reshape(P, EW)

    all_experts = [expert(n["L1_ffn_experts_gate_up"][e], n["L1_ffn_experts_down"][e]) for e in range(E)]
    all_experts.append(expert(n["L1_ffn_shared_gate_up"], n["L1_ffn_shared_down"]))
    bias = [part(n["L0_ffn_b_in"][:, None], FC)[:, :, 0], part(n["L0_ffn_b_out"][:, None], DC)[:, :, 0]]
    bias += [part(n[f"L1_cond_b_{g}"][:, None], DC)[:, :, 0] for g in "fih"]
    arrays = {
        "x_t": part(n["x"].reshape(TOK, D).T, DC),
        "cond_t": part(n["cond_1024"].T, DC),
        "cond_w": part(n["L0_cond_weight"], DC),
        "w_in_t": part(n["L0_ffn_W_in"].T, FC),
        "w_out": part(n["L0_ffn_W_out"], FC),
        "bias": np.concatenate(bias, 1),
        "rec_w": np.ascontiguousarray(np.stack([part(n[f"L1_cond_W_{g}"].T, DC) for g in "fih"], 1)),
        "gate_w": part(n["L1_ffn_gate_weight"].T, DC),
        "experts": np.stack(all_experts),
    }
    nc = bacc.Bacc("TRN2", target_bir_lowering=False, num_devices=1, dynamic_dma_scratch_size=4096)
    args = [nc.dram_tensor(f"in_{k}", a.shape, F32, kind="ExternalInput").ap() for k, a in arrays.items()]
    out = nc.dram_tensor("out_rows", (OUTR, D), F32, kind="ExternalOutput").ap()
    adaln_ffn_moe(nc, *args, out)
    r = run(nc, [{f"in_{k}": a for k, a in arrays.items()}], core_ids=[0])
    return r.results[0]["out_rows"][:TOK].reshape(BATCH, SEQ, D)
```

```python
import concourse.bass as bass
from concourse import mybir
from contextlib import ExitStack

F32 = mybir.dt.float32
F16 = mybir.dt.float16
BF16 = mybir.dt.bfloat16
I32 = mybir.dt.int32
U32 = mybir.dt.uint32
ALU = mybir.AluOpType
ACT = mybir.ActivationFunctionType
AX = mybir.AxisListType
ABSMAX = bass.bass_isa.ReduceOp.absmax

P = 128
BATCH, SEQ, D = 2, 1024, 256
TOK = BATCH * SEQ
DC = D // P
FF = 1024
FC = FF // P
E = 8
TOPK = 2
I = 938
IC = -(-I // P)
HALF = I // 2
PAIRS = 2 * DC
DU = IC * D // PAIRS
PAIR = I + DU
SHIFT = PAIR
EW = PAIRS * PAIR
BANK = 512
BLK = 512
NB = TOK // BLK
T = TOK // P
JT = TOPK * TOK // P + E
KT = T + JT
RING = 5
STEP0 = 1
ROUTED = (T - 1) // RING
LAST = (KT - 1) // RING
SPLIT_TO = E
assert 1 + ROUTED * RING == T and 1 + LAST * RING == KT
LOADS = ROUTED + 2
ROW = D + 4
INV, WGT, DST = D, D + 1, D + 2
SLOTS = (KT + 1) * P
OUTR = TOK + P
SHARED_SLOT = E - 1

ROUND = 1.5 * 2.0 ** 23
ROUND256 = ROUND * 256
EPS = 1e-8
TINY = 1e-30
TOP = 2.0 ** 14

STEPS = 4
BESIDE = {4 + n: divmod(n, STEPS) for n in range(ROUTED * STEPS)}
SENDS = {k: range(4 * (k - 4), 4 * (k - 3)) for k in range(4, 12)}


def adaln_ffn_moe(nc, x_t, cond_t, cond_w, w_in_t, w_out, bias, rec_w, gate_w, experts, out):
    moved = nc.dram_tensor("moved_rows", (SLOTS, ROW), F32, kind="Internal").ap()
    ctx = ExitStack()
    with ctx:
        def sb(name, shape, dt=F32):
            return ctx.enter_context(nc.sbuf_tensor(name, shape, dt))

        def sem(name):
            return ctx.enter_context(nc.semaphore(name))

        W = sb("weight_slots", [P, SHIFT + E * EW])
        Wh = W[:].bitcast(F16)

        def chunks(ap, c):
            return ap.rearrange("p (c n) -> p c n", c=c)

        def raw(e):
            return e * EW + SHIFT

        NX = DC * TOK
        x0 = chunks(W[:, 0:NX], DC)
        condw = chunks(W[:, NX:NX + DC * D], DC)
        condw_b = W[:, NX + DC * D:NX + 3 * DC * D].rearrange("p (b c n) -> p b c n", b=BATCH, c=DC)
        condw2 = chunks(W[:, NX + 3 * DC * D:NX + 4 * DC * D], DC)
        at = raw(1)
        win_raw = chunks(W[:, at:at + FC * D], FC)
        wout_q = win_raw
        at += FC * D
        win_q = W[:, at:at + DC * FF // 2].bitcast(BF16).rearrange("p (c f) -> p c f", c=DC)
        at += DC * FF // 2
        wout = chunks(W[:, at:at + FC * D], FC)
        at = raw(2)
        hid = chunks(W[:, at:at + FC * TOK], FC)
        fgate = chunks(W[:, at:at + NX], DC)
        igate = chunks(W[:, at + NX:at + 2 * NX], DC)
        cand = chunks(W[:, at + 2 * NX:at + 3 * NX], DC)
        at += 3 * NX
        rows = chunks(W[:, at:at + T * ROW], T)

        def gsum(b, c):
            g = at + b * BLK // SEQ * (T // BATCH * ROW) + (b % (SEQ // BLK) * DC + c) * BLK
            return W[:, g:g + BLK]

        x1 = chunks(W[:, raw(5):raw(5) + NX], DC)
        a5 = raw(5) + NX
        recw = W[:, a5:a5 + 3 * DC * D].rearrange("p (g c h) -> p g c h", g=3, c=DC)
        rt = chunks(W[:, a5:a5 + 8 * P], 8)
        top = W[:, a5 + 8 * P:a5 + 9 * P].rearrange("p (t n) -> p t n", t=T)
        topi = W[:, a5 + 9 * P:a5 + 10 * P].bitcast(U32).rearrange("p (t n) -> p t n", t=T)
        owner_f = W[0:1, a5:a5 + (JT + 1) * E].rearrange("p (j e) -> p j e", e=E)
        a6 = SHARED_SLOT * EW - NX - ROW
        assert a6 >= a5 + 3 * DC * D
        xq = W[:, a6:a6 + NX].bitcast(BF16).rearrange("p (h c t) -> p h c t", h=2, c=DC)
        hT = chunks(W[:, a6:a6 + NX], DC)
        blank = W[:, a6 + NX:a6 + NX + ROW]

        cond = sb("cond", [P, DC, BATCH])
        ys = sb("ys", [P, DC, BATCH])
        ys2 = sb("ys2", [P, DC, BATCH])
        dinv = sb("dinv", [P, DC, BATCH])
        bia = sb("bia", [P, 16])
        b_in, b_out = bia[:, 0:FC], bia[:, FC:FC + DC]
        b_rec = bia[:, FC + DC:FC + 4 * DC].rearrange("p (g c) -> p g c", g=3)
        eps = sb("eps", [P, 1])
        big = sb("big", [P, 1])
        ident = sb("ident", [P, P])
        ident_h = sb("ident_h", [P, P], F16)
        before = sb("before", [P, P], BF16)
        ones = sb("ones", [P, P], BF16)
        notfirst = sb("notfirst", [P, E, T])
        wstat = sb("wstat", [P, 8, FC])
        amax = sb("amax", [P, 44])
        sc = sb("sc", [P, 8])
        gsc = sb("gsc", [P, FC])
        gatew = sb("gatew", [P, DC, E])
        rstat = sb("rstat", [P, 3, 4])
        r1 = sb("r1", [P, 8, T])
        topf = sb("topf", [P, TOPK, T])
        chosen = sb("chosen", [P, T, E], BF16)
        iota_i = sb("iota_i", [P, JT + 1], I32)
        iota_f = sb("iota_f", [P, JT + 1])
        rowid = sb("rowid", [P, T], I32)
        r8 = sb("r8", [P, 6, E])
        slot_of = sb("slot_of", [P, TOPK, T], U32)
        owner_r = sb("owner_r", [1, JT + 1])
        tile_v = sb("tile_v", [1, KT + 1], I32)
        tile_at = sb("tile_at", [1, KT + 1], I32)
        part_max = sb("part_max", [P, 2, 2])
        own_max = sb("own_max", [P, 2])
        all_max = sb("all_max", [P, 2])
        winv_now = sb("winv_now", [P, 2])
        wscale = sb("wscale", [P, 2])
        winv = sb("winv", [P, 2, E + 1])
        xin = sb("xin", [P, RING, ROW])
        gup_inv = sb("gup_inv", [P, KT + 1])
        out_wgt = sb("out_wgt", [P, KT + 1])
        y_scale = sb("y_scale", [P, KT])
        dst = sb("dst", [P, KT + 1], I32)
        xT = sb("xT", [P, 2, DC, P], F16)
        work = sb("work", [P, 2 * I])
        silu = work[:, 0:I].rearrange("p (b n) -> p b n", b=2)
        h = work[:, I:2 * I]
        x0_hi = chunks(work[:, 0:DC * BLK], DC)
        x1r = chunks(work[:, 0:4 * D], 4)
        h_inv = sb("h_inv", [P, 3])
        hn = sb("hn", [P, IC * P])
        h_T = sb("h_T", [P, 2, IC, P], F16)
        yb = sb("yb", [P, RING, D])
        idx = sb("idx", [P, RING], U32)

        ps = ctx.enter_context(nc.psum_tensor("ps", [P, 8 * BANK], F32))

        def bank(b, a=0, n=BANK):
            return ps[:, b * BANK + a:b * BANK + a + n]

        def unit_views(slot, p, unit):
            a = slot * EW + (p * PAIR + unit * I)
            n = (I, DU)[unit]
            return W[:, bass.ds(a + SHIFT, n)], Wh[:, bass.ds(a * 2, n)], Wh[:, bass.ds(a * 2 + n, n)]

        ld_cond = sem("ld_cond")
        ld_small = sem("ld_small")
        ld_win = sem("ld_win")
        ld_wout = sem("ld_wout")
        ld_shared = sem("ld_shared")
        consts = sem("consts")
        ident_ok = sem("ident_ok")
        blank_ok = sem("blank_ok")
        blank_out = sem("blank_out")
        dve_step = sem("dve_step")
        pool_step = sem("pool_step")
        condw_ready = sem("condw_ready")
        dsum_done = sem("dsum_done")
        sqrt_done = sem("sqrt_done")
        dinv_ready = sem("dinv_ready")
        xs_mm = sem("xs_mm")
        x0_ready = sem("x0_ready")
        xmax_part = sem("xmax_part")
        xmax_all = sem("xmax_all")
        winq_ready = sem("winq_ready")
        wint_done = sem("wint_done")
        win_ready = sem("win_ready")
        wstat_ready = sem("wstat_ready")
        wq_step = sem("wq_step")
        gsc_ready = sem("gsc_ready")
        xround = sem("xround")
        xq_ready = sem("xq_ready")
        mm1_done = sem("mm1_done")
        gelu_done = sem("gelu_done")
        hmax_part = sem("hmax_part")
        hmax_all = sem("hmax_all")
        hsc_ready = sem("hsc_ready")
        hround = sem("hround")
        hq_ready = sem("hq_ready")
        woutq_ready = sem("woutq_ready")
        xb_ready = sem("xb_ready")
        mm2_done = sem("mm2_done")
        x1_ready = sem("x1_ready")
        rec_done = sem("rec_done")
        gates_done = sem("gates_done")
        inv_ready = sem("inv_ready")
        rec_step = sem("rec_step")
        info_ready = sem("info_ready")
        decay_ready = sem("decay_ready")
        hid_ready = sem("hid_ready")
        x1t_done = sem("x1t_done")
        x1r_ready = sem("x1r_ready")
        rowt_done = sem("rowt_done")
        rows_raw = sem("rows_raw")
        rows_ready = sem("rows_ready")
        rows_low = sem("rows_low")
        rows_high = sem("rows_high")
        logits_done = sem("logits_done")
        logits_kept = sem("logits_kept")
        shifted = sem("shifted")
        exp_done = sem("exp_done")
        chosen_ready = sem("chosen_ready")
        rank_done = sem("rank_done")
        ranks_kept = sem("ranks_kept")
        route_ready = sem("route_ready")
        weight_set = sem("weight_set")
        sent = sem("sent")
        owner_ready = sem("owner_ready")
        max_step = sem("max_step")
        wmax_part = sem("wmax_part")
        max_turn = sem("max_turn")
        winv_ready = sem("winv_ready")
        wmax_all = sem("wmax_all")
        wscale_ready = sem("wscale_ready")
        high_done = sem("high_done")
        low_done = sem("low_done")
        split_done = sem("split_done")
        xT_raw = sem("xT_raw")
        xT_ready = sem("xT_ready")
        meta_ready = sem("meta_ready")
        g_done = sem("g_done")
        u_done = sem("u_done")
        silu_ready = sem("silu_ready")
        h_ready = sem("h_ready")
        h_step = sem("h_step")
        yscale_ready = sem("yscale_ready")
        hn_ready = sem("hn_ready")
        t_done = sem("t_done")
        hT_high = sem("hT_high")
        hT_low = sem("hT_low")
        d_done = sem("d_done")
        y_ready = sem("y_ready")
        idx_ready = sem("idx_ready")
        add_turn = sem("add_turn")
        added = sem("added")
        ld_x = [sem(f"ld_x{b}") for b in range(NB)]
        stored = [sem(f"stored{u}") for u in range(4)]
        xin_ready = [sem(f"xin_ready{u}") for u in range(RING)]
        ld_exp = [sem(f"ld_exp{e}") for e in range(ROUTED)]
        ld_late = sem("ld_late")

        block = ctx.enter_context(nc.Block())

        @block.sync
        def _(sp):
            sp.dma_start(cond[:], cond_t).then_inc(ld_cond, 16)
            sp.dma_start(condw, cond_w).then_inc(ld_cond, 16)
            for b in range(NB):
                t = slice(b * BLK, (b + 1) * BLK)
                sp.dma_start(x1[:, :, t], x_t[:, :, t]).then_inc(ld_x[b], 16)
            sp.dma_start(win_raw, w_in_t).then_inc(ld_win, 16)
            sp.dma_start(bia[:], bias).then_inc(ld_small, 16)
            sp.dma_start(wout, w_out).then_inc(ld_wout, 16)
            sp.dma_start(recw, rec_w).then_inc(ld_small, 16)
            sp.dma_start(gatew[:], gate_w).then_inc(ld_small, 16)
            sp.dma_start(W[:, raw(SHARED_SLOT):raw(SHARED_SLOT) + EW], experts[E]).then_inc(ld_shared, 16)
            sp.wait_ge(blank_ok, 1)
            sp.dma_start(moved[TOK:SLOTS, :].rearrange("(j p) n -> p j n", p=P),
                         blank.unsqueeze(1).to_broadcast([P, JT + 1, ROW])).then_inc(blank_out, 16)

            def load_expert(e):
                sp.dma_start(W[:, raw(e):raw(e) + EW], experts[e]).then_inc(ld_exp[e], 16)

            sp.wait_ge(xq_ready, NB)
            sp.wait_ge(xs_mm, NB * DC)
            load_expert(0)
            sp.wait_ge(mm2_done, NB * DC)
            load_expert(1)
            for t in range(T):
                sp.wait_ge(x1r_ready, t + 1)
                sp.dma_start(out[t * P:(t + 1) * P, :], x1r[:, t % 4, :]).then_inc(stored[t % 4], 16)

            def store_rows(t0, n):
                for t in range(t0, t0 + n):
                    sp.wait_ge(rows_ready, t + 1)
                    sp.dma_start(moved[t * P:(t + 1) * P, :], rows[:, t, :]).then_inc(
                        rows_low if t < T // 2 else rows_high, 16)

            def load_x(i, u):
                sp.dma_start(xin[:, u, :], moved[bass.ds(i * P, P), :]).then_inc(xin_ready[u], 16)

            store_rows(0, T // 2)
            sp.wait_ge(rows_low, 16 * T // 2)
            for i in range(RING):
                load_x(i, i)
            sp.wait_ge(hid_ready, BATCH * DC)
            load_expert(2)

            def load_late(n, e):
                if n:
                    sp.wait_ge(ld_late, 16 * n)
                sp.dma_start(W[:, raw(e):raw(e) + EW], experts[e]).then_inc(ld_late, 16)

            load_late(0, 3)
            for i in range(RING, 1 + RING * LOADS):
                if i == 6:
                    store_rows(T // 2, 4)
                if i == 7:
                    store_rows(T // 2 + 4, 4)
                if i == T // 2:
                    sp.wait_ge(rows_high, 16 * T // 2)
                sp.wait_ge(xT_ready, i - RING + 1)
                sp.wait_ge(meta_ready, i - RING + 1)
                if i == T:
                    sp.wait_ge(sent, 16 * TOPK * T)
                    sp.wait_ge(blank_out, 16)
                    load_late(1, 4)
                load_x(i, i % RING)
                if i == 19:
                    sp.wait_ge(owner_ready, 1)
                    sp.wait_ge(rowt_done, T)
                    load_late(2, 5)
                if i == 22:
                    sp.wait_ge(d_done, T)
                    sp.wait_ge(rowt_done, T)
                    load_late(3, 6)
                if i == 25:
                    load_late(4, 7)
            with sp.Fori(LOADS, LAST) as q:
                for u in range(RING):
                    sp.wait_ge(xT_ready, q * RING + (u + 2 - RING))
                    sp.wait_ge(meta_ready, q * RING + (u + 2 - RING))
                    load_x(q * RING + (u + 1), (u + 1) % RING)
            sp.wait_ge(xT_ready, KT - RING + 1)
            sp.wait_ge(meta_ready, KT - RING + 1)
            load_x(KT, KT % RING)
            sp.wait_ge(xin_ready[KT % RING], 16 * (KT // RING + 1))
            sp.wait_ge(added, 16 * (KT + 2))

        @block.gpsimd
        def _(pool):
            G = nc.gpsimd
            G.memset(ident[:], 0.0).then_inc(pool_step, 1)
            G.memset(before[:], 1.0).then_inc(pool_step, 1)
            G.memset(notfirst[:], 1.0).then_inc(pool_step, 1)
            G.memset(blank, 0.0).then_inc(pool_step, 1)
            G.iota(iota_i[:], [[1, JT + 1]], base=0, channel_multiplier=0).then_inc(pool_step, 1)
            G.memset(eps[:], EPS).then_inc(consts, 1)
            G.memset(big[:], ROUND).then_inc(consts, 1)
            G.memset(ones[:], 1.0).then_inc(consts, 1)
            G.iota(rowid[:], [[P, T]], base=0, channel_multiplier=1).then_inc(consts, 1)
            G.memset(hn[:, I:IC * P], 0.0).then_inc(consts, 1)
            G.memset(tile_v[0:1, 0:T], 0).then_inc(consts, 1)
            G.memset(tile_at[0:1, 0:T], 2 * SHARED_SLOT * EW).then_inc(consts, 1)
            pool.wait_ge(pool_step, 5)
            G.affine_select(out=ident[:], in_=ident[:], compare_op=ALU.not_equal, fill=1.0, base=0,
                            pattern=[[-1, P]], channel_multiplier=1).then_inc(ident_ok, 1)
            G.affine_select(out=before[:], in_=before[:], compare_op=ALU.is_gt, fill=0.0, base=0,
                            pattern=[[1, P]], channel_multiplier=-1).then_inc(consts, 1)
            G.memset(notfirst[:, :, 0:1], 0.0).then_inc(consts, 1)
            G.iota(blank[:, DST:DST + 1].bitcast(I32), [[0, 1]], base=TOK, channel_multiplier=1)\
                .then_inc(blank_ok, 1)
            G.tensor_copy(iota_f[:], iota_i[:]).then_inc(consts, 1)
            pool.wait_ge(ident_ok, 1)
            G.tensor_copy(ident_h[:], ident[:]).then_inc(consts, 1)
            pool.wait_ge(blank_ok, 1)
            for q in range(2):
                G.dma_start(out[TOK + q * 64:TOK + q * 64 + 64, :], blank[q * 64:q * 64 + 64, 0:D])\
                    .then_inc(added, 16)
            pool.wait_ge(xmax_part, 1)
            G.partition_all_reduce(amax[:, 9:10], amax[:, 8:9], P, ABSMAX).then_inc(xmax_all, 1)
            pool.wait_ge(ld_small, 16 * 3)
            pool.wait_ge(xs_mm, NB * DC)
            for c in range(DC):
                G.tensor_scalar(x1[:, c, :], x1[:, c, :], b_out[:, c:c + 1], 1.0, ALU.add, ALU.mult)\
                    .then_inc(xb_ready, 1)
            pool.wait_ge(wstat_ready, 1)
            pool.wait_ge(wint_done, 2 * DC)
            for f in range(FC):
                G.tensor_scalar(wout[:, f, :], wout[:, f, :], wstat[:, 6, f:f + 1], ROUND, ALU.mult, ALU.add)\
                    .then_inc(wq_step, 1)
            pool.wait_ge(wq_step, FC)
            G.tensor_scalar(wout, wout, ROUND + 127.0, ROUND - 128.0, ALU.min, ALU.max).then_inc(wq_step, 1)
            pool.wait_ge(wq_step, FC + 1)
            for f in range(FC):
                G.tensor_scalar(wout_q[:, f, :], wout[:, f, :], -ROUND, wstat[:, 7, f:f + 1], ALU.add, ALU.mult)\
                    .then_inc(woutq_ready, 1)
            pool.wait_ge(hmax_part, 1)
            G.partition_all_reduce(amax[:, 43:44], amax[:, 42:43], P, ABSMAX).then_inc(hmax_all, 1)

            def full_max(v):
                pool.wait_ge(wmax_part, v + 1)
                pool.sem_inc(max_turn, 1)
                G.partition_all_reduce(all_max[:], own_max[:], P, ABSMAX).then_inc(wmax_all, 1)

            full_max(0)
            pool.wait_ge(wscale_ready, 1)
            for n in range(2 * PAIRS):
                p, unit = divmod(n, 2)
                src, hi, _ = unit_views(SHARED_SLOT, p, unit)
                pool.wait_ge(low_done, n + 1)
                G.tensor_scalar(hi, src, wscale[:, unit:unit + 1], 0.0, ALU.mult, ALU.add).then_inc(high_done, 1)
            n = 0
            for b in range(NB):
                for c in range(DC):
                    n += 1
                    t = slice(b * BLK, (b + 1) * BLK)
                    pool.wait_ge(inv_ready, n)
                    G.tensor_tensor(fgate[:, c, t], fgate[:, c, t], gsum(b, c), ALU.mult).then_inc(rec_step, 1)
                    G.tensor_tensor(igate[:, c, t], igate[:, c, t], gsum(b, c), ALU.mult).then_inc(rec_step, 1)
                    pool.wait_ge(rec_step, 2 * n - 1)
                    G.tensor_scalar(fgate[:, c, t], fgate[:, c, t], EPS, 1.0, ALU.add, ALU.mult)\
                        .then_inc(decay_ready, 1)
                    pool.wait_ge(rec_step, 2 * n)
                    G.tensor_tensor(igate[:, c, t], igate[:, c, t], cand[:, c, t], ALU.mult).then_inc(info_ready, 1)

            def add(i, u):
                G.tensor_copy(idx[:, u:u + 1].bitcast(I32), dst[:, bass.ds(i, 1)]).then_inc(idx_ready, 1)
                pool.wait_ge(y_ready, i + 1)
                pool.wait_ge(added, (i + 2) * 16)
                pool.wait_ge(idx_ready, i + 1)
                pool.sem_inc(add_turn, 1)
                G.indirect_dma_start(out, bass.IndirectOffsetOnAxis(ap=idx[:, u:u + 1], axis=0), yb[:, u, :],
                                     None, compute_op=ALU.add).then_inc(added, 16)

            for k in range(T):
                if k == 2:
                    for u in range(4):
                        pool.wait_ge(stored[u], 16 * T // 4)
                if k >= 2:
                    pool.wait_ge(meta_ready, k - 1)
                    add(k - 2, (k - 2) % RING)
                e, step = BESIDE.get(k, (0, 0))
                if step == 1:
                    full_max(e + 1)
                if k == 4:
                    pool.wait_ge(route_ready, 1)
                    pool.wait_ge(blank_out, 16)
                for n in SENDS.get(k, ()):
                    choice, t = divmod(n, T)
                    if n == T:
                        pool.wait_ge(sent, 16 * T)
                        G.tensor_copy(rows[:, :, WGT:WGT + 1], r1[:, 5, :].unsqueeze(2)).then_inc(weight_set, 1)
                        pool.wait_ge(weight_set, 1)
                    G.indirect_dma_start(moved, bass.IndirectOffsetOnAxis(ap=slot_of[:, choice, t:t + 1], axis=0),
                                         rows[:, t, :], None).then_inc(sent, 16)
            for steps, splits in (((ROUTED, SPLIT_TO), True), ((SPLIT_TO, LAST), False)):
                with pool.Fori(*steps) as q:
                    for u in range(RING):
                        add(q * RING + (u - 1), (u - 1) % RING)
                        if splits and u == 1:
                            full_max(q + 1)
            for i in range(KT - 2, KT):
                add(i, i % RING)

        @block.scalar
        def _(act):
            A = nc.scalar.activation
            act.wait_ge(consts, 2)
            act.wait_ge(dsum_done, 1)
            A(dinv[:].rearrange("p c b -> p (c b)"), bank(7, 0, DC * BATCH), ACT.Sqrt, bias=eps[:, 0:1])\
                .then_inc(sqrt_done, 1)
            act.wait_ge(dinv_ready, 1)
            n = 0
            for b in range(NB):
                for c in range(DC):
                    n += 1
                    act.wait_ge(xs_mm, n)
                    bb = b * BLK // SEQ
                    A(x0[:, c, b * BLK:(b + 1) * BLK], bank(n - 1), ACT.Copy, scale=dinv[:, c, bb:bb + 1])\
                        .then_inc(x0_ready, 1)
            for c in range(DC):
                for half in range(2):
                    act.wait_ge(wint_done, 2 * c + half + 1)
                    A(win_q[:, c, half * BANK:(half + 1) * BANK], bank(2 * c + half), ACT.Copy).then_inc(win_ready, 1)
            act.wait_ge(gsc_ready, 1)
            for b in range(NB):
                t = slice(b * BLK, (b + 1) * BLK)
                A(x0[:, :, t], x0[:, :, t], ACT.Identity, bias=big[:, 0:1], scale=sc[:, 2:3]).then_inc(xround, 1)
            for g in range(NB * FC):
                b, f = divmod(g, FC)
                act.wait_ge(mm1_done, g + 1)
                A(hid[:, f, b * BLK:(b + 1) * BLK], bank((g + 4) % 8), ACT.Gelu, bias=b_in[:, f:f + 1],
                  scale=gsc[:, f:f + 1]).then_inc(gelu_done, 1)
            act.wait_ge(hsc_ready, 1)
            for b in range(NB):
                for f in range(FC):
                    piece = hid[:, f, b * BLK:(b + 1) * BLK]
                    A(piece, piece, ACT.Identity, bias=big[:, 0:1], scale=sc[:, 4:5]).then_inc(hround, 1)

            def gates(n):
                b, c = divmod(n, DC)
                t = slice(b * BLK, (b + 1) * BLK)
                act.wait_ge(rec_done, n + 1)
                a = 3 * (n % 2)
                A(fgate[:, c, t], bank(a), ACT.Sigmoid, bias=b_rec[:, 0, c:c + 1])
                A(igate[:, c, t], bank(a + 1), ACT.Sigmoid, bias=b_rec[:, 1, c:c + 1])
                A(cand[:, c, t], bank(a + 2), ACT.Identity, bias=b_rec[:, 2, c:c + 1]).then_inc(gates_done, 1)

            for b in range(NB):
                gates(DC * b)
                gates(DC * b + 1)
                for t in range(4 * b, 4 * b + 4):
                    act.wait_ge(x1t_done, t + 1)
                    if t >= 4:
                        act.wait_ge(stored[t % 4], 16 * (t // 4))
                    A(x1r[:, t % 4, :], bank(6 + t % 2, 0, D), ACT.Copy).then_inc(x1r_ready, 1)

            def drain_rows(t0):
                for t in range(t0, t0 + 4):
                    act.wait_ge(rowt_done, t + 1)
                    if t >= 4:
                        act.wait_ge(rows_ready, t - 3)
                    A(yb[:, t % 4, :], bank(6 + t % 2, D, D), ACT.Copy).then_inc(rows_raw, 1)

            drain_rows(0)
            drain_rows(4)

            gate_ps = ps[:, 0:2 * BANK].rearrange("p (b n) -> p b n", b=2)[:, :, 0:HALF]

            def silu_of(k, first=False):
                act.wait_ge(g_done, k + 1)
                act.wait_ge(meta_ready, k + 1)
                if not first:
                    act.wait_ge(h_ready, k)
                A(silu, gate_ps, ACT.Silu, scale=gup_inv[:, bass.ds(k, 1)]).then_inc(silu_ready, 1)

            def drain_y(i, u):
                act.wait_ge(d_done, i + 1)
                act.wait_ge(yscale_ready, i + 1)
                A(yb[:, u, :], bank(6, 0, D), ACT.Copy, scale=y_scale[:, bass.ds(i, 1)]).then_inc(y_ready, 1)

            def drain_x(k):
                act.wait_ge(xT_raw, k + 1)
                A(xT[:].rearrange("p s c t -> p (s c t)"), bank(7, 0, D).bitcast(F16), ACT.Copy).then_inc(xT_ready, 1)

            def high_h(k):
                act.wait_ge(t_done, k + 1)
                A(h_T[:, 0].rearrange("p c t -> p (c t)"), ps[:, 4 * BANK:6 * BANK], ACT.Copy).then_inc(hT_high, 1)

            def norm_h(k):
                act.wait_ge(h_step, k * 3 + 3)
                A(hn[:, 0:I], h, ACT.Copy, scale=h_inv[:, 2:3]).then_inc(hn_ready, 1)

            def high_halves(e, step):
                v = e + 1
                act.wait_ge(wscale_ready, v + 1)
                for p in range(2 * step - 4, 2 * step - 2):
                    for unit in range(2):
                        src, hi, _ = unit_views(e, p, unit)
                        act.wait_ge(low_done, v * (2 * PAIRS) + (2 * p + unit + 1))
                        A(hi, src, ACT.Copy, scale=wscale[:, unit:unit + 1]).then_inc(high_done, 1)

            drain_x(0)
            for u in range(4):
                act.wait_ge(stored[u], 16 * T // 4)
            for k in range(T):
                silu_of(k, k == 0)
                if k >= 2:
                    if k == 2:
                        act.wait_ge(rows_ready, T)
                    if k >= 2 + RING:
                        act.wait_ge(added, (k + 1 - RING) * 16 + 16)
                    drain_y(k - 2, (k - 2) % RING)
                drain_x(k + 1)
                if k >= 1:
                    high_h(k - 1)
                if k == 0:
                    act.wait_ge(consts, 11)
                norm_h(k)
                if k < 2:
                    drain_rows(8 + 4 * k)
                if k == 2:
                    act.wait_ge(shifted, 1)
                    A(rt[:, 1, :], rt[:, 0, :], ACT.Exp).then_inc(exp_done, 1)
                e, step = BESIDE.get(k, (0, 0))
                if step >= 2:
                    high_halves(e, step)
            for steps, splits in (((ROUTED, SPLIT_TO), True), ((SPLIT_TO, LAST), False)):
                with act.Fori(*steps) as q:
                    for u in range(RING):
                        k = q * RING + (u + 1)
                        silu_of(k)
                        act.wait_ge(added, (q * RING + (u + 3 - RING)) * 16)
                        drain_y(q * RING + (u - 1), (u - 1) % RING)
                        drain_x(q * RING + (u + 2))
                        high_h(q * RING + u)
                        norm_h(k)
                        if splits and u in (2, 3):
                            high_halves(q, u)
            act.wait_ge(added, 16 * (KT - RING + 1))
            drain_y(KT - 2, (KT - 2) % RING)
            high_h(KT - 1)
            act.wait_ge(added, 16 * (KT - RING + 2))
            drain_y(KT - 1, (KT - 1) % RING)

        @block.vector
        def _(dve):
            steps = [0]

            def then(ins):
                steps[0] += 1
                ins.then_inc(dve_step, 1)
                dve.wait_ge(dve_step, steps[0])

            V = nc.vector
            dve.wait_ge(ld_cond, 32)
            then(V.tensor_scalar(ys[:], cond[:], 1.0 / 16.0, None, ALU.mult))
            for b in range(BATCH):
                for c in range(DC):
                    V.tensor_scalar(condw_b[:, b, c, :], condw[:, c, :], ys[:, c, b:b + 1], None, ALU.mult)\
                        .then_inc(condw_ready, 1)
            V.tensor_tensor(ys2[:], ys[:], ys[:], ALU.mult).then_inc(condw_ready, 1)
            V.tensor_tensor(condw2, condw, condw, ALU.mult).then_inc(condw_ready, 1)
            dve.wait_ge(sqrt_done, 1)
            V.reciprocal(dinv[:], dinv[:]).then_inc(dinv_ready, 1)

            def weight_scale(w, a):
                then(V.tensor_reduce(wstat[:, a, :], w, AX.X, ALU.max, apply_absolute_value=True))
                then(V.tensor_scalar(wstat[:, a, :], wstat[:, a, :], EPS, None, ALU.max))
                then(V.reciprocal(wstat[:, a + 1, :], wstat[:, a, :]))
                V.tensor_scalar(wstat[:, a + 2, :], wstat[:, a + 1, :], 127.0, None, ALU.mult)
                return V.tensor_scalar(wstat[:, a + 3, :], wstat[:, a, :], 1.0 / 127.0, None, ALU.mult)

            dve.wait_ge(ld_win, 16)
            then(weight_scale(win_raw, 0))
            for f in range(FC):
                ins = V.tensor_scalar(win_raw[:, f, :], win_raw[:, f, :], wstat[:, 2, f:f + 1], ROUND, ALU.mult,
                                      ALU.add)
            then(ins)
            then(V.tensor_scalar(win_raw, win_raw, ROUND + 127.0, ROUND - 128.0, ALU.min, ALU.max))
            V.tensor_scalar(win_raw, win_raw, ROUND, None, ALU.subtract).then_inc(winq_ready, 1)
            n = 0
            for b in range(NB):
                for c in range(DC):
                    n += 1
                    dve.wait_ge(x0_ready, n)
                    ins = V.tensor_reduce(amax[:, n - 1:n], x0[:, c, b * BLK:(b + 1) * BLK], AX.X, ALU.max,
                                          apply_absolute_value=True)
                    if n == 2:
                        dve.wait_ge(ld_wout, 16)
                        weight_scale(wout, 4).then_inc(wstat_ready, 1)
            then(ins)
            V.tensor_reduce(amax[:, 8:9], amax[:, 0:8], AX.X, ALU.max).then_inc(xmax_part, 1)
            dve.wait_ge(xmax_all, 1)
            then(V.tensor_scalar(sc[:, 0:1], amax[:, 9:10], EPS, None, ALU.max))
            then(V.reciprocal(sc[:, 1:2], sc[:, 0:1]))
            V.tensor_scalar(sc[:, 2:3], sc[:, 1:2], 32767.0, None, ALU.mult)
            then(V.tensor_scalar(sc[:, 3:4], sc[:, 0:1], 1.0 / 32767.0, None, ALU.mult))
            V.tensor_scalar(gsc[:], wstat[:, 3, :], sc[:, 3:4], None, ALU.mult).then_inc(gsc_ready, 1)
            for b in range(NB):
                t = slice(b * BLK, (b + 1) * BLK)
                dve.wait_ge(xround, b + 1)
                then(V.tensor_scalar(x0[:, :, t], x0[:, :, t], ROUND - 32768.0, ROUND + 32767.0, ALU.max, ALU.min))
                then(V.tensor_scalar(x0_hi, x0[:, :, t], ROUND, ROUND256, ALU.subtract, ALU.add))
                then(V.tensor_scalar(xq[:, 0, :, t], x0_hi, ROUND256, None, ALU.subtract))
                V.scalar_tensor_tensor(xq[:, 1, :, t], x0[:, :, t], ROUND, xq[:, 0, :, t], ALU.subtract,
                                       ALU.subtract).then_inc(xq_ready, 1)
            for n in range(NB * FC):
                b, f = divmod(n, FC)
                dve.wait_ge(gelu_done, n + 1)
                ins = V.tensor_reduce(amax[:, 10 + n:11 + n], hid[:, f, b * BLK:(b + 1) * BLK], AX.X, ALU.max,
                                      apply_absolute_value=True)
            then(ins)
            V.tensor_reduce(amax[:, 42:43], amax[:, 10:42], AX.X, ALU.max).then_inc(hmax_part, 1)
            dve.wait_ge(hmax_all, 1)
            then(V.tensor_scalar(sc[:, 5:6], amax[:, 43:44], EPS, None, ALU.max))
            then(V.reciprocal(sc[:, 6:7], sc[:, 5:6]))
            V.tensor_scalar(sc[:, 7:8], sc[:, 5:6], 1.0 / 32767.0, None, ALU.mult)
            V.tensor_scalar(sc[:, 4:5], sc[:, 6:7], 32767.0, None, ALU.mult).then_inc(hsc_ready, 1)

            def round_hidden(b):
                for f in range(FC):
                    piece = hid[:, f, b * BLK:(b + 1) * BLK]
                    dve.wait_ge(hround, b * FC + f + 1)
                    then(V.tensor_scalar(piece, piece, ROUND - 32768.0, ROUND + 32767.0, ALU.max, ALU.min))
                    V.tensor_scalar(piece, piece, ROUND, None, ALU.subtract).then_inc(hq_ready, 1)

            def drain_x1(b):
                dve.wait_ge(xb_ready, DC)
                for c in range(DC):
                    g = DC * b + c
                    t = slice(b * BLK, (b + 1) * BLK)
                    dve.wait_ge(mm2_done, g + 1)
                    V.scalar_tensor_tensor(x1[:, c, t], bank(g), sc[:, 7:8], x1[:, c, t], ALU.mult, ALU.add)\
                        .then_inc(x1_ready, 1)

            def maxima(slot, half):
                pairs = W[:, bass.ds(raw(slot) + half * 2 * PAIR, 2 * PAIR)].rearrange("p (q n) -> p q n", q=2)
                V.tensor_reduce(part_max[:, 0, half:half + 1], pairs[:, :, 0:I], AX.XY, ALU.max,
                                apply_absolute_value=True)
                V.tensor_reduce(part_max[:, 1, half:half + 1], pairs[:, :, I:PAIR], AX.XY, ALU.max,
                                apply_absolute_value=True).then_inc(max_step, 1)

            def own_maximum(v):
                dve.wait_ge(max_step, v * 2 + 2)
                V.tensor_reduce(own_max[:], part_max[:], AX.X, ALU.max).then_inc(wmax_part, 1)

            def weight_scales(v):
                dve.wait_ge(wmax_all, v + 1)
                col = bass.ds(v, 1)
                V.tensor_scalar(winv[:, :, col], all_max[:].unsqueeze(2), TINY, 1.0 / TOP, ALU.max, ALU.mult)
                V.tensor_scalar(winv_now[:], all_max[:], TINY, 1.0 / TOP, ALU.max, ALU.mult).then_inc(winv_ready, 1)
                dve.wait_ge(winv_ready, v + 1)
                V.reciprocal(wscale[:], winv_now[:]).then_inc(wscale_ready, 1)
                dve.wait_ge(wscale_ready, v + 1)

            def low_halves(slot, v, pairs):
                for p in pairs:
                    for unit in range(2):
                        src, hi, lo = unit_views(slot, p, unit)
                        dve.wait_ge(high_done, v * (2 * PAIRS) + (2 * p + unit + 1))
                        V.scalar_tensor_tensor(lo, src, wscale[:, unit:unit + 1], hi, ALU.mult, ALU.subtract)\
                            .then_inc(low_done, 1)
                if p == PAIRS - 1:
                    dve.wait_ge(low_done, v * (2 * PAIRS) + (2 * PAIRS + 2))
                    dve.sem_inc(split_done, 1)

            def weight_step(e, step):
                if step < 2:
                    maxima(e, step)
                    if step == 1:
                        own_maximum(e + 1)
                else:
                    low_halves(e, e + 1, range(2 * step - 4, 2 * step - 2))

            dve.sem_inc(low_done, 2)
            round_hidden(0)
            round_hidden(1)
            dve.wait_ge(ld_shared, 16)
            for half in range(2):
                maxima(SHARED_SLOT, half)
            own_maximum(0)
            round_hidden(2)
            drain_x1(0)
            weight_scales(0)
            low_halves(SHARED_SLOT, 0, range(PAIRS))
            round_hidden(3)
            drain_x1(1)
            drain_x1(2)
            drain_x1(NB - 1)

            def gate_sum(b, c):
                t = slice(b * BLK, (b + 1) * BLK)
                n = DC * b + c + 1
                dve.wait_ge(gates_done, n)
                then(V.scalar_tensor_tensor(gsum(b, c), fgate[:, c, t], EPS, igate[:, c, t], ALU.add, ALU.add))
                V.reciprocal(gsum(b, c), gsum(b, c)).then_inc(inv_ready, 1)

            def recur(bb, c):
                t = slice(bb * SEQ, (bb + 1) * SEQ)
                dve.wait_ge(decay_ready, DC * (bb + 1) * (SEQ // BLK))
                f = fgate[:, c, t]
                V.tensor_tensor_scan(hT[:, c, t], f, f, cond[:, c, bb:bb + 1], ALU.mult, ALU.bypass)
                dve.wait_ge(info_ready, DC * (bb + 1) * (SEQ // BLK))
                suffix = cand[:, c, t]
                then(V.tensor_tensor_scan(suffix[:, ::-1], f[:, ::-1], f[:, ::-1], 1.0, ALU.mult, ALU.bypass))
                i = igate[:, c, t]
                then(V.tensor_tensor(i, i, suffix, ALU.mult))
                then(V.tensor_tensor_scan(suffix, i, i, 0.0, ALU.add, ALU.bypass))
                V.tensor_tensor(hT[:, c, t], hT[:, c, t], suffix, ALU.add).then_inc(hid_ready, 1)

            def make_rows(t0):
                dve.wait_ge(rows_raw, t0 + 4)
                then(V.tensor_reduce(rstat[:, 0, :], yb[:, 0:4, :], AX.X, ALU.max, apply_absolute_value=True))
                then(V.tensor_scalar(rstat[:, 1, :], rstat[:, 0, :], TINY, 1.0 / TOP, ALU.max, ALU.mult))
                then(V.reciprocal(rstat[:, 2, :], rstat[:, 1, :]))
                r = rows[:, t0:t0 + 4, :]
                V.tensor_copy(r[:, :, INV:INV + 1], rstat[:, 1, :].unsqueeze(2))
                V.memset(r[:, :, WGT:WGT + 1], 1.0)
                V.memset(r[:, :, ROW - 1:ROW], 0.0)
                V.tensor_copy(r[:, :, DST:DST + 1].bitcast(I32), rowid[:, t0:t0 + 4].unsqueeze(2))
                for q in range(4):
                    halves = r[:, q, 0:D].bitcast(F16)
                    ins = V.tensor_scalar(halves[:, 0:D], yb[:, q, :], rstat[:, 2, q:q + 1], None, ALU.mult)
                then(ins)
                for q in range(4):
                    halves = r[:, q, 0:D].bitcast(F16)
                    V.scalar_tensor_tensor(halves[:, D:2 * D], yb[:, q, :], rstat[:, 2, q:q + 1], halves[:, 0:D],
                                           ALU.mult, ALU.subtract).then_inc(rows_ready, 1)

            gate_sum(0, 0)
            gate_sum(0, 1)
            gate_sum(1, 0)
            gate_sum(1, 1)
            gate_sum(2, 0)
            recur(0, 0)
            gate_sum(2, 1)
            recur(0, 1)
            gate_sum(3, 0)
            gate_sum(3, 1)
            dve.wait_ge(consts, 11)
            make_rows(0)
            make_rows(4)
            recur(1, 0)
            recur(1, 1)

            def te(i):
                return rt[:, i, :].rearrange("p (t e) -> p t e", e=E)

            def per_tile(i):
                return r1[:, i, :].unsqueeze(2).to_broadcast([P, T, E])

            def choose():
                logits = te(7)
                dve.wait_ge(logits_kept, 1)
                then(V.tensor_reduce(r1[:, 0, :], logits, AX.X, ALU.max))
                V.tensor_tensor(te(0), logits, per_tile(0), ALU.subtract).then_inc(shifted, 1)
                dve.wait_ge(exp_done, 1)
                then(V.tensor_reduce(r1[:, 1, :], te(1), AX.X, ALU.add))
                then(V.reciprocal(r1[:, 2, :], r1[:, 1, :]))
                then(V.tensor_tensor(te(2), te(1), per_tile(2), ALU.mult))
                for t in range(T):
                    ins = V.max(top[:, t, :], te(2)[:, t, :])
                then(ins)
                for t in range(T):
                    ins = V.max_index(topi[:, t, :], top[:, t, :], te(2)[:, t, :])
                then(ins)
                V.tensor_copy(topf[:], topi[:, :, 0:TOPK].rearrange("p t k -> p k t"))
                then(V.tensor_tensor(r1[:, 3, :], top[:, :, 0], top[:, :, 1], ALU.add))
                then(V.tensor_scalar(r1[:, 3, :], r1[:, 3, :], EPS, None, ALU.add))
                then(V.reciprocal(r1[:, 4, :], r1[:, 3, :]))
                V.tensor_tensor(r1[:, 5, :], top[:, :, 1], r1[:, 4, :], ALU.mult)
                V.tensor_tensor(r1[:, 6, :], top[:, :, 0], r1[:, 4, :], ALU.mult)
                experts_row = iota_f[:, 0:E].unsqueeze(1).to_broadcast([P, T, E])
                for k in range(TOPK):
                    ins = V.tensor_tensor(te(3 + k), experts_row, topf[:, k, :].unsqueeze(2).to_broadcast([P, T, E]),
                                          ALU.is_equal)
                then(ins)
                V.tensor_tensor(chosen[:], te(3), te(4), ALU.add).then_inc(chosen_ready, 1)

            def place():
                dve.wait_ge(rank_done, 1)
                V.tensor_copy(te(7), bank(7, D, P).rearrange("p (t e) -> p t e", e=E))
                et = rt[:, 5, :].rearrange("p (e t) -> p e t", e=E)
                V.tensor_copy(et, bank(7, D + P, P).rearrange("p (t e) -> p e t", e=E)).then_inc(ranks_kept, 1)
                dve.wait_ge(ranks_kept, 1)
                then(V.tensor_tensor_scan(rt[:, 6, :], notfirst.rearrange("p e t -> p (e t)"), rt[:, 5, :], 0.0,
                                          ALU.mult, ALU.add))
                count = rt[:, 6, :].rearrange("p (e t) -> p e t", e=E)
                then(V.tensor_scalar(r8[:, 0, :], count[:, :, T - 1], 1.0 / P, 0.5 - 0.5 / P, ALU.mult, ALU.add))
                then(V.tensor_scalar(r8[:, 1, :], r8[:, 0, :], ROUND, ROUND, ALU.add, ALU.subtract))
                then(V.tensor_scalar(r8[:, 2, :], r8[:, 1, :], 1.0, None, ALU.max))
                then(V.tensor_tensor_scan(r8[:, 3, :], r8[:, 2, :], r8[:, 2, :], 0.0, ALU.add, ALU.bypass))
                then(V.tensor_tensor(r8[:, 4, :], r8[:, 3, :], r8[:, 2, :], ALU.subtract))
                then(V.tensor_scalar(r8[:, 5, :], r8[:, 4, :], float(P), None, ALU.mult))
                then(V.tensor_tensor(rt[:, 5, :], rt[:, 6, :], rt[:, 5, :], ALU.subtract))
                then(V.tensor_tensor(te(7), te(7), et.rearrange("p e t -> p t e"), ALU.add))
                then(V.tensor_tensor(te(7), te(7), r8[:, 5, :].unsqueeze(1).to_broadcast([P, T, E]), ALU.add))
                for k in range(TOPK):
                    then(V.tensor_tensor(te(3 + k), te(3 + k), te(7), ALU.mult))
                    then(V.tensor_reduce(topf[:, k, :], te(3 + k), AX.X, ALU.add))
                V.tensor_scalar(slot_of[:], topf[:], float(TOK), None, ALU.add)
                dve.wait_ge(rows_low, 16 * T // 2)
                dve.wait_ge(rows_high, 16 * T // 2)
                V.tensor_copy(rows[:, :, WGT:WGT + 1], r1[:, 6, :].unsqueeze(2)).then_inc(route_ready, 1)
                then(V.tensor_tensor(owner_f, r8[0:1, 3, :].unsqueeze(1).to_broadcast([1, JT + 1, E]),
                                     iota_f[0:1, :].unsqueeze(2).to_broadcast([1, JT + 1, E]), ALU.is_le))
                then(V.tensor_reduce(owner_r[:], owner_f, AX.X, ALU.add))
                then(V.tensor_scalar(owner_r[:], owner_r[:], E - 1.0, None, ALU.min))
                V.tensor_scalar(tile_v[0:1, T:KT + 1], owner_r[:], 1.0, None, ALU.add)
                V.tensor_scalar(tile_at[0:1, T:KT + 1], owner_r[:], 2.0 * EW, None, ALU.mult).then_inc(owner_ready, 1)

            up_ps = ps[:, 2 * BANK:4 * BANK].rearrange("p (b n) -> p b n", b=2)[:, :, 0:HALF]

            def times_up(k, first=False):
                dve.wait_ge(u_done, k + 1)
                dve.wait_ge(silu_ready, k + 1)
                if not first:
                    dve.wait_ge(hn_ready, k)
                V.tensor_tensor(h.rearrange("p (b n) -> p b n", b=2), silu, up_ps, ALU.mult).then_inc(h_ready, 1)
                dve.wait_ge(h_ready, k + 1)
                V.tensor_reduce(h_inv[:, 0:1], h, AX.X, ALU.max, apply_absolute_value=True).then_inc(h_step, 1)
                dve.wait_ge(h_step, k * 3 + 1)
                V.tensor_scalar(h_inv[:, 1:2], h_inv[:, 0:1], TINY, 1.0 / TOP, ALU.max, ALU.mult).then_inc(h_step, 1)
                dve.wait_ge(h_step, k * 3 + 2)
                V.reciprocal(h_inv[:, 2:3], h_inv[:, 1:2]).then_inc(h_step, 1)
                one = bass.ds(k, 1)
                V.scalar_tensor_tensor(y_scale[:, one], h_inv[:, 1:2], gup_inv[:, one], out_wgt[:, one], ALU.mult,
                                       ALU.mult).then_inc(yscale_ready, 1)

            def take_meta(k, u, loaded, v):
                dve.wait_ge(*loaded)
                one = bass.ds(k, 1)
                V.tensor_tensor(gup_inv[:, one], xin[:, u, INV:INV + 1], winv[:, 0, bass.ds(v, 1)], ALU.mult)
                V.tensor_tensor(out_wgt[:, one], xin[:, u, WGT:WGT + 1], winv[:, 1, bass.ds(v, 1)], ALU.mult)
                V.tensor_copy(dst[:, one], xin[:, u, DST:DST + 1].bitcast(I32)).then_inc(meta_ready, 1)

            def low_h(k):
                dve.wait_ge(hT_high, k + 1)
                V.tensor_tensor(h_T[:, 1].rearrange("p c t -> p (c t)"), ps[:, 4 * BANK:6 * BANK],
                                h_T[:, 0].rearrange("p c t -> p (c t)"), ALU.subtract).then_inc(hT_low, 1)

            def scales_of(k):
                return dve.value_load(tile_v[0:1, bass.ds(k, 1)], min_val=0, max_val=E)

            take_meta(0, 0, (xin_ready[0], 16), 0)
            for k in range(T):
                times_up(k, k == 0)
                i = k + 1
                take_meta(i, i % RING, (xin_ready[i % RING], 16 * (i // RING + 1)), scales_of(i) if i >= T else 0)
                e, step = BESIDE.get(k, (0, 0))
                if step == 2:
                    weight_scales(e + 1)
                if k >= 1:
                    low_h(k - 1)
                if k == 0:
                    dve.wait_ge(logits_done, 1)
                    V.tensor_copy(rt[:, 7, :], bank(5, 0, P)).then_inc(logits_kept, 1)
                if k < 2:
                    make_rows(8 + 4 * k)
                if k == 2:
                    choose()
                if k == 3:
                    place()
                if k in BESIDE:
                    if step == 0:
                        dve.wait_ge(ld_exp[e], 16)
                    weight_step(e, step)
            for steps_, splits in (((ROUTED, SPLIT_TO), True), ((SPLIT_TO, LAST), False)):
                with dve.Fori(*steps_) as q:
                    for u in range(RING):
                        k = q * RING + (u + 1)
                        times_up(k)
                        i = q * RING + (u + 2)
                        more, v = divmod(u + 2, RING)
                        take_meta(i, v, (xin_ready[v], (q + (more + 1)) * 16), scales_of(i))
                        if splits and u == 2:
                            weight_scales(q + 1)
                        low_h(q * RING + u)
                        if splits and u < STEPS:
                            if u == 0:
                                dve.wait_ge(ld_late, 16 * (q - (ROUTED - 1)))
                            weight_step(q, u)
            low_h(KT - 1)

        @block.tensor
        def _(pe):
            M = nc.tensor.matmul
            pe.wait_ge(condw_ready, BATCH * DC)
            n = 0
            for b in range(NB):
                pe.wait_ge(ld_x[b], 16)
                for o in range(DC):
                    n += 1
                    if n == 3:
                        pe.wait_ge(condw_ready, BATCH * DC + 2)
                        for oo in range(DC):
                            for c in range(DC):
                                ins = M(bank(7, oo * BATCH, BATCH), condw2[:, c, oo * P:(oo + 1) * P], ys2[:, c, :],
                                        start=(c == 0), stop=(c == DC - 1))
                        ins.then_inc(dsum_done, 1)
                    if n == 8:
                        pe.wait_ge(sqrt_done, 1)
                    for c in range(DC):
                        ins = M(bank(n - 1), condw_b[:, b * BLK // SEQ, c, o * P:(o + 1) * P],
                                x1[:, c, b * BLK:(b + 1) * BLK], start=(c == 0), stop=(c == DC - 1))
                    ins.then_inc(xs_mm, 1)
            pe.wait_ge(ident_ok, 1)
            pe.wait_ge(winq_ready, 1)
            for c in range(DC):
                for half in range(2):
                    pe.wait_ge(x0_ready, 2 * c + half + 1)
                    for q in range(4):
                        f = half * 4 + q
                        ins = nc.tensor.transpose(bank(2 * c + half, q * P, P), win_raw[:, f, c * P:(c + 1) * P],
                                                  ident[:])
                    ins.then_inc(wint_done, 1)
            pe.wait_ge(win_ready, 4)
            for g in range(NB * FC):
                b, f = divmod(g, FC)
                if f == 0:
                    pe.wait_ge(xq_ready, b + 1)
                if g < 4:
                    pe.wait_ge(x0_ready, 4 + g + 1)
                if g >= 8:
                    pe.wait_ge(gelu_done, g - 7)
                for c in range(DC):
                    for half in range(2):
                        ins = M(bank((g + 4) % 8), win_q[:, c, f * P:(f + 1) * P],
                                xq[:, half, c, b * BLK:(b + 1) * BLK], start=(c == 0 and half == 0),
                                stop=(c == DC - 1 and half == 1))
                ins.then_inc(mm1_done, 1)
            pe.wait_ge(woutq_ready, FC)
            pe.wait_ge(gelu_done, NB * FC)
            for b in range(NB):
                for f in range(FC):
                    pe.wait_ge(hq_ready, b * FC + f + 1)
                    for o in range(DC):
                        ins = M(bank(DC * b + o), wout_q[:, f, o * P:(o + 1) * P], hid[:, f, b * BLK:(b + 1) * BLK],
                                start=(f == 0), stop=(f == FC - 1))
                        if f == FC - 1:
                            ins.then_inc(mm2_done, 1)
            pe.wait_ge(ld_small, 16 * 3)
            for n in range(NB * DC):
                b, o = divmod(n, DC)
                a = 3 * (n % 2)
                pe.wait_ge(x1_ready, max(DC * (b + 1), a + 3))
                if n >= 2:
                    pe.wait_ge(gates_done, n - 1)
                for g in range(3):
                    for c in range(DC):
                        ins = M(bank(a + g), recw[:, g, c, o * P:(o + 1) * P], x1[:, c, b * BLK:(b + 1) * BLK],
                                start=(c == 0), stop=(c == DC - 1))
                ins.then_inc(rec_done, 1)
                if o:
                    pe.wait_ge(x1_ready, NB * DC)
                    for t in range(4 * b, 4 * b + 4):
                        if t >= 2:
                            pe.wait_ge(x1r_ready, t - 1)
                        for c in range(DC):
                            ins = nc.tensor.transpose(bank(6 + t % 2, c * P, P),
                                                      x1[:, c, t * P:(t + 1) * P], ident[:])
                        ins.then_inc(x1t_done, 1)

            def turn_rows(t0):
                for t in range(t0, t0 + 4):
                    if t >= 2:
                        pe.wait_ge(rows_raw, t - 1)
                    for c in range(DC):
                        ins = nc.tensor.transpose(bank(6 + t % 2, D + c * P, P), hT[:, c, t * P:(t + 1) * P],
                                                  ident[:])
                    ins.then_inc(rowt_done, 1)

            pe.wait_ge(x1r_ready, T)
            pe.wait_ge(hid_ready, DC)
            turn_rows(0)
            turn_rows(4)

            def turn_x(u, loaded):
                pe.wait_ge(*loaded)
                halves = xin[:, u, 0:D].bitcast(F16)
                to = bank(7, 0, D).bitcast(F16)
                for q in range(2 * DC):
                    ins = nc.tensor.transpose(to[:, q * P:(q + 1) * P], halves[:, q * P:(q + 1) * P], ident_h[:])
                ins.then_inc(xT_raw, 1)

            def product(which, at):
                for c in range(DC):
                    a = 2 * PAIR * (2 * c + which)
                    for part, low in ((0, 0), (0, 1), (1, 0)):
                        for b in range(2):
                            ins = M(bank(2 * which + b, 0, HALF), xT[:, part, c, :],
                                    Wh[:, bass.ds(at + (a + low * I + b * HALF), HALF)],
                                    start=(c == 0 and part == 0 and low == 0), stop=(c == DC - 1 and part == 1))
                return ins

            def gate_up(k, at, first=False):
                pe.wait_ge(xT_ready, k + 1)
                if not first:
                    pe.wait_ge(silu_ready, k)
                product(0, at).then_inc(g_done, 1)
                if not first:
                    pe.wait_ge(h_ready, k)
                product(1, at).then_inc(u_done, 1)

            def down(i, at, first=False):
                pe.wait_ge(hT_low, i + 1)
                if not first:
                    pe.wait_ge(y_ready, i)
                for c in range(IC):
                    a = 2 * (c // 2 * PAIR + I) + c % 2 * D
                    for part, low in ((0, 0), (0, 1), (1, 0)):
                        ins = M(bank(6, 0, D), h_T[:, part, c, :], Wh[:, bass.ds(at + (a + low * DU), D)],
                                start=(c == 0 and part == 0 and low == 0), stop=(c == IC - 1 and part == 1))
                ins.then_inc(d_done, 1)

            def turn_h(i, first=False):
                pe.wait_ge(hn_ready, i + 1)
                if not first:
                    pe.wait_ge(hT_low, i)
                for c in range(IC):
                    ins = nc.tensor.transpose(bank(4, c * P, P), hn[:, c * P:(c + 1) * P], ident[:])
                ins.then_inc(t_done, 1)

            def weights_of(k):
                v = pe.value_load(tile_v[0:1, bass.ds(k, 1)], min_val=0, max_val=E)
                pe.wait_ge(split_done, v + 1)
                return place_of(k)

            def place_of(k):
                return pe.value_load(tile_at[0:1, bass.ds(k, 1)], min_val=0, max_val=2 * SHARED_SLOT * EW)

            shared = 2 * SHARED_SLOT * EW
            pe.wait_ge(consts, 11)
            pe.wait_ge(split_done, 1)
            pe.wait_ge(gates_done, NB * DC)
            pe.wait_ge(rows_raw, 8)
            turn_x(0, (xin_ready[0], 16))
            for k in range(1 + RING * STEP0):
                gate_up(k, shared, k == 0)
                if k in (1, 2):
                    pe.wait_ge(rows_raw, 8 + 4 * k)
                if k == 4:
                    pe.wait_ge(ranks_kept, 1)
                if k >= 2:
                    down(k - 2, shared, k == 2)
                i = k + 1
                turn_x(i % RING, (xin_ready[i % RING], 16 * (i // RING + 1)))
                if k >= 1:
                    turn_h(k - 1, k == 1)
                if k == 0:
                    pe.wait_ge(hid_ready, BATCH * DC)
                    for t in range(T):
                        for c in range(DC):
                            ins = M(bank(5, t * E, E), hT[:, c, t * P:(t + 1) * P], gatew[:, c, :],
                                    start=(c == 0), stop=(c == DC - 1))
                    ins.then_inc(logits_done, 1)
                    pe.wait_ge(logits_kept, 1)
                if k < 2:
                    pe.wait_ge(xT_ready, k + 2)
                    turn_rows(8 + 4 * k)
                if k == 3:
                    pe.wait_ge(xT_ready, k + 2)
                    pe.wait_ge(chosen_ready, 1)
                    flat = chosen[:].rearrange("p t e -> p (t e)")
                    M(bank(7, D, P), before[:], flat, start=True, stop=True)
                    M(bank(7, D + P, P), ones[:], flat, start=True, stop=True).then_inc(rank_done, 1)
            pe.wait_ge(owner_ready, 1)
            with pe.Fori(STEP0, LAST) as q:
                for u in range(RING):
                    k = q * RING + (u + 1)
                    gate_up(k, weights_of(k))
                    down(q * RING + (u - 1), place_of(q * RING + (u - 1)))
                    more, v = divmod(u + 2, RING)
                    turn_x(v, (xin_ready[v], (q + (more + 1)) * 16))
                    turn_h(q * RING + u)
            down(KT - 2, place_of(KT - 2))
            turn_h(KT - 1)
            down(KT - 1, place_of(KT - 1))


def kernel(**inputs):
    import numpy as np
    import concourse.bacc as bacc
    from concourse.bass_utils import run_bass_kernel_spmd as run

    def part(a, c):
        return np.ascontiguousarray(a.reshape(c, P, -1).transpose(1, 0, 2))

    n = {k: np.asarray(v) for k, v in inputs.items()}

    def expert(gate_up, down):
        gu = part(gate_up.T, DC).reshape(P, PAIRS, I)
        dn = part(np.pad(down.T, ((0, IC * P - I), (0, 0))), IC).reshape(P, PAIRS, DU)
        return np.concatenate([gu, dn], 2).reshape(P, EW)

    all_experts = [expert(n["L1_ffn_experts_gate_up"][e], n["L1_ffn_experts_down"][e]) for e in range(E)]
    all_experts.append(expert(n["L1_ffn_shared_gate_up"], n["L1_ffn_shared_down"]))
    bias = [part(n["L0_ffn_b_in"][:, None], FC)[:, :, 0], part(n["L0_ffn_b_out"][:, None], DC)[:, :, 0]]
    bias += [part(n[f"L1_cond_b_{g}"][:, None], DC)[:, :, 0] for g in "fih"]
    arrays = {
        "x_t": part(n["x"].reshape(TOK, D).T, DC),
        "cond_t": part(n["cond_1024"].T, DC),
        "cond_w": part(n["L0_cond_weight"], DC),
        "w_in_t": part(n["L0_ffn_W_in"].T, FC),
        "w_out": part(n["L0_ffn_W_out"], FC),
        "bias": np.concatenate(bias, 1),
        "rec_w": np.ascontiguousarray(np.stack([part(n[f"L1_cond_W_{g}"].T, DC) for g in "fih"], 1)),
        "gate_w": part(n["L1_ffn_gate_weight"].T, DC),
        "experts": np.stack(all_experts),
    }
    nc = bacc.Bacc("TRN2", target_bir_lowering=False, num_devices=1, dynamic_dma_scratch_size=4096)
    args = [nc.dram_tensor(f"in_{k}", a.shape, F32, kind="ExternalInput").ap() for k, a in arrays.items()]
    out = nc.dram_tensor("out_rows", (OUTR, D), F32, kind="ExternalOutput").ap()
    adaln_ffn_moe(nc, *args, out)
    r = run(nc, [{f"in_{k}": a for k, a in arrays.items()}], core_ids=[0])
    return r.results[0]["out_rows"][:TOK].reshape(BATCH, SEQ, D)
```

```python
import concourse.bass as bass
from concourse import mybir
from contextlib import ExitStack

F32 = mybir.dt.float32
F16 = mybir.dt.float16
BF16 = mybir.dt.bfloat16
I32 = mybir.dt.int32
U32 = mybir.dt.uint32
ALU = mybir.AluOpType
ACT = mybir.ActivationFunctionType
AX = mybir.AxisListType
ABSMAX = bass.bass_isa.ReduceOp.absmax

P = 128
BATCH, SEQ, D = 2, 1024, 256
TOK = BATCH * SEQ
DC = D // P
FF = 1024
FC = FF // P
E = 8
TOPK = 2
I = 938
IC = -(-I // P)
HALF = I // 2
PAIRS = 2 * DC
DU = IC * D // PAIRS
PAIR = I + DU
SHIFT = PAIR
EW = PAIRS * PAIR
BANK = 512
BLK = 512
NB = TOK // BLK
PAIRS_H = NB * FC // 2
T = TOK // P
JT = TOPK * TOK // P + E
KT = T + JT
RING = 5
ROUTED = (T - 1) // RING
LAST = (KT - 1) // RING
assert 1 + ROUTED * RING == T and 1 + LAST * RING == KT
ROW = D + 4
INV, WGT, DST = D, D + 1, D + 2
SLOTS = (JT + 1) * P
OUTR = TOK + P
SHARED_SLOT = E - 1

ROUND = 1.5 * 2.0 ** 23
ROUND256 = ROUND * 256
EPS = 1e-8
TINY = 1e-30
TOP = 2.0 ** 14
TOP_SUM = 2.0 ** 15

UNITS = 2 * PAIRS
STEP_UNITS = {2: range(0, 3), 3: range(3, 6), 4: range(6, UNITS)}
BESIDE = {3: [(0, 0)], 7: [(0, 1)], 8: [(0, 2)], 10: [(0, 3)], 11: [(0, 4)], 12: [(1, 0), (1, 1)], 13: [(1, 2)],
          14: [(1, 3)], 15: [(1, 4)]}
FIRST_LATE = 2
SPLIT_TO = ROUTED + E - FIRST_LATE
SENDS = {9 + n: range(8 * n, 8 * n + 8) for n in range(4)}
TURN = (6, 7)
LOGITS, CHOOSE, WEIGH, PLACE = 6, 7, 8, 9
LOGIT_BANKS = (2, 1)


def adaln_ffn_moe(nc, x_t, cond_t, cond_w, w_in_t, w_out, bias, rec_w, gate_w, experts, out):
    moved = nc.dram_tensor("moved_rows", (SLOTS, ROW), F32, kind="Internal").ap()
    ctx = ExitStack()
    with ctx:
        def sb(name, shape, dt=F32):
            return ctx.enter_context(nc.sbuf_tensor(name, shape, dt))

        def sem(name):
            return ctx.enter_context(nc.semaphore(name))

        W = sb("weight_slots", [P, SHIFT + E * EW])
        Wh = W[:].bitcast(F16)

        def chunks(ap, c):
            return ap.rearrange("p (c n) -> p c n", c=c)

        def raw(e):
            return e * EW + SHIFT

        NX = DC * TOK
        x0 = chunks(W[:, 0:NX], DC)
        condw = chunks(W[:, NX:NX + DC * D], DC)
        condw_b = W[:, NX + DC * D:NX + 3 * DC * D].rearrange("p (b c n) -> p b c n", b=BATCH, c=DC)
        condw2 = chunks(W[:, NX + 3 * DC * D:NX + 4 * DC * D], DC)
        at = raw(1)
        win_raw = chunks(W[:, at:at + FC * D], FC)
        wout_q = W[:, at:at + FC * D // 2].bitcast(F16).rearrange("p (c n) -> p c n", c=FC)
        at += FC * D
        wout = chunks(W[:, at:at + FC * D], FC)
        at += FC * D
        win_q = W[:, at:at + DC * FF // 2].bitcast(BF16).rearrange("p (c f) -> p c f", c=DC)
        at = raw(2)
        fgate = chunks(W[:, at:at + NX], DC)
        igate = chunks(W[:, at + NX:at + 2 * NX], DC)
        cand = chunks(W[:, at + 2 * NX:at + 3 * NX], DC)
        at += 3 * NX
        rows = chunks(W[:, at:at + T * ROW], T)

        def hid(b, f):
            g = raw(5) - FC * TOK + (b * FC + f) * BLK
            return W[:, g:g + BLK]

        def hid_pair(m):
            g = raw(5) - FC * TOK + 2 * m * BLK
            return W[:, g:g + 2 * BLK]

        def hid_halves(m):
            g = raw(5) - FC * TOK + 2 * (m - 2) * BLK
            return Wh[:, 2 * g:2 * g + 4 * BLK].rearrange("p (q h n) -> p q h n", q=2, h=2)

        assert raw(5) - FC * TOK - 4 * BLK >= raw(1) + 2 * FC * D

        def gsum(b, c):
            g = at + b * BLK // SEQ * (T // BATCH * ROW) + (b % (SEQ // BLK) * DC + c) * BLK
            return W[:, g:g + BLK]

        x1 = chunks(W[:, raw(5):raw(5) + NX], DC)
        a5 = raw(5) + NX
        recw = W[:, a5:a5 + 3 * DC * D].rearrange("p (g c h) -> p g c h", g=3, c=DC)
        hrow = chunks(W[:, raw(5):raw(5) + 4 * D], 4)
        rt = chunks(W[:, a5:a5 + 8 * P], 8)
        top = W[:, a5 + 8 * P:a5 + 9 * P].rearrange("p (t n) -> p t n", t=T)
        topi = W[:, a5 + 9 * P:a5 + 10 * P].bitcast(U32).rearrange("p (t n) -> p t n", t=T)
        owner_f = W[0:1, a5:a5 + (JT + 1) * E].rearrange("p (j e) -> p j e", e=E)
        a6 = SHARED_SLOT * EW - NX - ROW
        assert a6 >= a5 + 3 * DC * D
        xq = W[:, a6:a6 + NX].bitcast(BF16).rearrange("p (h c t) -> p h c t", h=2, c=DC)
        hT = chunks(W[:, a6:a6 + NX], DC)
        blank = W[:, a6 + NX:a6 + NX + ROW]

        cond = sb("cond", [P, DC, BATCH])
        ys = sb("ys", [P, DC, BATCH])
        ys2 = sb("ys2", [P, DC, BATCH])
        dinv = sb("dinv", [P, DC, BATCH])
        bia = sb("bia", [P, 16])
        b_in, b_out = bia[:, 0:FC], bia[:, FC:FC + DC]
        b_rec = bia[:, FC + DC:FC + 4 * DC].rearrange("p (g c) -> p g c", g=3)
        eps = sb("eps", [P, 1])
        big = sb("big", [P, 1])
        ident = sb("ident", [P, P])
        ident_h = sb("ident_h", [P, P], F16)
        before = sb("before", [P, P], BF16)
        ones = sb("ones", [P, P], BF16)
        notfirst = sb("notfirst", [P, E, T])
        wstat = sb("wstat", [P, 8, FC])
        amax = sb("amax", [P, 44])
        sc = sb("sc", [P, 8])
        wtop = sb("wtop", [P, 4])
        wsf = sb("wsf", [P, FC])
        gsc = sb("gsc", [P, FC])
        gatew = sb("gatew", [P, DC, E])
        rstat = sb("rstat", [P, 3, 4])
        r1 = sb("r1", [P, 8, T])
        topf = sb("topf", [P, TOPK, T])
        chosen = sb("chosen", [P, T, E], BF16)
        iota_i = sb("iota_i", [P, JT + 1], I32)
        iota_f = sb("iota_f", [P, JT + 1])
        rowid = sb("rowid", [P, T], I32)
        r8 = sb("r8", [P, 6, E])
        slot_of = sb("slot_of", [P, TOPK, T], U32)
        owner_r = sb("owner_r", [1, JT + 1])
        tile_slot = sb("tile_slot", [1, KT + 1], I32)
        part_max = sb("part_max", [P, 2, 2])
        own_max = sb("own_max", [P, 2])
        all_max = sb("all_max", [P, 2])
        winv_now = sb("winv_now", [P, 2])
        wscale = sb("wscale", [P, 2])
        winv = sb("winv", [P, 2, E + 1])
        xin = sb("xin", [P, RING, ROW])
        gup_inv = sb("gup_inv", [P, KT + 1])
        out_wgt = sb("out_wgt", [P, KT + 1])
        y_scale = sb("y_scale", [P, KT])
        dst = sb("dst", [P, KT + 1], I32)
        xT = sb("xT", [P, 2, DC, P], F16)
        work = sb("work", [P, 2 * I])
        silu = work[:, 0:I].rearrange("p (b n) -> p b n", b=2)
        h = work[:, I:2 * I]
        x0_hi = chunks(work[:, 0:DC * BLK], DC)
        x1r = chunks(work[:, 0:4 * D], 4)
        h_inv = sb("h_inv", [P, 3])
        hn = sb("hn", [P, IC * P])
        h_T = sb("h_T", [P, 2, IC, P], F16)
        yb = sb("yb", [P, RING, D])
        idx = sb("idx", [P, RING], U32)

        ps = ctx.enter_context(nc.psum_tensor("ps", [P, 8 * BANK], F32))

        def bank(b, a=0, n=BANK):
            return ps[:, b * BANK + a:b * BANK + a + n]

        def unit_views(slot, n):
            a = slot * EW + (n // 2 * PAIR + n % 2 * I)
            w = (I, DU)[n % 2]
            return W[:, bass.ds(a + SHIFT, w)], Wh[:, bass.ds(a * 2, w)], Wh[:, bass.ds(a * 2 + w, w)]

        ld_cond = sem("ld_cond")
        ld_bias = sem("ld_bias")
        ld_small = sem("ld_small")
        ld_win = sem("ld_win")
        ld_wout = sem("ld_wout")
        ld_shared = sem("ld_shared")
        consts = sem("consts")
        ident_ok = sem("ident_ok")
        blank_ok = sem("blank_ok")
        blank_out = sem("blank_out")
        dve_step = sem("dve_step")
        pool_step = sem("pool_step")
        condw_ready = sem("condw_ready")
        dsum_done = sem("dsum_done")
        sqrt_done = sem("sqrt_done")
        dinv_ready = sem("dinv_ready")
        xs_mm = sem("xs_mm")
        x0_ready = sem("x0_ready")
        xmax_part = sem("xmax_part")
        xmax_all = sem("xmax_all")
        winq_ready = sem("winq_ready")
        wint_done = sem("wint_done")
        win_ready = sem("win_ready")
        wstat_ready = sem("wstat_ready")
        wq_step = sem("wq_step")
        gsc_ready = sem("gsc_ready")
        xround = sem("xround")
        xq_ready = sem("xq_ready")
        mm1_done = sem("mm1_done")
        gelu_done = sem("gelu_done")
        hmax_part = sem("hmax_part")
        hmax_all = sem("hmax_all")
        hsc_ready = sem("hsc_ready")
        hround = sem("hround")
        hclamp = sem("hclamp")
        hscaled = sem("hscaled")
        hhigh = sem("hhigh")
        wtop_part = sem("wtop_part")
        wtop_all = sem("wtop_all")
        wsf_ready = sem("wsf_ready")
        hq_ready = sem("hq_ready")
        woutq_ready = sem("woutq_ready")
        xb_ready = sem("xb_ready")
        mm2_done = sem("mm2_done")
        x1_ready = sem("x1_ready")
        rec_done = sem("rec_done")
        gates_done = sem("gates_done")
        inv_ready = sem("inv_ready")
        rec_step = sem("rec_step")
        info_ready = sem("info_ready")
        decay_ready = sem("decay_ready")
        hid_ready = sem("hid_ready")
        x1t_done = sem("x1t_done")
        x1r_ready = sem("x1r_ready")
        rowt_done = sem("rowt_done")
        rows_raw = sem("rows_raw")
        rows_ready = sem("rows_ready")
        logits_done = sem("logits_done")
        logits_kept = sem("logits_kept")
        shifted = sem("shifted")
        exp_done = sem("exp_done")
        chosen_ready = sem("chosen_ready")
        top_ready = sem("top_ready")
        rank_done = sem("rank_done")
        ranks_kept = sem("ranks_kept")
        route_ready = sem("route_ready")
        weight_set = sem("weight_set")
        sent = sem("sent")
        owner_ready = sem("owner_ready")
        max_step = sem("max_step")
        wmax_part = sem("wmax_part")
        max_turn = sem("max_turn")
        winv_ready = sem("winv_ready")
        wmax_all = sem("wmax_all")
        wscale_ready = sem("wscale_ready")
        high_done = sem("high_done")
        low_done = sem("low_done")
        split_done = sem("split_done")
        xT_raw = sem("xT_raw")
        xT_ready = sem("xT_ready")
        meta_ready = sem("meta_ready")
        g_done = sem("g_done")
        u_done = sem("u_done")
        silu_ready = sem("silu_ready")
        h_ready = sem("h_ready")
        h_summed = sem("h_summed")
        h_step = sem("h_step")
        yscale_ready = sem("yscale_ready")
        hn_ready = sem("hn_ready")
        t_done = sem("t_done")
        hT_high = sem("hT_high")
        hT_low = sem("hT_low")
        d_done = sem("d_done")
        y_ready = sem("y_ready")
        idx_ready = sem("idx_ready")
        add_turn = sem("add_turn")
        added = sem("added")
        ld_x = [sem(f"ld_x{b}") for b in range(NB)]
        stored = [sem(f"stored{u}") for u in range(4)]
        xin_ready = [sem(f"xin_ready{u}") for u in range(RING)]
        ld_exp = [sem(f"ld_exp{e}") for e in range(ROUTED)]
        ld_late = sem("ld_late")

        block = ctx.enter_context(nc.Block())

        @block.sync
        def _(sp):
            sp.dma_start(cond[:], cond_t).then_inc(ld_cond, 16)
            sp.dma_start(condw, cond_w).then_inc(ld_cond, 16)
            for b in range(NB):
                t = slice(b * BLK, (b + 1) * BLK)
                sp.dma_start(x1[:, :, t], x_t[:, :, t]).then_inc(ld_x[b], 16)
            sp.dma_start(win_raw, w_in_t).then_inc(ld_win, 16)
            sp.dma_start(bia[:], bias).then_inc(ld_bias, 16)
            sp.dma_start(wout, w_out).then_inc(ld_wout, 16)
            sp.dma_start(W[:, raw(SHARED_SLOT):raw(SHARED_SLOT) + EW], experts[E]).then_inc(ld_shared, 16)
            sp.dma_start(recw, rec_w).then_inc(ld_small, 16)
            sp.dma_start(gatew[:], gate_w).then_inc(ld_small, 16)
            sp.wait_ge(blank_ok, 1)
            sp.dma_start(moved.rearrange("(j p) n -> p j n", p=P),
                         blank.unsqueeze(1).to_broadcast([P, JT + 1, ROW])).then_inc(blank_out, 16)

            def load_expert(e):
                sp.dma_start(W[:, raw(e):raw(e) + EW], experts[e]).then_inc(ld_exp[e], 16)

            sp.wait_ge(xq_ready, NB)
            sp.wait_ge(xs_mm, NB * DC)
            load_expert(0)
            sp.wait_ge(mm2_done, NB * DC)
            load_expert(1)
            for t in range(T):
                sp.wait_ge(x1r_ready, t + 1)
                sp.dma_start(out[t * P:(t + 1) * P, :], x1r[:, t % 4, :]).then_inc(stored[t % 4], 16)

            def load_x(j, u):
                sp.dma_start(xin[:, u, :], moved[bass.ds(j * P, P), :]).then_inc(xin_ready[u], 16)

            def load_late(e):
                if e > FIRST_LATE:
                    sp.wait_ge(ld_late, 16 * (e - FIRST_LATE))
                sp.dma_start(W[:, raw(e):raw(e) + EW], experts[e]).then_inc(ld_late, 16)

            sp.wait_ge(hid_ready, BATCH * DC)
            load_late(2)
            load_late(3)
            sp.wait_ge(sent, 16 * TOPK * T)
            sp.wait_ge(blank_out, 16)
            for j in range(RING):
                load_x(j, j)
            sp.wait_ge(xT_ready, T)
            sp.wait_ge(meta_ready, T)
            load_late(4)
            sp.wait_ge(owner_ready, 1)
            for j in range(RING, 3 * RING):
                sp.wait_ge(xT_ready, T + j - RING + 1)
                sp.wait_ge(meta_ready, T + j - RING + 1)
                load_x(j, j % RING)
                if j == RING:
                    load_late(5)
                if j == 2 * RING - 1:
                    sp.wait_ge(d_done, T)
                    load_late(6)
                if j == 3 * RING - 2:
                    load_late(7)
            with sp.Fori(3, JT // RING) as g:
                for u in range(RING):
                    sp.wait_ge(xT_ready, g * RING + (u + 1 + T - RING))
                    sp.wait_ge(meta_ready, g * RING + (u + 1 + T - RING))
                    load_x(g * RING + u, u)
            sp.wait_ge(xT_ready, KT - RING + 1)
            sp.wait_ge(meta_ready, KT - RING + 1)
            load_x(JT, 0)
            sp.wait_ge(xin_ready[0], 16 * (JT // RING + 1))
            sp.wait_ge(added, 16 * (KT + 2))

        @block.gpsimd
        def _(pool):
            G = nc.gpsimd
            G.memset(ident[:], 0.0).then_inc(pool_step, 1)
            G.memset(before[:], 1.0).then_inc(pool_step, 1)
            G.memset(notfirst[:], 1.0).then_inc(pool_step, 1)
            G.memset(blank, 0.0).then_inc(pool_step, 1)
            G.iota(iota_i[:], [[1, JT + 1]], base=0, channel_multiplier=0).then_inc(pool_step, 1)
            G.memset(eps[:], EPS).then_inc(consts, 1)
            G.memset(big[:], ROUND).then_inc(consts, 1)
            G.memset(ones[:], 1.0).then_inc(consts, 1)
            G.iota(rowid[:], [[P, T]], base=0, channel_multiplier=1).then_inc(consts, 1)
            G.memset(hn[:, I:IC * P], 0.0).then_inc(consts, 1)
            G.memset(tile_slot[0:1, 0:T], SHARED_SLOT).then_inc(consts, 1)
            pool.wait_ge(pool_step, 5)
            G.affine_select(out=ident[:], in_=ident[:], compare_op=ALU.not_equal, fill=1.0, base=0,
                            pattern=[[-1, P]], channel_multiplier=1).then_inc(ident_ok, 1)
            G.affine_select(out=before[:], in_=before[:], compare_op=ALU.is_gt, fill=0.0, base=0,
                            pattern=[[1, P]], channel_multiplier=-1).then_inc(consts, 1)
            G.memset(notfirst[:, :, 0:1], 0.0).then_inc(consts, 1)
            G.iota(blank[:, DST:DST + 1].bitcast(I32), [[0, 1]], base=TOK, channel_multiplier=1)\
                .then_inc(blank_ok, 1)
            G.tensor_copy(iota_f[:], iota_i[:]).then_inc(consts, 1)
            pool.wait_ge(ident_ok, 1)
            G.tensor_copy(ident_h[:], ident[:]).then_inc(consts, 1)
            pool.wait_ge(blank_ok, 1)
            for q in range(2):
                G.dma_start(out[TOK + q * 64:TOK + q * 64 + 64, :], blank[q * 64:q * 64 + 64, 0:D])\
                    .then_inc(added, 16)
            pool.wait_ge(xmax_part, 1)
            G.partition_all_reduce(amax[:, 9:10], amax[:, 8:9], P, ABSMAX).then_inc(xmax_all, 1)
            pool.wait_ge(ld_bias, 16)
            pool.wait_ge(xs_mm, NB * DC)
            for c in range(DC):
                G.tensor_scalar(x1[:, c, :], x1[:, c, :], b_out[:, c:c + 1], 1.0, ALU.add, ALU.mult)\
                    .then_inc(xb_ready, 1)
            pool.wait_ge(wstat_ready, 1)
            pool.wait_ge(wint_done, 2 * DC)
            for f in range(FC):
                G.tensor_scalar(wout[:, f, :], wout[:, f, :], wstat[:, 6, f:f + 1], ROUND, ALU.mult, ALU.add)\
                    .then_inc(wq_step, 1)
            pool.wait_ge(wq_step, FC)
            G.tensor_scalar(wout, wout, ROUND + 127.0, ROUND - 128.0, ALU.min, ALU.max).then_inc(wq_step, 1)
            pool.wait_ge(wq_step, FC + 1)
            G.tensor_scalar(wout_q, wout, -ROUND, 1.0, ALU.add, ALU.mult).then_inc(woutq_ready, 1)
            pool.wait_ge(wtop_part, 1)
            G.partition_all_reduce(wtop[:, 1:2], wtop[:, 0:1], P, ABSMAX).then_inc(wtop_all, 1)
            def full_max(v):
                pool.wait_ge(wmax_part, v + 1)
                pool.sem_inc(max_turn, 1)
                G.partition_all_reduce(all_max[:], own_max[:], P, ABSMAX).then_inc(wmax_all, 1)

            pool.wait_ge(hmax_part, 1)
            G.partition_all_reduce(amax[:, 43:44], amax[:, 42:43], P, ABSMAX).then_inc(hmax_all, 1)

            pool.wait_ge(wsf_ready, 1)
            for n in range(NB * FC):
                pool.wait_ge(hclamp, n // 2 + 1)
                G.tensor_scalar(hid(*divmod(n, FC)), hid(*divmod(n, FC)), -ROUND, wsf[:, n % FC:n % FC + 1],
                                ALU.add, ALU.mult).then_inc(hscaled, 1)

            full_max(0)

            def shared_high(units):
                pool.wait_ge(wscale_ready, 1)
                for n in units:
                    src, hi, _ = unit_views(SHARED_SLOT, n)
                    pool.wait_ge(low_done, n + 1)
                    G.tensor_scalar(hi, src, wscale[:, n % 2:n % 2 + 1], 0.0, ALU.mult, ALU.add).then_inc(high_done, 1)

            for n in range(1, NB * DC + 1):
                b, c = divmod(n - 1, DC)
                t = slice(b * BLK, (b + 1) * BLK)
                pool.wait_ge(inv_ready, n)
                G.tensor_tensor(fgate[:, c, t], fgate[:, c, t], gsum(b, c), ALU.mult).then_inc(rec_step, 1)
                G.tensor_tensor(igate[:, c, t], igate[:, c, t], gsum(b, c), ALU.mult).then_inc(rec_step, 1)
                pool.wait_ge(rec_step, 2 * n - 1)
                G.tensor_scalar(fgate[:, c, t], fgate[:, c, t], EPS, 1.0, ALU.add, ALU.mult).then_inc(decay_ready, 1)
                pool.wait_ge(rec_step, 2 * n)
                G.tensor_tensor(igate[:, c, t], igate[:, c, t], cand[:, c, t], ALU.mult).then_inc(info_ready, 1)
                if 2 <= n <= 4:
                    shared_high(((0, 1), (2, 3), range(4, UNITS))[n - 2])

            def add(i, u):
                G.tensor_copy(idx[:, u:u + 1].bitcast(I32), dst[:, bass.ds(i, 1)]).then_inc(idx_ready, 1)
                pool.wait_ge(y_ready, i + 1)
                pool.wait_ge(added, (i + 2) * 16)
                pool.wait_ge(idx_ready, i + 1)
                pool.sem_inc(add_turn, 1)
                G.indirect_dma_start(out, bass.IndirectOffsetOnAxis(ap=idx[:, u:u + 1], axis=0), yb[:, u, :],
                                     None, compute_op=ALU.add).then_inc(added, 16)

            for k in range(T):
                if k == 2:
                    for u in range(4):
                        pool.wait_ge(stored[u], 16 * T // 4)
                if k >= 2:
                    pool.wait_ge(meta_ready, k - 1)
                    add(k - 2, (k - 2) % RING)
                for e, step in BESIDE.get(k, ()):
                    if step == 1:
                        full_max(e + 1)
                if k == PLACE:
                    pool.wait_ge(route_ready, 1)
                    pool.wait_ge(blank_out, 16)
                for n in SENDS.get(k, ()):
                    choice, t = divmod(n, T)
                    if n == T:
                        pool.wait_ge(sent, 16 * T)
                        G.tensor_copy(rows[:, :, WGT:WGT + 1], r1[:, 5, :].unsqueeze(2)).then_inc(weight_set, 1)
                        pool.wait_ge(weight_set, 1)
                    G.indirect_dma_start(moved, bass.IndirectOffsetOnAxis(ap=slot_of[:, choice, t:t + 1], axis=0),
                                         rows[:, t, :], None).then_inc(sent, 16)
            for steps, splits in (((ROUTED, SPLIT_TO), True), ((SPLIT_TO, LAST), False)):
                with pool.Fori(*steps) as q:
                    for u in range(RING):
                        add(q * RING + (u - 1), (u - 1) % RING)
                        if splits and u == 1:
                            full_max(q + (FIRST_LATE - ROUTED + 1))
            for i in range(KT - 2, KT):
                add(i, i % RING)

        @block.scalar
        def _(act):
            A = nc.scalar.activation
            act.wait_ge(consts, 2)
            act.wait_ge(dsum_done, 1)
            A(dinv[:].rearrange("p c b -> p (c b)"), bank(7, 0, DC * BATCH), ACT.Sqrt, bias=eps[:, 0:1])\
                .then_inc(sqrt_done, 1)
            act.wait_ge(dinv_ready, 1)
            n = 0
            for b in range(NB):
                for c in range(DC):
                    n += 1
                    act.wait_ge(xs_mm, n)
                    bb = b * BLK // SEQ
                    A(x0[:, c, b * BLK:(b + 1) * BLK], bank(n - 1), ACT.Copy, scale=dinv[:, c, bb:bb + 1])\
                        .then_inc(x0_ready, 1)
            for c in range(DC):
                for half in range(2):
                    act.wait_ge(wint_done, 2 * c + half + 1)
                    A(win_q[:, c, half * BANK:(half + 1) * BANK], bank(2 * c + half), ACT.Copy).then_inc(win_ready, 1)
            act.wait_ge(gsc_ready, 1)
            for b in range(NB):
                t = slice(b * BLK, (b + 1) * BLK)
                A(x0[:, :, t], x0[:, :, t], ACT.Identity, bias=big[:, 0:1], scale=sc[:, 2:3]).then_inc(xround, 1)
            act.wait_ge(ld_bias, 16)
            for g in range(NB * FC):
                b, f = divmod(g, FC)
                act.wait_ge(mm1_done, g + 1)
                A(hid(b, f), bank((g + 4) % 8), ACT.Gelu, bias=b_in[:, f:f + 1],
                  scale=gsc[:, f:f + 1]).then_inc(gelu_done, 1)
            act.wait_ge(hsc_ready, 1)
            for m in range(PAIRS_H + 2):
                if m < PAIRS_H:
                    A(hid_pair(m), hid_pair(m), ACT.Identity, bias=big[:, 0:1], scale=sc[:, 4:5]).then_inc(hround, 1)
                if m >= 2:
                    act.wait_ge(hscaled, 2 * (m - 1))
                    if m >= 4:
                        act.wait_ge(hq_ready, m - 3)
                    A(hid_halves(m - 2)[:, :, 0, :], hid_pair(m - 2).rearrange("p (q n) -> p q n", q=2), ACT.Copy)\
                        .then_inc(hhigh, 1)

            def gates(n):
                b, c = divmod(n, DC)
                t = slice(b * BLK, (b + 1) * BLK)
                act.wait_ge(rec_done, n + 1)
                a = 3 * (n % 2)
                A(fgate[:, c, t], bank(a), ACT.Sigmoid, bias=b_rec[:, 0, c:c + 1])
                A(igate[:, c, t], bank(a + 1), ACT.Sigmoid, bias=b_rec[:, 1, c:c + 1])
                A(cand[:, c, t], bank(a + 2), ACT.Identity, bias=b_rec[:, 2, c:c + 1]).then_inc(gates_done, 1)

            for n in range(NB * DC):
                gates(n)
                for t in (2 * n, 2 * n + 1):
                    act.wait_ge(x1t_done, t + 1)
                    if t >= 4:
                        act.wait_ge(stored[t % 4], 16 * (t // 4))
                    A(x1r[:, t % 4, :], bank(6 + t % 2, 0, D), ACT.Copy).then_inc(x1r_ready, 1)

            def drain_rows(t0):
                for t in range(t0, t0 + 4):
                    act.wait_ge(rowt_done, t0 + 4)
                    if t >= 4:
                        act.wait_ge(rows_ready, t - 3)
                    A(hrow[:, t % 4, :], bank(t // 2 % 2, t % 2 * D, D), ACT.Copy).then_inc(rows_raw, 1)

            drain_rows(0)
            drain_rows(4)

            gate_ps = ps[:, 0:2 * BANK].rearrange("p (b n) -> p b n", b=2)[:, :, 0:HALF]

            def silu_of(k, first=False):
                act.wait_ge(g_done, k + 1)
                act.wait_ge(meta_ready, k + 1)
                if not first:
                    act.wait_ge(h_ready, k)
                A(silu, gate_ps, ACT.Silu, scale=gup_inv[:, bass.ds(k, 1)]).then_inc(silu_ready, 1)

            def sum_h(k):
                act.wait_ge(h_ready, k + 1)
                A(work[:, 0:I], h, ACT.Abs, accum_out=h_inv[:, 0:1]).then_inc(h_summed, 1)

            def drain_y(i, u):
                act.wait_ge(d_done, i + 1)
                act.wait_ge(yscale_ready, i + 1)
                A(yb[:, u, :], bank(6, 0, D), ACT.Copy, scale=y_scale[:, bass.ds(i, 1)]).then_inc(y_ready, 1)

            def drain_x(k):
                act.wait_ge(xT_raw, k + 1)
                A(xT[:].rearrange("p s c t -> p (s c t)"), bank(7, 0, D).bitcast(F16), ACT.Copy).then_inc(xT_ready, 1)

            def high_h(k):
                act.wait_ge(t_done, k + 1)
                A(h_T[:, 0].rearrange("p c t -> p (c t)"), ps[:, 4 * BANK:6 * BANK], ACT.Copy).then_inc(hT_high, 1)

            def norm_h(k):
                act.wait_ge(h_step, k * 2 + 2)
                A(hn[:, 0:I], h, ACT.Copy, scale=h_inv[:, 2:3]).then_inc(hn_ready, 1)

            drain_x(0)
            for u in range(4):
                act.wait_ge(stored[u], 16 * T // 4)
            for k in range(T):
                silu_of(k, k == 0)
                if k in TURN:
                    drain_rows(T // 2 + 4 * TURN.index(k))
                drain_x(k + 1)
                sum_h(k)
                if k >= 2:
                    if k >= 2 + RING:
                        act.wait_ge(added, (k + 1 - RING) * 16 + 16)
                    drain_y(k - 2, (k - 2) % RING)
                if k >= 1:
                    high_h(k - 1)
                if k == 0:
                    act.wait_ge(consts, 10)
                norm_h(k)
                if k == CHOOSE:
                    act.wait_ge(shifted, 1)
                    A(rt[:, 1, :], rt[:, 0, :], ACT.Exp).then_inc(exp_done, 1)
            with act.Fori(ROUTED, LAST) as q:
                for u in range(RING):
                    k = q * RING + (u + 1)
                    silu_of(k)
                    drain_x(q * RING + (u + 2))
                    sum_h(k)
                    act.wait_ge(added, (q * RING + (u + 3 - RING)) * 16)
                    drain_y(q * RING + (u - 1), (u - 1) % RING)
                    high_h(q * RING + u)
                    norm_h(k)

            act.wait_ge(added, 16 * (KT - RING + 1))
            drain_y(KT - 2, (KT - 2) % RING)
            high_h(KT - 1)
            act.wait_ge(added, 16 * (KT - RING + 2))
            drain_y(KT - 1, (KT - 1) % RING)

        @block.vector
        def _(dve):
            steps = [0]

            def then(ins):
                steps[0] += 1
                ins.then_inc(dve_step, 1)
                dve.wait_ge(dve_step, steps[0])

            V = nc.vector
            dve.wait_ge(ld_cond, 32)
            then(V.tensor_scalar(ys[:], cond[:], 1.0 / 16.0, None, ALU.mult))
            for b in range(BATCH):
                for c in range(DC):
                    V.tensor_scalar(condw_b[:, b, c, :], condw[:, c, :], ys[:, c, b:b + 1], None, ALU.mult)\
                        .then_inc(condw_ready, 1)
            V.tensor_tensor(ys2[:], ys[:], ys[:], ALU.mult).then_inc(condw_ready, 1)
            V.tensor_tensor(condw2, condw, condw, ALU.mult).then_inc(condw_ready, 1)
            dve.wait_ge(sqrt_done, 1)
            V.reciprocal(dinv[:], dinv[:]).then_inc(dinv_ready, 1)

            def weight_scale(w, a):
                then(V.tensor_reduce(wstat[:, a, :], w, AX.X, ALU.max, apply_absolute_value=True))
                then(V.tensor_scalar(wstat[:, a, :], wstat[:, a, :], EPS, None, ALU.max))
                then(V.reciprocal(wstat[:, a + 1, :], wstat[:, a, :]))
                V.tensor_scalar(wstat[:, a + 2, :], wstat[:, a + 1, :], 127.0, None, ALU.mult)
                return V.tensor_scalar(wstat[:, a + 3, :], wstat[:, a, :], 1.0 / 127.0, None, ALU.mult)

            dve.wait_ge(ld_win, 16)
            then(weight_scale(win_raw, 0))
            for f in range(FC):
                ins = V.tensor_scalar(win_raw[:, f, :], win_raw[:, f, :], wstat[:, 2, f:f + 1], ROUND, ALU.mult,
                                      ALU.add)
            then(ins)
            then(V.tensor_scalar(win_raw, win_raw, ROUND + 127.0, ROUND - 128.0, ALU.min, ALU.max))
            V.tensor_scalar(win_raw, win_raw, ROUND, None, ALU.subtract).then_inc(winq_ready, 1)
            n = 0
            for b in range(NB):
                for c in range(DC):
                    n += 1
                    dve.wait_ge(x0_ready, n)
                    ins = V.tensor_reduce(amax[:, n - 1:n], x0[:, c, b * BLK:(b + 1) * BLK], AX.X, ALU.max,
                                          apply_absolute_value=True)
            then(ins)
            V.tensor_reduce(amax[:, 8:9], amax[:, 0:8], AX.X, ALU.max).then_inc(xmax_part, 1)
            dve.wait_ge(xmax_all, 1)
            then(V.tensor_scalar(sc[:, 0:1], amax[:, 9:10], EPS, None, ALU.max))
            then(V.reciprocal(sc[:, 1:2], sc[:, 0:1]))
            V.tensor_scalar(sc[:, 2:3], sc[:, 1:2], 32767.0, None, ALU.mult)
            then(V.tensor_scalar(sc[:, 3:4], sc[:, 0:1], 1.0 / 32767.0, None, ALU.mult))
            V.tensor_scalar(gsc[:], wstat[:, 3, :], sc[:, 3:4], None, ALU.mult).then_inc(gsc_ready, 1)
            for b in range(NB):
                t = slice(b * BLK, (b + 1) * BLK)
                dve.wait_ge(xround, b + 1)
                then(V.tensor_scalar(x0[:, :, t], x0[:, :, t], ROUND - 32768.0, ROUND + 32767.0, ALU.max, ALU.min))
                then(V.tensor_scalar(x0_hi, x0[:, :, t], ROUND, ROUND256, ALU.subtract, ALU.add))
                then(V.tensor_scalar(xq[:, 0, :, t], x0_hi, ROUND256, None, ALU.subtract))
                V.scalar_tensor_tensor(xq[:, 1, :, t], x0[:, :, t], ROUND, xq[:, 0, :, t], ALU.subtract,
                                       ALU.subtract).then_inc(xq_ready, 1)
            def maxima(slot, half, down):
                pairs = W[:, bass.ds(raw(slot) + half * 2 * PAIR, 2 * PAIR)].rearrange("p (q n) -> p q n", q=2)
                ins = V.tensor_reduce(part_max[:, down, half:half + 1], pairs[:, :, I:PAIR] if down else pairs[:, :, 0:I],
                                      AX.XY, ALU.max, apply_absolute_value=True)
                if not down:
                    ins.then_inc(max_step, 1)

            def own_maximum(v):
                dve.wait_ge(max_step, v * 2 + 2)
                V.tensor_reduce(own_max[:], part_max[:], AX.X, ALU.max).then_inc(wmax_part, 1)

            def weight_scales(v):
                dve.wait_ge(wmax_all, v + 1)
                col = bass.ds(v, 1)
                V.tensor_scalar(winv[:, :, col], all_max[:].unsqueeze(2), TINY, 1.0 / TOP, ALU.max, ALU.mult)
                V.tensor_scalar(winv_now[:], all_max[:], TINY, 1.0 / TOP, ALU.max, ALU.mult).then_inc(winv_ready, 1)
                dve.wait_ge(winv_ready, v + 1)
                V.reciprocal(wscale[:], winv_now[:]).then_inc(wscale_ready, 1)
                dve.wait_ge(wscale_ready, v + 1)

            dve.wait_ge(ld_wout, 16)
            weight_scale(wout, 4).then_inc(wstat_ready, 1)
            dve.wait_ge(wstat_ready, 1)
            V.tensor_reduce(wtop[:, 0:1], wstat[:, 7, :], AX.X, ALU.max).then_inc(wtop_part, 1)
            for n in range(NB * FC):
                b, f = divmod(n, FC)
                dve.wait_ge(gelu_done, n + 1)
                ins = V.tensor_reduce(amax[:, 10 + n:11 + n], hid(b, f), AX.X, ALU.max,
                                      apply_absolute_value=True)
            then(ins)
            V.tensor_reduce(amax[:, 42:43], amax[:, 10:42], AX.X, ALU.max).then_inc(hmax_part, 1)
            dve.wait_ge(hmax_all, 1)
            then(V.tensor_scalar(sc[:, 5:6], amax[:, 43:44], EPS, None, ALU.max))
            then(V.reciprocal(sc[:, 6:7], sc[:, 5:6]))
            V.tensor_scalar(sc[:, 7:8], sc[:, 5:6], 1.0 / 32767.0, None, ALU.mult)
            V.tensor_scalar(sc[:, 4:5], sc[:, 6:7], 32767.0, None, ALU.mult).then_inc(hsc_ready, 1)
            dve.wait_ge(hsc_ready, 1)
            dve.wait_ge(wtop_all, 1)
            V.tensor_scalar(wtop[:, 3:4], wtop[:, 1:2], 2.0, sc[:, 7:8], ALU.mult, ALU.mult)
            then(V.reciprocal(wtop[:, 2:3], wtop[:, 1:2]))
            V.tensor_scalar(wsf[:], wstat[:, 7, :], wtop[:, 2:3], 0.5, ALU.mult, ALU.mult).then_inc(wsf_ready, 1)

            def split_hidden(m):
                if m < PAIRS_H:
                    dve.wait_ge(hround, m + 1)
                    V.tensor_scalar(hid_pair(m), hid_pair(m), ROUND + 32767.0, ROUND - 32768.0, ALU.min, ALU.max)\
                        .then_inc(hclamp, 1)
                if m >= 2:
                    dve.wait_ge(hhigh, m - 1)
                    halves = hid_halves(m - 2)
                    V.tensor_tensor(halves[:, :, 1, :], hid_pair(m - 2).rearrange("p (q n) -> p q n", q=2),
                                    halves[:, :, 0, :], ALU.subtract).then_inc(hq_ready, 1)

            def drain_x1(b):
                dve.wait_ge(xb_ready, DC)
                for c in range(DC):
                    g = DC * b + c
                    t = slice(b * BLK, (b + 1) * BLK)
                    dve.wait_ge(mm2_done, g + 1)
                    V.scalar_tensor_tensor(x1[:, c, t], bank(g), wtop[:, 3:4], x1[:, c, t], ALU.mult, ALU.add)\
                        .then_inc(x1_ready, 1)

            def low_halves(slot, v, units, high=False):
                for n in units:
                    src, hi, lo = unit_views(slot, n)
                    if high:
                        dve.wait_ge(low_done, v * UNITS + (n + 1))
                        V.tensor_scalar(hi, src, wscale[:, n % 2:n % 2 + 1], None, ALU.mult).then_inc(high_done, 1)
                    dve.wait_ge(high_done, v * UNITS + (n + 1))
                    V.scalar_tensor_tensor(lo, src, wscale[:, n % 2:n % 2 + 1], hi, ALU.mult, ALU.subtract)\
                        .then_inc(low_done, 1)
                if n == UNITS - 1:
                    dve.wait_ge(low_done, v * UNITS + (UNITS + 2))
                    dve.sem_inc(split_done, 1)

            def weight_step(e, step, place):
                if step < 2:
                    if place == 0:
                        maxima(e, step, 1)
                    if place == 1:
                        maxima(e, step, 0)
                        if step == 1:
                            own_maximum(e + 1)
                else:
                    units = STEP_UNITS[step]
                    if place == 0 and step == 2:
                        weight_scales(e + 1)
                    if place < len(units):
                        low_halves(e, e + 1, units[place:place + 1], high=True)

            dve.sem_inc(low_done, 2)
            for m in range(PAIRS_H + 2):
                split_hidden(m)
                if m >= FC and m % (FC // 2) == 2:
                    drain_x1(m // (FC // 2) - 2)
            drain_x1(NB - 2)
            drain_x1(NB - 1)
            dve.wait_ge(ld_shared, 16)
            for half in range(2):
                maxima(SHARED_SLOT, half, 1)
                maxima(SHARED_SLOT, half, 0)
            own_maximum(0)

            def gate_sum(b, c):
                t = slice(b * BLK, (b + 1) * BLK)
                n = DC * b + c + 1
                dve.wait_ge(gates_done, n)
                then(V.scalar_tensor_tensor(gsum(b, c), fgate[:, c, t], EPS, igate[:, c, t], ALU.add, ALU.add))
                V.reciprocal(gsum(b, c), gsum(b, c)).then_inc(inv_ready, 1)

            def recur(bb, c):
                t = slice(bb * SEQ, (bb + 1) * SEQ)
                dve.wait_ge(decay_ready, DC * (bb + 1) * (SEQ // BLK))
                f = fgate[:, c, t]
                V.tensor_tensor_scan(hT[:, c, t], f, f, cond[:, c, bb:bb + 1], ALU.mult, ALU.bypass)
                dve.wait_ge(info_ready, DC * (bb + 1) * (SEQ // BLK))
                suffix = cand[:, c, t]
                then(V.tensor_tensor_scan(suffix[:, ::-1], f[:, ::-1], f[:, ::-1], 1.0, ALU.mult, ALU.bypass))
                i = igate[:, c, t]
                then(V.tensor_tensor(i, i, suffix, ALU.mult))
                then(V.tensor_tensor_scan(suffix, i, i, 0.0, ALU.add, ALU.bypass))
                V.tensor_tensor(hT[:, c, t], hT[:, c, t], suffix, ALU.add).then_inc(hid_ready, 1)

            def make_rows(t0):
                dve.wait_ge(rows_raw, t0 + 4)
                then(V.tensor_reduce(rstat[:, 0, :], hrow, AX.X, ALU.max, apply_absolute_value=True))
                then(V.tensor_scalar(rstat[:, 1, :], rstat[:, 0, :], TINY, 1.0 / TOP, ALU.max, ALU.mult))
                then(V.reciprocal(rstat[:, 2, :], rstat[:, 1, :]))
                r = rows[:, t0:t0 + 4, :]
                V.tensor_copy(r[:, :, INV:INV + 1], rstat[:, 1, :].unsqueeze(2))
                V.memset(r[:, :, ROW - 1:ROW], 0.0)
                V.tensor_copy(r[:, :, DST:DST + 1].bitcast(I32), rowid[:, t0:t0 + 4].unsqueeze(2))
                for q in range(4):
                    halves = r[:, q, 0:D].bitcast(F16)
                    ins = V.tensor_scalar(halves[:, 0:D], hrow[:, q, :], rstat[:, 2, q:q + 1], None, ALU.mult)
                then(ins)
                for q in range(4):
                    halves = r[:, q, 0:D].bitcast(F16)
                    V.scalar_tensor_tensor(halves[:, D:2 * D], hrow[:, q, :], rstat[:, 2, q:q + 1], halves[:, 0:D],
                                           ALU.mult, ALU.subtract).then_inc(rows_ready, 1)

            def keep_logits(half):
                dve.wait_ge(logits_done, half + 1)
                V.tensor_copy(rt[:, 7, half * P // 2:(half + 1) * P // 2], bank(LOGIT_BANKS[half], 0, P // 2)).then_inc(logits_kept, 1)
                dve.wait_ge(logits_kept, half + 1)

            def take_shared_meta(k):
                dve.wait_ge(rows_ready, k + 1)
                V.tensor_tensor(gup_inv[:, k:k + 1], rows[:, k, INV:INV + 1], winv[:, 0, 0:1], ALU.mult)
                V.tensor_copy(out_wgt[:, k:k + 1], winv[:, 1, 0:1])
                V.tensor_copy(dst[:, k:k + 1], rowid[:, k:k + 1]).then_inc(meta_ready, 1)

            gate_sum(0, 0)
            weight_scales(0)
            gate_sum(0, 1)
            gate_sum(1, 0)
            low_halves(SHARED_SLOT, 0, range(0, 2))
            gate_sum(1, 1)
            low_halves(SHARED_SLOT, 0, range(2, 3))
            recur(0, 0)
            low_halves(SHARED_SLOT, 0, range(3, 4))
            recur(0, 1)
            low_halves(SHARED_SLOT, 0, range(4, UNITS))
            dve.wait_ge(consts, 10)
            make_rows(0)
            keep_logits(0)
            take_shared_meta(0)
            make_rows(4)

            def te(i):
                return rt[:, i, :].rearrange("p (t e) -> p t e", e=E)

            def per_tile(i):
                return r1[:, i, :].unsqueeze(2).to_broadcast([P, T, E])

            def choose():
                logits = te(7)
                then(V.tensor_reduce(r1[:, 0, :], logits, AX.X, ALU.max))
                V.tensor_tensor(te(0), logits, per_tile(0), ALU.subtract).then_inc(shifted, 1)
                dve.wait_ge(exp_done, 1)
                then(V.tensor_reduce(r1[:, 1, :], te(1), AX.X, ALU.add))
                then(V.reciprocal(r1[:, 2, :], r1[:, 1, :]))
                then(V.tensor_tensor(te(2), te(1), per_tile(2), ALU.mult))
                for t in range(T):
                    V.max(top[:, t, :], te(2)[:, t, :]).then_inc(top_ready, 1)

            def weigh():
                dve.wait_ge(top_ready, T)
                for t in range(T):
                    ins = V.max_index(topi[:, t, :], top[:, t, :], te(2)[:, t, :])
                then(ins)
                V.tensor_copy(topf[:], topi[:, :, 0:TOPK].rearrange("p t k -> p k t"))
                then(V.tensor_tensor(r1[:, 3, :], top[:, :, 0], top[:, :, 1], ALU.add))
                then(V.tensor_scalar(r1[:, 3, :], r1[:, 3, :], EPS, None, ALU.add))
                then(V.reciprocal(r1[:, 4, :], r1[:, 3, :]))
                V.tensor_tensor(r1[:, 5, :], top[:, :, 1], r1[:, 4, :], ALU.mult)
                V.tensor_tensor(r1[:, 6, :], top[:, :, 0], r1[:, 4, :], ALU.mult)
                experts_row = iota_f[:, 0:E].unsqueeze(1).to_broadcast([P, T, E])
                for k in range(TOPK):
                    ins = V.tensor_tensor(te(3 + k), experts_row, topf[:, k, :].unsqueeze(2).to_broadcast([P, T, E]),
                                          ALU.is_equal)
                then(ins)
                V.tensor_tensor(chosen[:], te(3), te(4), ALU.add).then_inc(chosen_ready, 1)

            def keep_ranks():
                dve.wait_ge(rank_done, 1)
                V.tensor_copy(te(7), bank(7, D, P).rearrange("p (t e) -> p t e", e=E))
                V.tensor_copy(rt[:, 5, :].rearrange("p (e t) -> p e t", e=E),
                              bank(7, D + P, P).rearrange("p (t e) -> p e t", e=E)).then_inc(ranks_kept, 1)
                dve.wait_ge(ranks_kept, 1)

            def place():
                et = rt[:, 5, :].rearrange("p (e t) -> p e t", e=E)
                then(V.tensor_tensor_scan(rt[:, 6, :], notfirst.rearrange("p e t -> p (e t)"), rt[:, 5, :], 0.0,
                                          ALU.mult, ALU.add))
                count = rt[:, 6, :].rearrange("p (e t) -> p e t", e=E)
                then(V.tensor_scalar(r8[:, 0, :], count[:, :, T - 1], 1.0 / P, 0.5 - 0.5 / P, ALU.mult, ALU.add))
                then(V.tensor_scalar(r8[:, 1, :], r8[:, 0, :], ROUND, ROUND, ALU.add, ALU.subtract))
                then(V.tensor_scalar(r8[:, 2, :], r8[:, 1, :], 1.0, None, ALU.max))
                then(V.tensor_tensor_scan(r8[:, 3, :], r8[:, 2, :], r8[:, 2, :], 0.0, ALU.add, ALU.bypass))
                then(V.tensor_tensor(r8[:, 4, :], r8[:, 3, :], r8[:, 2, :], ALU.subtract))
                then(V.tensor_scalar(r8[:, 5, :], r8[:, 4, :], float(P), None, ALU.mult))
                then(V.tensor_tensor(rt[:, 5, :], rt[:, 6, :], rt[:, 5, :], ALU.subtract))
                then(V.tensor_tensor(te(7), te(7), et.rearrange("p e t -> p t e"), ALU.add))
                then(V.tensor_tensor(te(7), te(7), r8[:, 5, :].unsqueeze(1).to_broadcast([P, T, E]), ALU.add))
                for k in range(TOPK):
                    then(V.tensor_tensor(te(3 + k), te(3 + k), te(7), ALU.mult))
                    then(V.tensor_reduce(topf[:, k, :], te(3 + k), AX.X, ALU.add))
                V.tensor_copy(slot_of[:], topf[:])
                V.tensor_copy(rows[:, :, WGT:WGT + 1], r1[:, 6, :].unsqueeze(2)).then_inc(route_ready, 1)
                then(V.tensor_tensor(owner_f, r8[0:1, 3, :].unsqueeze(1).to_broadcast([1, JT + 1, E]),
                                     iota_f[0:1, :].unsqueeze(2).to_broadcast([1, JT + 1, E]), ALU.is_le))
                then(V.tensor_reduce(owner_r[:], owner_f, AX.X, ALU.add))
                then(V.tensor_scalar(owner_r[:], owner_r[:], E - 1.0, None, ALU.min))
                V.tensor_copy(tile_slot[0:1, T:KT + 1], owner_r[:]).then_inc(owner_ready, 1)

            up_ps = ps[:, 2 * BANK:4 * BANK].rearrange("p (b n) -> p b n", b=2)[:, :, 0:HALF]

            def times_up(k, first=False):
                dve.wait_ge(u_done, k + 1)
                dve.wait_ge(silu_ready, k + 1)
                if not first:
                    dve.wait_ge(hn_ready, k)
                V.tensor_tensor(h.rearrange("p (b n) -> p b n", b=2), silu, up_ps, ALU.mult).then_inc(h_ready, 1)

            def h_scales(k):
                dve.wait_ge(h_summed, k + 1)
                V.tensor_scalar(h_inv[:, 1:2], h_inv[:, 0:1], TINY, 1.0 / TOP_SUM, ALU.max, ALU.mult)\
                    .then_inc(h_step, 1)
                dve.wait_ge(h_step, k * 2 + 1)
                V.reciprocal(h_inv[:, 2:3], h_inv[:, 1:2]).then_inc(h_step, 1)
                one = bass.ds(k, 1)
                V.scalar_tensor_tensor(y_scale[:, one], h_inv[:, 1:2], gup_inv[:, one], out_wgt[:, one], ALU.mult,
                                       ALU.mult).then_inc(yscale_ready, 1)

            def take_meta(k, u, loaded, v):
                dve.wait_ge(*loaded)
                one = bass.ds(k, 1)
                V.tensor_tensor(gup_inv[:, one], xin[:, u, INV:INV + 1], winv[:, 0, bass.ds(v, 1)], ALU.mult)
                V.tensor_tensor(out_wgt[:, one], xin[:, u, WGT:WGT + 1], winv[:, 1, bass.ds(v, 1)], ALU.mult)
                V.tensor_copy(dst[:, one], xin[:, u, DST:DST + 1].bitcast(I32)).then_inc(meta_ready, 1)

            def low_h(k):
                dve.wait_ge(hT_high, k + 1)
                V.tensor_tensor(h_T[:, 1].rearrange("p c t -> p (c t)"), ps[:, 4 * BANK:6 * BANK],
                                h_T[:, 0].rearrange("p c t -> p (c t)"), ALU.subtract).then_inc(hT_low, 1)

            def scales_of(k):
                return dve.value_load(tile_slot[0:1, bass.ds(k, 1)], min_val=0, max_val=E - 1) + 1

            for k in range(T):
                times_up(k, k == 0)
                if k == LOGITS:
                    keep_logits(1)
                if k + 1 < T:
                    take_shared_meta(k + 1)
                else:
                    take_meta(T, 0, (xin_ready[0], 16), scales_of(T))
                beside = BESIDE.get(k, ())
                for e, step in beside:
                    if step == 0:
                        dve.wait_ge(ld_exp[e], 16)
                    weight_step(e, step, 0)
                h_scales(k)
                if k < 4:
                    gate_sum(2 + k // 2, k % 2)
                elif k < 6:
                    recur(1, k - 4)
                if k in TURN:
                    make_rows(T // 2 + 4 * TURN.index(k))
                for e, step in beside:
                    weight_step(e, step, 1)
                if k >= 1:
                    low_h(k - 1)
                if k == CHOOSE:
                    choose()
                if k == WEIGH:
                    weigh()
                if k == PLACE:
                    keep_ranks()
                    place()
                for e, step in beside:
                    weight_step(e, step, 2)
            for steps_, splits in (((ROUTED, SPLIT_TO), True), ((SPLIT_TO, LAST), False)):
                with dve.Fori(*steps_) as q:
                    for u in range(RING):
                        k = q * RING + (u + 1)
                        times_up(k)
                        i = q * RING + (u + 2)
                        more, v = divmod(u + 1, RING)
                        take_meta(i, v, (xin_ready[v], (q + (more + 1 - ROUTED)) * 16), scales_of(i))
                        e = q - (ROUTED - FIRST_LATE)
                        if splits:
                            if u == 0:
                                dve.wait_ge(ld_late, (q - (ROUTED - 1)) * 16)
                            weight_step(e, u, 0)
                        h_scales(k)
                        if splits:
                            weight_step(e, u, 1)
                        low_h(q * RING + u)
                        if splits:
                            weight_step(e, u, 2)
            low_h(KT - 1)

        @block.tensor
        def _(pe):
            M = nc.tensor.matmul
            pe.wait_ge(condw_ready, BATCH * DC)
            n = 0
            for b in range(NB):
                pe.wait_ge(ld_x[b], 16)
                for o in range(DC):
                    n += 1
                    if n == 3:
                        pe.wait_ge(condw_ready, BATCH * DC + 2)
                        for oo in range(DC):
                            for c in range(DC):
                                ins = M(bank(7, oo * BATCH, BATCH), condw2[:, c, oo * P:(oo + 1) * P], ys2[:, c, :],
                                        start=(c == 0), stop=(c == DC - 1))
                        ins.then_inc(dsum_done, 1)
                    if n == 8:
                        pe.wait_ge(sqrt_done, 1)
                    for c in range(DC):
                        ins = M(bank(n - 1), condw_b[:, b * BLK // SEQ, c, o * P:(o + 1) * P],
                                x1[:, c, b * BLK:(b + 1) * BLK], start=(c == 0), stop=(c == DC - 1))
                    ins.then_inc(xs_mm, 1)
            pe.wait_ge(ident_ok, 1)
            pe.wait_ge(winq_ready, 1)
            for c in range(DC):
                for half in range(2):
                    pe.wait_ge(x0_ready, 2 * c + half + 1)
                    for q in range(4):
                        f = half * 4 + q
                        ins = nc.tensor.transpose(bank(2 * c + half, q * P, P), win_raw[:, f, c * P:(c + 1) * P],
                                                  ident[:])
                    ins.then_inc(wint_done, 1)
            pe.wait_ge(win_ready, 4)
            for g in range(NB * FC):
                b, f = divmod(g, FC)
                if f == 0:
                    pe.wait_ge(xq_ready, b + 1)
                if g < 4:
                    pe.wait_ge(x0_ready, 4 + g + 1)
                if g >= 8:
                    pe.wait_ge(gelu_done, g - 7)
                for c in range(DC):
                    for half in range(2):
                        ins = M(bank((g + 4) % 8), win_q[:, c, f * P:(f + 1) * P],
                                xq[:, half, c, b * BLK:(b + 1) * BLK], start=(c == 0 and half == 0),
                                stop=(c == DC - 1 and half == 1))
                ins.then_inc(mm1_done, 1)
            pe.wait_ge(woutq_ready, 1)
            pe.wait_ge(gelu_done, NB * FC)
            for b in range(NB):
                for f in range(FC):
                    pe.wait_ge(hq_ready, (b * FC + f) // 2 + 1)
                    for o in range(DC):
                        for low in range(2):
                            ins = M(bank(DC * b + o), wout_q[:, f, o * P:(o + 1) * P], hid_halves((b * FC + f) // 2)[:, f % 2, low, :],
                                    start=(f == 0 and not low), stop=(f == FC - 1 and low == 1))
                        if f == FC - 1:
                            ins.then_inc(mm2_done, 1)
            def turn_rows(t0):
                for t in range(t0, t0 + 4):
                    for c in range(DC):
                        ins = nc.tensor.transpose(bank(t // 2 % 2, (t % 2 * DC + c) * P, P),
                                                  hT[:, c, t * P:(t + 1) * P], ident[:])
                    ins.then_inc(rowt_done, 1)

            pe.wait_ge(ld_small, 16 * 2)
            for n in range(NB * DC):
                b, o = divmod(n, DC)
                a = 3 * (n % 2)
                pe.wait_ge(x1_ready, max(DC * (b + 1), a + 3))
                if n >= 2:
                    pe.wait_ge(gates_done, n - 1)
                for g in range(3):
                    for c in range(DC):
                        ins = M(bank(a + g), recw[:, g, c, o * P:(o + 1) * P], x1[:, c, b * BLK:(b + 1) * BLK],
                                start=(c == 0), stop=(c == DC - 1))
                ins.then_inc(rec_done, 1)
                pe.wait_ge(x1_ready, NB * DC)
                for t in (2 * n, 2 * n + 1):
                    if t >= 2:
                        pe.wait_ge(x1r_ready, t - 1)
                    for c in range(DC):
                        ins = nc.tensor.transpose(bank(6 + t % 2, c * P, P), x1[:, c, t * P:(t + 1) * P], ident[:])
                    ins.then_inc(x1t_done, 1)

            def logits(half):
                for t in range(half * T // 2, (half + 1) * T // 2):
                    for c in range(DC):
                        ins = M(bank(LOGIT_BANKS[half], t % (T // 2) * E, E), hT[:, c, t * P:(t + 1) * P], gatew[:, c, :],
                                start=(c == 0), stop=(c == DC - 1))
                ins.then_inc(logits_done, 1)

            pe.wait_ge(gates_done, NB * DC)
            pe.wait_ge(hid_ready, DC)
            turn_rows(0)
            logits(0)
            pe.wait_ge(rows_raw, 4)
            turn_rows(4)

            def turn_x(row, loaded):
                pe.wait_ge(*loaded)
                halves = row[:, 0:D].bitcast(F16)
                to = bank(7, 0, D).bitcast(F16)
                for q in range(2 * DC):
                    ins = nc.tensor.transpose(to[:, q * P:(q + 1) * P], halves[:, q * P:(q + 1) * P], ident_h[:])
                ins.then_inc(xT_raw, 1)

            def product(which, at):
                for c in range(DC):
                    a = 2 * PAIR * (2 * c + which)
                    for part, low in ((0, 0), (0, 1), (1, 0)):
                        for b in range(2):
                            ins = M(bank(2 * which + b, 0, HALF), xT[:, part, c, :],
                                    Wh[:, bass.ds(at + (a + low * I + b * HALF), HALF)],
                                    start=(c == 0 and part == 0 and low == 0), stop=(c == DC - 1 and part == 1))
                return ins

            def gate(k, at, first=False):
                pe.wait_ge(xT_ready, k + 1)
                if not first:
                    pe.wait_ge(silu_ready, k)
                product(0, at).then_inc(g_done, 1)

            def up(k, at, first=False):
                if not first:
                    pe.wait_ge(h_ready, k)
                product(1, at).then_inc(u_done, 1)

            def down(i, at, first=False):
                pe.wait_ge(hT_low, i + 1)
                if not first:
                    pe.wait_ge(y_ready, i)
                for c in range(IC):
                    a = 2 * (c // 2 * PAIR + I) + c % 2 * D
                    for part, low in ((0, 0), (0, 1), (1, 0)):
                        ins = M(bank(6, 0, D), h_T[:, part, c, :], Wh[:, bass.ds(at + (a + low * DU), D)],
                                start=(c == 0 and part == 0 and low == 0), stop=(c == IC - 1 and part == 1))
                ins.then_inc(d_done, 1)

            def turn_h(i, first=False):
                pe.wait_ge(hn_ready, i + 1)
                if not first:
                    pe.wait_ge(hT_low, i)
                for c in range(IC):
                    ins = nc.tensor.transpose(bank(4, c * P, P), hn[:, c * P:(c + 1) * P], ident[:])
                ins.then_inc(t_done, 1)

            def slot_of_tile(k):
                return pe.value_load(tile_slot[0:1, bass.ds(k, 1)], min_val=0, max_val=E - 1)

            def place_of(slot):
                return pe.snap(slot * (2 * EW))

            shared = 2 * SHARED_SLOT * EW
            pe.wait_ge(consts, 10)
            turn_x(rows[:, 0, :], (rows_ready, 1))
            pe.wait_ge(split_done, 1)
            pe.wait_ge(rows_raw, 8)
            pe.wait_ge(logits_kept, 1)
            for k in range(T):
                if k - 1 in TURN:
                    pe.wait_ge(rows_raw, T // 2 + 4 * (TURN.index(k - 1) + 1))
                if k - 1 == LOGITS:
                    pe.wait_ge(logits_kept, 2)
                gate(k, shared, k == 0)
                up(k, shared, k == 0)
                if k in TURN:
                    pe.wait_ge(silu_ready, k + 1)
                    pe.wait_ge(hid_ready, BATCH * DC)
                    turn_rows(T // 2 + 4 * TURN.index(k))
                if k == LOGITS:
                    pe.wait_ge(rows_raw, 12)
                    logits(1)
                if k - 1 == PLACE:
                    pe.wait_ge(ranks_kept, 1)
                if k + 1 < T:
                    turn_x(rows[:, k + 1, :], (rows_ready, k + 2))
                else:
                    turn_x(xin[:, 0, :], (xin_ready[0], 16))
                if k >= 2:
                    down(k - 2, shared, k == 2)
                if k >= 1:
                    turn_h(k - 1, k == 1)
                if k == PLACE:
                    pe.wait_ge(xT_ready, k + 2)
                    pe.wait_ge(chosen_ready, 1)
                    flat = chosen[:].rearrange("p t e -> p (t e)")
                    M(bank(7, D, P), before[:], flat, start=True, stop=True)
                    M(bank(7, D + P, P), ones[:], flat, start=True, stop=True).then_inc(rank_done, 1)
            pe.wait_ge(owner_ready, 1)
            with pe.Fori(ROUTED, LAST) as q:
                for u in range(RING):
                    k = q * RING + (u + 1)
                    if u == 0:
                        slot = slot_of_tile(k)
                        at = {0: place_of(slot)}
                    pe.wait_ge(split_done, slot + 2)
                    gate(k, at[u])
                    if u < 2:
                        at[u - 2] = place_of(slot_of_tile(q * RING + (u - 1)))
                    up(k, at[u])
                    if u < RING - 1:
                        slot = slot_of_tile(q * RING + (u + 2))
                        at[u + 1] = place_of(slot)
                    more, w = divmod(u + 1, RING)
                    turn_x(xin[:, w, :], (xin_ready[w], (q + (more + 1 - ROUTED)) * 16))
                    down(q * RING + (u - 1), at[u - 2])
                    turn_h(q * RING + u)
            down(KT - 2, place_of(slot_of_tile(KT - 2)))
            turn_h(KT - 1)
            down(KT - 1, place_of(slot_of_tile(KT - 1)))


def kernel(**inputs):
    import numpy as np
    import concourse.bacc as bacc
    from concourse.bass_utils import run_bass_kernel_spmd as run

    def part(a, c):
        return np.ascontiguousarray(a.reshape(c, P, -1).transpose(1, 0, 2))

    n = {k: np.asarray(v) for k, v in inputs.items()}

    def expert(gate_up, down):
        gu = part(gate_up.T, DC).reshape(P, PAIRS, I)
        dn = part(np.pad(down.T, ((0, IC * P - I), (0, 0))), IC).reshape(P, PAIRS, DU)
        return np.concatenate([gu, dn], 2).reshape(P, EW)

    all_experts = [expert(n["L1_ffn_experts_gate_up"][e], n["L1_ffn_experts_down"][e]) for e in range(E)]
    all_experts.append(expert(n["L1_ffn_shared_gate_up"], n["L1_ffn_shared_down"]))
    bias = [part(n["L0_ffn_b_in"][:, None], FC)[:, :, 0], part(n["L0_ffn_b_out"][:, None], DC)[:, :, 0]]
    bias += [part(n[f"L1_cond_b_{g}"][:, None], DC)[:, :, 0] for g in "fih"]
    arrays = {
        "x_t": part(n["x"].reshape(TOK, D).T, DC),
        "cond_t": part(n["cond_1024"].T, DC),
        "cond_w": part(n["L0_cond_weight"], DC),
        "w_in_t": part(n["L0_ffn_W_in"].T, FC),
        "w_out": part(n["L0_ffn_W_out"], FC),
        "bias": np.concatenate(bias, 1),
        "rec_w": np.ascontiguousarray(np.stack([part(n[f"L1_cond_W_{g}"].T, DC) for g in "fih"], 1)),
        "gate_w": part(n["L1_ffn_gate_weight"].T, DC),
        "experts": np.stack(all_experts),
    }
    nc = bacc.Bacc("TRN2", target_bir_lowering=False, num_devices=1, dynamic_dma_scratch_size=4096)
    args = [nc.dram_tensor(f"in_{k}", a.shape, F32, kind="ExternalInput").ap() for k, a in arrays.items()]
    out = nc.dram_tensor("out_rows", (OUTR, D), F32, kind="ExternalOutput").ap()
    adaln_ffn_moe(nc, *args, out)
    r = run(nc, [{f"in_{k}": a for k, a in arrays.items()}], core_ids=[0])
    return r.results[0]["out_rows"][:TOK].reshape(BATCH, SEQ, D)
```
